# Optimizing a Trainium2 kernel written in Bass

```python
import numpy as np
import jax
import jax.numpy as jnp

def _softmax(x, axis=-1):
    return jax.nn.softmax(x, axis=axis)

def _gelu(x):
    return jax.nn.gelu(x, approximate=True)

def _silu(x):
    return jax.nn.silu(x)

def _sigmoid(x):
    return jax.nn.sigmoid(x)

def _layernorm(x, axis=-1, eps=1e-05):
    m = jnp.mean(x, axis=axis, keepdims=True)
    v = jnp.var(x, axis=axis, keepdims=True)
    return (x - m) / jnp.sqrt(v + eps)

def _scatter_add(tgt, idx, src, axis=0):
    return tgt.at[idx].add(src)

def _segment_sum(src, seg, n):
    return jax.ops.segment_sum(src, seg, n)
kernel_name = 'mk_decoder_postln_d2_seqx_r8_298680'

def setup_inputs(seed: int=0):
    np.random.seed(seed)
    _w = jnp.asarray

    def _rec_inputs():
        import jax
        import jax.numpy as jnp
        _rk = jax.random.key(seed)
        x = -0.0003929 + 0.9999 * jax.random.normal(jax.random.fold_in(_rk, 1), (8, 128, 256), jnp.float32)
        _lenS = 128 - jax.random.randint(jax.random.fold_in(_rk, 7), (8,), 0, max(1, 128 // 4) + 1, jnp.int32)
        _lenS2 = 128 - jax.random.randint(jax.random.fold_in(_rk, 8), (8,), 0, max(1, 128 // 4) + 1, jnp.int32)
        _ctx_2048P = jax.random.normal(jax.random.fold_in(_rk, 11), (8, 16, 256), jnp.float32)
        _ctx_2048c = jax.random.dirichlet(jax.random.fold_in(_rk, 511), 0.3 * jnp.ones((16,), jnp.float32), (8, 128))
        _ctx_2048t = jnp.einsum('bsk,bkd->bsd', _ctx_2048c, _ctx_2048P)
        _ctx_2048t = _ctx_2048t * jax.lax.rsqrt(jnp.mean(jnp.square(_ctx_2048t)) + 1e-12) * 0.953939
        ctx_2048 = -0.000514642 + 1.00011 * (_ctx_2048t + 0.3 * jax.random.normal(jax.random.fold_in(_rk, 611), (8, 128, 256), jnp.float32))
        return (x, ctx_2048)
    x, ctx_2048 = _rec_inputs()

    def _L0_attn_setup():
        import jax, jax.numpy as jnp
        import numpy as np
        B, S, H = (2, 256, 256)
        N_HEADS = 16
        HEAD_DIM = H // N_HEADS
        key = jax.random.key(seed)
        k1, k2, k3 = jax.random.split(key, 3)
        lim_in = float(np.sqrt(6.0 / (H + 3 * H)))
        lim_out = float(np.sqrt(6.0 / (H + H)))
        return {'hidden_states': jax.random.normal(k1, (B, S, H), dtype=jnp.float32), 'W_in': jax.random.uniform(k2, (3 * H, H), jnp.float32, -lim_in, lim_in), 'b_in': jnp.zeros((3 * H,), jnp.float32), 'W_out': jax.random.uniform(k3, (H, H), jnp.float32, -lim_out, lim_out), 'b_out': jnp.zeros((H,), jnp.float32)}
    _L0_attn_all = _L0_attn_setup()
    _L0_attn_in = {k: v for k, v in _L0_attn_all.items() if k in ('W_in', 'b_in', 'W_out', 'b_out')}
    del _L0_attn_all

    def _L0_xattn_setup():
        import jax, jax.numpy as jnp
        import numpy as np
        FEAT = 256
        G = 16
        DG = FEAT // G
        key = jax.random.key(seed)
        ks = jax.random.split(key, 8)
        bs, N1, N2 = (2, 512, 64)
        s = 1.0 / np.sqrt(FEAT)
        return {'ref_feat': jax.random.normal(ks[0], (bs, N1, FEAT), jnp.float32), 'sup_feat': jax.random.normal(ks[1], (bs, N2, FEAT), jnp.float32), 'W_fc': jax.random.normal(ks[2], (FEAT, FEAT), jnp.float32) * s, 'b_fc': jnp.zeros((FEAT,), jnp.float32), 'W_q': jax.random.normal(ks[3], (FEAT, FEAT), jnp.float32) * s, 'b_q': jnp.zeros((FEAT,), jnp.float32), 'W_k': jax.random.normal(ks[4], (FEAT, FEAT), jnp.float32) * s, 'b_k': jnp.zeros((FEAT,), jnp.float32), 'W_v': jax.random.normal(ks[5], (FEAT, FEAT, 1, 1), jnp.float32) * 0.01, 'b_v': jnp.zeros((FEAT,), jnp.float32)}
    _L0_xattn_all = _L0_xattn_setup()
    _L0_xattn_in = {k: v for k, v in _L0_xattn_all.items() if k in ('W_fc', 'b_fc', 'W_q', 'b_q', 'W_k', 'b_k', 'W_v', 'b_v')}
    del _L0_xattn_all

    def _L0_ffn_setup():
        import jax, jax.numpy as jnp
        import numpy as np
        from jax import lax
        B, S, H = (2, 64, 256)
        I = 96
        E = 64
        K = 8
        key = jax.random.key(seed)
        k1, k2, k3, k4 = jax.random.split(key, 4)
        hidden_states = jax.random.normal(k1, (B, S, H), jnp.float32)
        gate_weight = jax.random.normal(k2, (E, H), jnp.float32) * 0.02
        gate_up_weights = jax.random.normal(k3, (E, H, 2 * I), jnp.float32) * 0.02
        down_weights = jax.random.normal(k4, (E, I, H), jnp.float32) * 0.02
        return {'hidden_states': hidden_states, 'gate_weight': gate_weight, 'gate_up_weights': gate_up_weights, 'down_weights': down_weights}
    _L0_ffn_all = _L0_ffn_setup()
    _L0_ffn_in = {k: v for k, v in _L0_ffn_all.items() if k in ('gate_weight', 'gate_up_weights', 'down_weights')}
    del _L0_ffn_all

    def _L1_attn_setup():
        import jax, jax.numpy as jnp
        import numpy as np
        from jax import lax
        B, T, D, H, CS = (4, 512, 256, 16, 64)
        DK = D // H

        def apply_rope(x):
            t, d = (x.shape[-2], x.shape[-1])
            inv_freq = 1.0 / 10000.0 ** (jnp.arange(0, d, 2, dtype=jnp.float32) / d)
            pos = jnp.arange(t, dtype=jnp.float32)
            sinusoid = pos[:, None] * inv_freq[None, :]
            sin, cos = (jnp.sin(sinusoid), jnp.cos(sinusoid))
            x1, x2 = (x[..., ::2], x[..., 1::2])
            out = jnp.stack([x1 * cos - x2 * sin, x1 * sin + x2 * cos], axis=-1)
            return out.reshape(x.shape)
        key = jax.random.key(seed)
        ks = jax.random.split(key, 6)
        s = 0.02
        return {'x': jax.random.normal(ks[0], (B, T, D), dtype=jnp.float32), 'Wq': jax.random.normal(ks[1], (D, D), dtype=jnp.float32) * s, 'bq': jnp.zeros((D,), jnp.float32), 'Wk': jax.random.normal(ks[2], (D, D), dtype=jnp.float32) * s, 'bk': jnp.zeros((D,), jnp.float32), 'Wv': jax.random.normal(ks[3], (D, D), dtype=jnp.float32) * s, 'bv': jnp.zeros((D,), jnp.float32), 'Wg': jax.random.normal(ks[4], (D, D), dtype=jnp.float32) * s, 'bg': jnp.zeros((D,), jnp.float32), 'Wo': jax.random.normal(ks[5], (D, D), dtype=jnp.float32) * s, 'bo': jnp.zeros((D,), jnp.float32)}
    _L1_attn_all = _L1_attn_setup()
    _L1_attn_in = {k: v for k, v in _L1_attn_all.items() if k in ('Wq', 'bq', 'Wk', 'bk', 'Wv', 'bv', 'Wg', 'bg', 'Wo', 'bo')}
    del _L1_attn_all

    def _L1_xattn_setup():
        import jax, jax.numpy as jnp
        import numpy as np
        HID = 256
        H = 32
        HK = 8
        G = H // HK
        D = HID // H
        T = 128
        W_ATT = 32
        W_SSM = 64

        def _heads(x, n):
            B, Tt, _ = x.shape
            return x.reshape(B, Tt, n, D).transpose(0, 2, 1, 3)

        def _attend(q, k, v):
            pos = jnp.arange(T)
            rel = pos[None, :] - pos[:, None]
            slopes = jnp.power(2.0, -8.0 * jnp.arange(H, dtype=jnp.float32) / H)
            alibi = slopes[:, None, None] * rel.astype(jnp.float32)
            bias = jnp.concatenate([alibi, alibi], axis=-1)
            delta = -rel
            ssm_mask = (delta >= 0) & (delta < W_SSM)
            att_mask = (delta >= 0) & (delta < W_ATT)
            mask = jnp.concatenate([ssm_mask, att_mask], axis=-1)
            scores = jnp.einsum('bhqd,bhkd->bhqk', q, k) / np.sqrt(D).astype(np.float32)
            scores = scores + bias[None]
            scores = jnp.where(mask[None, None], scores, -jnp.inf)
            wei = jax.nn.softmax(scores, axis=-1)
            return jnp.einsum('bhqk,bhkd->bhqd', wei, v)
        key = jax.random.key(seed)
        ks = jax.random.split(key, 8)
        s = lambda fan_in: 1.0 / np.sqrt(fan_in)
        return {'hidden_states': jax.random.normal(ks[0], (2, T, HID), jnp.float32), 'ssm_states': jax.random.normal(ks[1], (2, T, HID), jnp.float32), 'Wq': jax.random.normal(ks[2], (2 * HID, HID), jnp.float32) * s(2 * HID), 'Wk': jax.random.normal(ks[3], (HID, HK * D), jnp.float32) * s(HID), 'Wv': jax.random.normal(ks[4], (HID, HK * D), jnp.float32) * s(HID), 'Wsk': jax.random.normal(ks[5], (HID, HK * D), jnp.float32) * s(HID), 'Wsv': jax.random.normal(ks[6], (HID, HK * D), jnp.float32) * s(HID), 'Wo': jax.random.normal(ks[7], (HID, HID), jnp.float32) * s(HID)}
    _L1_xattn_all = _L1_xattn_setup()
    _L1_xattn_in = {k: v for k, v in _L1_xattn_all.items() if k in ('Wq', 'Wk', 'Wv', 'Wsk', 'Wsv', 'Wo')}
    del _L1_xattn_all

    def _L1_ffn_setup():
        import jax, jax.numpy as jnp
        import numpy as np
        E = 8
        TOP_K = 2
        H = 256
        I_MOE = 176
        I_SH = 704
        B, S = (2, 256)

        def _moe_forward(hidden_states, router_weight, gate_up_proj, down_proj, sh_gate_w, sh_up_w, sh_down_w, shared_gate_w):
            b, s, h = hidden_states.shape
            x = hidden_states.reshape(-1, h)
            shared = jnp.einsum('ti,hi->th', jax.nn.silu(x @ sh_gate_w.T) * (x @ sh_up_w.T), sh_down_w)
            logits = x @ router_weight.T
            probs = jax.nn.softmax(logits.astype(jnp.float32), axis=-1)
            top_v, top_i = jax.lax.top_k(probs, TOP_K)
            top_v = top_v / top_v.sum(axis=-1, keepdims=True)
            combine = (jax.nn.one_hot(top_i, E, dtype=top_v.dtype) * top_v[..., None]).sum(axis=1)
            out = jnp.zeros_like(x)
            for e in range(E):
                gu = x @ gate_up_proj[e].T
                gate, up = (gu[:, :I_MOE], gu[:, I_MOE:])
                cur = jax.nn.silu(gate) * up @ down_proj[e].T
                out = out + cur * combine[:, e:e + 1]
            out = out + jax.nn.sigmoid(x @ shared_gate_w.T) * shared
            return out.reshape(b, s, h)
        key = jax.random.key(seed)
        ks = jax.random.split(key, 8)
        scale = 0.02
        return {'hidden_states': jax.random.normal(ks[0], (B, S, H), dtype=jnp.float32), 'router_weight': jax.random.normal(ks[1], (E, H), dtype=jnp.float32) * scale, 'gate_up_proj': jax.random.normal(ks[2], (E, 2 * I_MOE, H), dtype=jnp.float32) * scale, 'down_proj': jax.random.normal(ks[3], (E, H, I_MOE), dtype=jnp.float32) * scale, 'sh_gate_w': jax.random.normal(ks[4], (I_SH, H), dtype=jnp.float32) * scale, 'sh_up_w': jax.random.normal(ks[5], (I_SH, H), dtype=jnp.float32) * scale, 'sh_down_w': jax.random.normal(ks[6], (H, I_SH), dtype=jnp.float32) * scale, 'shared_gate_w': jax.random.normal(ks[7], (1, H), dtype=jnp.float32) * scale}
    _L1_ffn_all = _L1_ffn_setup()
    _L1_ffn_in = {k: v for k, v in _L1_ffn_all.items() if k in ('router_weight', 'gate_up_proj', 'down_proj', 'sh_gate_w', 'sh_up_w', 'sh_down_w', 'shared_gate_w')}
    del _L1_ffn_all
    return {'x': x, 'ctx_2048': ctx_2048, 'L0_attn_W_in': _L0_attn_in['W_in'], 'L0_attn_b_in': _L0_attn_in['b_in'], 'L0_attn_W_out': _L0_attn_in['W_out'], 'L0_attn_b_out': _L0_attn_in['b_out'], 'L0_xattn_W_fc': _L0_xattn_in['W_fc'], 'L0_xattn_b_fc': _L0_xattn_in['b_fc'], 'L0_xattn_W_q': _L0_xattn_in['W_q'], 'L0_xattn_b_q': _L0_xattn_in['b_q'], 'L0_xattn_W_k': _L0_xattn_in['W_k'], 'L0_xattn_b_k': _L0_xattn_in['b_k'], 'L0_xattn_W_v': _L0_xattn_in['W_v'], 'L0_xattn_b_v': _L0_xattn_in['b_v'], 'L0_ffn_gate_weight': _L0_ffn_in['gate_weight'], 'L0_ffn_gate_up_weights': _L0_ffn_in['gate_up_weights'], 'L0_ffn_down_weights': _L0_ffn_in['down_weights'], 'L1_attn_Wq': _L1_attn_in['Wq'], 'L1_attn_bq': _L1_attn_in['bq'], 'L1_attn_Wk': _L1_attn_in['Wk'], 'L1_attn_bk': _L1_attn_in['bk'], 'L1_attn_Wv': _L1_attn_in['Wv'], 'L1_attn_bv': _L1_attn_in['bv'], 'L1_attn_Wg': _L1_attn_in['Wg'], 'L1_attn_bg': _L1_attn_in['bg'], 'L1_attn_Wo': _L1_attn_in['Wo'], 'L1_attn_bo': _L1_attn_in['bo'], 'L1_xattn_Wq': _L1_xattn_in['Wq'], 'L1_xattn_Wk': _L1_xattn_in['Wk'], 'L1_xattn_Wv': _L1_xattn_in['Wv'], 'L1_xattn_Wsk': _L1_xattn_in['Wsk'], 'L1_xattn_Wsv': _L1_xattn_in['Wsv'], 'L1_xattn_Wo': _L1_xattn_in['Wo'], 'L1_ffn_router_weight': _L1_ffn_in['router_weight'], 'L1_ffn_gate_up_proj': _L1_ffn_in['gate_up_proj'], 'L1_ffn_down_proj': _L1_ffn_in['down_proj'], 'L1_ffn_sh_gate_w': _L1_ffn_in['sh_gate_w'], 'L1_ffn_sh_up_w': _L1_ffn_in['sh_up_w'], 'L1_ffn_sh_down_w': _L1_ffn_in['sh_down_w'], 'L1_ffn_shared_gate_w': _L1_ffn_in['shared_gate_w']}

def reference(x, ctx_2048, L0_attn_W_in, L0_attn_b_in, L0_attn_W_out, L0_attn_b_out, L0_xattn_W_fc, L0_xattn_b_fc, L0_xattn_W_q, L0_xattn_b_q, L0_xattn_W_k, L0_xattn_b_k, L0_xattn_W_v, L0_xattn_b_v, L0_ffn_gate_weight, L0_ffn_gate_up_weights, L0_ffn_down_weights, L1_attn_Wq, L1_attn_bq, L1_attn_Wk, L1_attn_bk, L1_attn_Wv, L1_attn_bv, L1_attn_Wg, L1_attn_bg, L1_attn_Wo, L1_attn_bo, L1_xattn_Wq, L1_xattn_Wk, L1_xattn_Wv, L1_xattn_Wsk, L1_xattn_Wsv, L1_xattn_Wo, L1_ffn_router_weight, L1_ffn_gate_up_proj, L1_ffn_down_proj, L1_ffn_sh_gate_w, L1_ffn_sh_up_w, L1_ffn_sh_down_w, L1_ffn_shared_gate_w):
    import jax
    import jax.numpy as jnp

    def _L0_attn_ref(hidden_states, W_in, b_in, W_out, b_out):
        import jax, jax.numpy as jnp
        import numpy as np
        B, S, H = (2, 256, 256)
        N_HEADS = 16
        HEAD_DIM = H // N_HEADS
        b, s, h = hidden_states.shape
        qkv = hidden_states @ W_in.T + b_in
        q, k, v = jnp.split(qkv, 3, axis=-1)

        def to_heads(x):
            return x.reshape(b, s, N_HEADS, HEAD_DIM).transpose(0, 2, 1, 3)
        q, k, v = (to_heads(q), to_heads(k), to_heads(v))
        scale = HEAD_DIM ** (-0.5)
        scores = jnp.einsum('bnqd,bnkd->bnqk', q, k) * scale
        causal = jnp.triu(jnp.ones((s, s), dtype=bool), k=1)
        scores = jnp.where(causal, -jnp.inf, scores)
        weights = jax.nn.softmax(scores, axis=-1)
        attn = jnp.einsum('bnqk,bnkd->bnqd', weights, v)
        attn = attn.transpose(0, 2, 1, 3).reshape(b, s, h)
        return attn @ W_out.T + b_out

    def _L0_xattn_ref(ref_feat, sup_feat, W_fc, b_fc, W_q, b_q, W_k, b_k, W_v, b_v):
        import jax, jax.numpy as jnp
        import numpy as np
        FEAT = 256
        G = 16
        DG = FEAT // G
        bs, N1, _ = ref_feat.shape
        sup = jax.nn.relu(sup_feat @ W_fc.T + b_fc)
        ref = jax.nn.relu(ref_feat @ W_fc.T + b_fc)
        q = (ref @ W_q.T + b_q).reshape(bs, N1, G, DG)
        k = (sup @ W_k.T + b_k).reshape(bs, -1, G, DG)
        aff = jnp.einsum('bqhd,bkhd->bhqk', q, k) * (1.0 / np.sqrt(DG))
        p = jax.nn.softmax(aff, axis=-1)
        out_h = jnp.einsum('bhqk,bkf->bhqf', p, sup)
        Wv = W_v.reshape(G, DG, FEAT)
        attn = jnp.einsum('bhqf,hjf->bqhj', out_h, Wv).reshape(bs, N1, FEAT) + b_v
        return ref + attn

    def _L0_ffn_ref(hidden_states, gate_weight, gate_up_weights, down_weights):
        import jax, jax.numpy as jnp
        import numpy as np
        from jax import lax
        B, S, H = (2, 64, 256)
        I = 96
        E = 64
        K = 8
        orig_shape = hidden_states.shape
        x = hidden_states.reshape(-1, H)
        T = x.shape[0]
        logits = x @ gate_weight.T
        probs = jax.nn.softmax(logits.astype(jnp.float32), axis=-1)
        routing_weights, selected_experts = lax.top_k(probs, K)
        wsum = routing_weights.sum(axis=-1, keepdims=True)
        wsum = jnp.where(wsum == 0, 1.0, wsum)
        routing_weights = (routing_weights / wsum).astype(x.dtype)
        combine = jnp.zeros((T, E), x.dtype).at[jnp.arange(T)[:, None], selected_experts].add(routing_weights)

        def body(acc, ws):
            wgu, wd, we = ws
            gu = x @ wgu
            gate, up = jnp.split(gu, 2, axis=-1)
            act = jax.nn.silu(gate) * up
            out = act @ wd
            return (acc + we[:, None] * out, None)
        init = jnp.zeros_like(x)
        final, _ = lax.scan(body, init, (gate_up_weights, down_weights, combine.T))
        return final.reshape(orig_shape)

    def _L1_attn_ref(x, Wq, bq, Wk, bk, Wv, bv, Wg, bg, Wo, bo):
        import jax, jax.numpy as jnp
        import numpy as np
        from jax import lax
        B, T, D, H, CS = (4, 512, 256, 16, 64)
        DK = D // H

        def apply_rope(x):
            t, d = (x.shape[-2], x.shape[-1])
            inv_freq = 1.0 / 10000.0 ** (jnp.arange(0, d, 2, dtype=jnp.float32) / d)
            pos = jnp.arange(t, dtype=jnp.float32)
            sinusoid = pos[:, None] * inv_freq[None, :]
            sin, cos = (jnp.sin(sinusoid), jnp.cos(sinusoid))
            x1, x2 = (x[..., ::2], x[..., 1::2])
            out = jnp.stack([x1 * cos - x2 * sin, x1 * sin + x2 * cos], axis=-1)
            return out.reshape(x.shape)
        b, t, c = x.shape
        h, dk, cs = (H, DK, CS)
        nc = t // cs

        def heads(y):
            return y.reshape(b, t, h, dk).transpose(0, 2, 1, 3)
        q = heads(x @ Wq.T + bq)
        k = heads(x @ Wk.T + bk)
        v = heads(x @ Wv.T + bv)
        g = jax.nn.sigmoid(heads(x @ Wg.T + bg))
        q = jax.nn.elu(apply_rope(q)) + 1.0
        k = jax.nn.elu(apply_rope(k)) + 1.0

        def chunked(y):
            return y.reshape(b, h, nc, cs, dk).transpose(2, 0, 1, 3, 4)
        qc, kc, vc, gc = (chunked(q), chunked(k), chunked(v), chunked(g))
        S0 = jnp.zeros((b, h, dk, dk), x.dtype)
        Z0 = jnp.zeros((b, h, dk), x.dtype)

        def step(carry, inp):
            S, Z = carry
            qi, ki, vi, gi = inp
            S = S + jnp.einsum('bhtd,bhte->bhde', ki, vi)
            Z = Z + ki.sum(axis=2)
            num = jnp.einsum('bhtd,bhde->bhte', qi, S)
            den = jnp.einsum('bhtd,bhd->bht', qi, Z)[..., None] + 1e-06
            return ((S, Z), gi * num / den)
        _, out = lax.scan(step, (S0, Z0), (qc, kc, vc, gc))
        out = out.transpose(1, 2, 0, 3, 4).reshape(b, h, t, dk)
        out = out.transpose(0, 2, 1, 3).reshape(b, t, c)
        return out @ Wo.T + bo

    def _L1_xattn_ref(hidden_states, ssm_states, Wq, Wk, Wv, Wsk, Wsv, Wo):
        import jax, jax.numpy as jnp
        import numpy as np
        HID = 256
        H = 32
        HK = 8
        G = H // HK
        D = HID // H
        T = 128
        W_ATT = 32
        W_SSM = 64

        def _heads(x, n):
            B, Tt, _ = x.shape
            return x.reshape(B, Tt, n, D).transpose(0, 2, 1, 3)

        def _attend(q, k, v):
            pos = jnp.arange(T)
            rel = pos[None, :] - pos[:, None]
            slopes = jnp.power(2.0, -8.0 * jnp.arange(H, dtype=jnp.float32) / H)
            alibi = slopes[:, None, None] * rel.astype(jnp.float32)
            bias = jnp.concatenate([alibi, alibi], axis=-1)
            delta = -rel
            ssm_mask = (delta >= 0) & (delta < W_SSM)
            att_mask = (delta >= 0) & (delta < W_ATT)
            mask = jnp.concatenate([ssm_mask, att_mask], axis=-1)
            scores = jnp.einsum('bhqd,bhkd->bhqk', q, k) / np.sqrt(D).astype(np.float32)
            scores = scores + bias[None]
            scores = jnp.where(mask[None, None], scores, -jnp.inf)
            wei = jax.nn.softmax(scores, axis=-1)
            return jnp.einsum('bhqk,bhkd->bhqd', wei, v)
        B = hidden_states.shape[0]
        q = _heads(jnp.concatenate([ssm_states, hidden_states], axis=-1) @ Wq, H)
        k = _heads(hidden_states @ Wk, HK)
        v = _heads(hidden_states @ Wv, HK)
        ssm_k = _heads(ssm_states @ Wsk, HK)
        ssm_v = _heads(ssm_states @ Wsv, HK)
        rep = lambda x: jnp.repeat(x, G, axis=1)
        kcat = jnp.concatenate([rep(ssm_k), rep(k)], axis=2)
        vcat = jnp.concatenate([rep(ssm_v), rep(v)], axis=2)
        o = _attend(q, kcat, vcat)
        o = o.transpose(0, 2, 1, 3).reshape(B, T, HID)
        return o @ Wo

    def _L1_ffn_ref(hidden_states, router_weight, gate_up_proj, down_proj, sh_gate_w, sh_up_w, sh_down_w, shared_gate_w):
        import jax, jax.numpy as jnp
        import numpy as np
        E = 8
        TOP_K = 2
        H = 256
        I_MOE = 176
        I_SH = 704
        B, S = (2, 256)

        def _moe_forward(hidden_states, router_weight, gate_up_proj, down_proj, sh_gate_w, sh_up_w, sh_down_w, shared_gate_w):
            b, s, h = hidden_states.shape
            x = hidden_states.reshape(-1, h)
            shared = jnp.einsum('ti,hi->th', jax.nn.silu(x @ sh_gate_w.T) * (x @ sh_up_w.T), sh_down_w)
            logits = x @ router_weight.T
            probs = jax.nn.softmax(logits.astype(jnp.float32), axis=-1)
            top_v, top_i = jax.lax.top_k(probs, TOP_K)
            top_v = top_v / top_v.sum(axis=-1, keepdims=True)
            combine = (jax.nn.one_hot(top_i, E, dtype=top_v.dtype) * top_v[..., None]).sum(axis=1)
            out = jnp.zeros_like(x)
            for e in range(E):
                gu = x @ gate_up_proj[e].T
                gate, up = (gu[:, :I_MOE], gu[:, I_MOE:])
                cur = jax.nn.silu(gate) * up @ down_proj[e].T
                out = out + cur * combine[:, e:e + 1]
            out = out + jax.nn.sigmoid(x @ shared_gate_w.T) * shared
            return out.reshape(b, s, h)
        return _moe_forward(hidden_states, router_weight, gate_up_proj, down_proj, sh_gate_w, sh_up_w, sh_down_w, shared_gate_w)
    x = _layernorm(x + _L0_attn_ref(x, L0_attn_W_in, L0_attn_b_in, L0_attn_W_out, L0_attn_b_out), axis=-1)
    x = _layernorm(x + _L0_xattn_ref(x, ctx_2048, L0_xattn_W_fc, L0_xattn_b_fc, L0_xattn_W_q, L0_xattn_b_q, L0_xattn_W_k, L0_xattn_b_k, L0_xattn_W_v, L0_xattn_b_v), axis=-1)
    x = _layernorm(x + _L0_ffn_ref(x, L0_ffn_gate_weight, L0_ffn_gate_up_weights, L0_ffn_down_weights), axis=-1)
    x = _layernorm(x + _L1_attn_ref(x, L1_attn_Wq, L1_attn_bq, L1_attn_Wk, L1_attn_bk, L1_attn_Wv, L1_attn_bv, L1_attn_Wg, L1_attn_bg, L1_attn_Wo, L1_attn_bo), axis=-1)
    x = _layernorm(x + _L1_xattn_ref(x, ctx_2048, L1_xattn_Wq, L1_xattn_Wk, L1_xattn_Wv, L1_xattn_Wsk, L1_xattn_Wsv, L1_xattn_Wo), axis=-1)
    x = _layernorm(x + _L1_ffn_ref(x, L1_ffn_router_weight, L1_ffn_gate_up_proj, L1_ffn_down_proj, L1_ffn_sh_gate_w, L1_ffn_sh_up_w, L1_ffn_sh_down_w, L1_ffn_shared_gate_w), axis=-1)
    return x

_drawn_inputs = setup_inputs


def setup_inputs(seed=0):
    import zlib

    import numpy as np

    out = dict(_drawn_inputs(seed))
    spreads = {'L0_attn_b_in': (0.0, 0.1),
     'L0_attn_b_out': (0.0, 0.1),
     'L0_xattn_b_fc': (0.0, 0.1),
     'L0_xattn_b_q': (0.0, 0.8),
     'L0_xattn_b_k': (0.0, 2.0),
     'L0_xattn_b_v': (0.0, 0.1),
     'L1_attn_bq': (0.0, 2.0),
     'L1_attn_bk': (0.0, 2.0),
     'L1_attn_bv': (0.0, 0.454),
     'L1_attn_bg': (0.0, 0.8),
     'L1_attn_bo': (0.0, 0.1)}
    factors = {'L0_xattn_W_q': 8.0,
     'L0_xattn_W_k': 8.0,
     'L0_ffn_gate_weight': 8.0,
     'L0_ffn_gate_up_weights': 8.0,
     'L0_ffn_down_weights': 8.0,
     'L1_attn_Wq': 8.0,
     'L1_attn_Wk': 8.0,
     'L1_attn_Wv': 4.336,
     'L1_attn_Wg': 8.0,
     'L1_ffn_router_weight': 6.519,
     'L1_ffn_gate_up_proj': 5.666,
     'L1_ffn_down_proj': 5.683,
     'L1_ffn_sh_gate_w': 3.962,
     'L1_ffn_sh_up_w': 3.892,
     'L1_ffn_sh_down_w': 3.899,
     'L1_ffn_shared_gate_w': 8.0}
    for name, (base, spread) in spreads.items():
        noise = np.random.default_rng([zlib.crc32(name.encode()), seed]).standard_normal(out[name].shape)
        drawn = base * np.exp(spread * noise) if base else spread * noise
        out[name] = jnp.asarray(drawn.astype(out[name].dtype))
    for name, factor in factors.items():
        out[name] = (out[name] * factor).astype(out[name].dtype)
    return out
```

```python
from contextlib import ExitStack

import numpy as np

import concourse.bass as bass
from concourse import mybir

F32 = mybir.dt.float32
F32R = mybir.dt.float32r
BF16 = mybir.dt.bfloat16
ALU = mybir.AluOpType
ACT = mybir.ActivationFunctionType
AX = mybir.AxisListType

P = 128
B = 8
T = B * P
D = 256
C = D // P
VW = 32
DH0, H0 = 16, 16
DH1, KV1, G1 = 8, 8, 4
HALF = 512
EPS = 1e-5
E0, I0, TOP0 = 64, 96, 8
E1, I1, TOP1 = 8, 176, 2
IH1 = 88
ISH = 704
PARTS1 = E1 * I1 // IH1 + ISH // IH1
SENT = -3.0e38


def build(nc, a, out):
    ctx = ExitStack()
    with ctx:
        def sb(name, shape, dt=F32):
            return ctx.enter_context(nc.sbuf_tensor(name, shape, dt))

        sems = {}

        def S(name):
            if name not in sems:
                sems[name] = ctx.enter_context(nc.semaphore(name))
            return sems[name]

        loads = {}

        def const(layer, name, dt=F32):
            src = a[name]
            t = sb("c_" + name, list(src.shape), dt)
            loads.setdefault(layer, []).append((t[:, :].bitcast(src.dtype) if dt == BF16 else t, src))
            return t

        arena = sb("arena", [P, 9856])
        filled = {"AB": 0, "DE": 0}

        def weight(layer, name):
            src = a[f"{layer}_{name}"]
            both = "AB" if layer in "AB" else "DE"
            n = int(np.prod(src.shape[1:]))
            t = arena[:, filled[both]:filled[both] + n]
            filled[both] += n
            assert filled[both] <= arena.shape[1]
            if len(src.shape) == 3:
                t = t.rearrange("p (c n) -> p c n", c=src.shape[1])
            loads.setdefault(layer, []).append((t, src))
            W[layer, name] = t

        W = {}

        XT = const("A", "x_t")
        X = const("A", "x_rows")
        hmask = const("A", "head_mask")
        causal = const("A", "causal_bf16", BF16)
        ident16 = const("A", "ident_bf16", BF16)
        ident = const("A", "ident")
        CTXT = const("B", "ctx_t")
        for layer, names in (("A", "wq wk wv bq bk bv wo bo"),
                             ("B", "wfc bfc wq wk wv bq bk bv ones_v wr"),
                             ("D", "wqk wv wg bqk bv bg wo bo cos sin_lo sin_hi blocks"),
                             ("E", "wq wk wsk wv wsv wo ones_v wr")):
            for n in names.split():
                weight(layer, n)
        gmask = const("E", "group_mask")
        window = const("E", "window_bf16", BF16)

        xs = [sb(f"xs{u}", [P, C, P]) for u in range(2)]
        cs = [sb(f"cs{u}", [P, C, P]) for u in range(2)]
        refT = [sb(f"refT{u}", [P, C, P]) for u in range(2)]
        supT = [sb(f"supT{u}", [P, C, P]) for u in range(2)]
        qT = [sb(f"qT{u}", [P, C, P]) for u in range(2)]
        kbd = [sb(f"kbd{u}", [P, C, 8, P]) for u in range(2)]
        qm = [sb(f"qm{u}", [P, KV1, G1, P]) for u in range(2)]
        kT = [sb(f"kT{u}", [P, 2, P]) for u in range(2)]
        v = [sb(f"v{u}", [P, 2 * D]) for u in range(2)]
        e = [sb(f"e{u}", [P, 1024]) for u in range(2)]
        pT = [sb(f"pT{u}", [P, 1024]) for u in range(2)]
        mx = [sb(f"mx{u}", [P, 8]) for u in range(2)]
        oT = sb("oT", [P, 2, HALF])
        rden = sb("rden", [P, 2, 16])
        an = sb("an", [P, D])
        aT = sb("aT", [P, C, P])
        xb = sb("xb", [P, D])
        z1 = sb("z1", [P, D])
        z = sb("z", [P, D])
        stats = sb("stats", [P, 6])
        agg = sb("agg", [P, 2])
        ve = sb("ve", [P, 1])
        lnv = sb("lnv", [P, 1])
        y0 = sb("y0", [P, 1])
        nt = sb("nt", [P, 3])
        rstd = sb("rstd", [P, 1])
        xn = [sb(f"xn{u}", [P, D]) for u in range(2)]
        qk = e[0][:, 0:512]
        ra = e[0][:, 512:1024]
        rb = e[1][:, 0:512]
        rr = e[1][:, 512:1024]
        rn = pT[0][:, 0:512]
        re = pT[0][:, 512:1024]
        f = [sb(f"f{u}", [P, 2 * D]) for u in range(2)]
        gx = refT[0][:, :, :].rearrange("p c q -> p (c q)")
        eg = [supT[u][:, :, :].rearrange("p c q -> p (c q)") for u in range(2)]
        qfT = cs[0]
        gm = oT
        den = sb("den", [P, 16])
        d2 = sb("d2", [P, D])
        r2 = sb("r2", [P, D])
        xf = sb("xf", [P, C, P])
        lg = sb("lg", [P, 64 + 16])
        top = sb("top", [P, 8])
        nmax = sb("nmax", [P, 1])
        lrep = sb("lrep", [P, 64 + 16])
        msk = sb("msk", [P, 64])
        ex = sb("ex", [P, 64])
        em = sb("em", [P, 64])
        esum = sb("esum", [P, 1])
        einv = sb("einv", [P, 1])
        cm = sb("cm", [P, P])
        sg = sb("sg", [P, 3])
        cT = sb("cT", [64, T])
        XH = sb("XH", [P, C, T], F32R)
        XL = sb("XL", [P, C, T], F32R)
        WCOLS = 2 * 2 * I0 + D
        NW = 4
        qm_flat = [m[:, :, :, :].rearrange("p g j q -> p (g j q)") for m in qm]
        wraw = [qm_flat[k // 2][:, (k % 2) * WCOLS:(k % 2 + 1) * WCOLS] for k in range(NW)]
        wh = [sb(f"wh{u}", [P, WCOLS], F32R) for u in range(2)]
        wl = [sb(f"wl{u}", [P, WCOLS], F32R) for u in range(2)]
        wbc = [kbd[k // 2][:, k % 2].rearrange("p h k -> p (h k)") for k in range(NW)]
        sgt = [e[u][:, 0:HALF] for u in range(2)]
        a1 = [e[u][:, HALF:2 * HALF] for u in range(2)]
        a2 = [pT[u][:, 0:HALF] for u in range(2)]
        ah = [sb(f"ah{u}", [P, HALF], F32R) for u in range(2)]
        al = [sb(f"al{u}", [P, HALF], F32R) for u in range(2)]
        zero16 = sb("zero16", [P, HALF], BF16)
        yT = xs

        combine = {"C": nc.dram_tensor("combine0", [E0, T], F32).ap(),
                   "F": nc.dram_tensor("combine1", [PARTS1, T], F32).ap()}

        ps = ctx.enter_context(nc.psum_tensor("ps", [P, 8, HALF], F32))
        SLOT = [ps[:, 2 * s:2 * s + 2, :] for s in range(2)]
        PT = [ps[:, 4 + s, :] for s in range(2)]
        OB = ps[:, 6, :]
        MB = ps[:, 7, :]
        Y = ps[:, 0:4, :]
        GU = [[ps[:, 4 + 2 * t + s, :] for s in range(2)] for t in range(2)]

        def tok(b):
            return bass.ds(b * P, P)

        def bc(ap, axis, n):
            x = ap.unsqueeze(axis)
            shape = list(x.shape)
            shape[axis] = n
            return x.to_broadcast(shape)

        ATTN = ("A", "B", "D", "E")
        UNITS = {"A": 2, "B": 2, "E": 8, "D": 0}
        ORDER = "ABCDEF"

        def nb(L, n):
            return ORDER.index(L) * B + n

        def nu(L, n):
            return sum(UNITS[M] * B for M in ORDER[:ORDER.index(L)] if M in UNITS) + n

        BEFORE = {"B": "A", "C": "B", "D": "C", "E": "D", "F": "E"}
        NEXT_IS_MOE = ("B", "E")
        OTN = {"A": 1, "B": 1, "E": 2}
        LNSTEPS = 8

        def loaded(eng, layer):
            eng.wait_ge(S(f"{layer}_loaded"), 16 * len(loads[layer]))

        def settle(eng):
            eng.sem_inc(S("settled"), 1)

        def before_done(eng, L):
            if L in BEFORE:
                p = BEFORE[L]

                eng.wait_ge(S("xt"), nb(L, 1))
                eng.wait_ge(S("xrow"), nb(L, 2))
                if p in NEXT_IS_MOE:
                    eng.wait_ge(S(f"{p}_xl"), B)
                    eng.wait_ge(S(f"{p}_cT"), B)

        def batches(eng, proj, core, fin):
            proj(0, 0)
            with eng.Fori(0, B // 2 - 1) as j:
                core(j * 2, 0)
                proj(j * 2 + 1, 1)
                fin(j * 2, 0)
                core(j * 2 + 1, 1)
                proj(j * 2 + 2, 0)
                fin(j * 2 + 1, 1)
            core(B - 2, 0)
            proj(B - 1, 1)
            fin(B - 2, 0)
            core(B - 1, 1)
            fin(B - 1, 1)

        block = ctx.enter_context(nc.Block())

        def moe_loads(sp, L):
            n_e, I, src = (E0, I0, "C") if L == "C" else (PARTS1, IH1, "F")
            sp.wait_ge(S(f"{BEFORE[L]}_cT"), B)
            settle(sp)
            if L == "C":
                sp.dma_start(combine[L], cT[0:E0, :]).then_inc(S("combine0_out"), 16)
                sp.wait_ge(S("combine0_out"), 16)
                settle(sp)
            else:
                two = E1 * I1 // IH1 // E1
                for k in range(two):
                    sp.dma_start(combine[L][0:E1 * two].rearrange("(e k) t -> k e t", k=two)[k],
                                 cT[0:E1, :]).then_inc(S("combine1_out"), 16)
                for k in range(ISH // IH1):
                    sp.dma_start(combine[L][E1 * two + k:E1 * two + k + 1], cT[E1:E1 + 1, :])\
                      .then_inc(S("combine1_out"), 16)
                sp.wait_ge(S("combine1_out"), 16 * (two + ISH // IH1))
                settle(sp)

            def load(x, k):
                w = wraw[k]
                gu = w[:, 0:4 * I].rearrange("p (c n) -> p c n", c=C)
                sp.dma_start(gu, a[f"{L}_gu"][bass.ds(x, 1)].rearrange("o (c p) n -> p (o c) n", p=P))\
                  .then_inc(S(f"{L}_w{k}"), 16)
                sp.dma_start(w[0:I, 4 * I:4 * I + D], a[f"{L}_down"][bass.ds(x, 1)].rearrange("o i n -> i (o n)"))\
                  .then_inc(S(f"{L}_w{k}"), 16)
                sp.dma_start(wbc[k][0:I, :], combine[L][bass.ds(x, 1)].to_broadcast([I, T]))\
                  .then_inc(S(f"{L}_w{k}"), 16)

            for k in range(NW):
                load(k, k)
            if L == "C":
                for M in ("D", "E"):
                    for t, src in loads[M]:
                        sp.dma_start(t[tuple(slice(None) for _ in t.shape)], src).then_inc(S(f"{M}_loaded"), 16)
            with sp.Fori(1, n_e // NW) as j:
                for k in range(NW):
                    sp.wait_ge(S(f"{L}_wl"), j * (2 * NW) - 2 * NW + 2 * k + 2)
                    settle(sp)
                    sp.wait_ge(S(f"{L}_a2"), j * (2 * NW) - 2 * NW + 2 * k + 2)
                    settle(sp)
                    load(j * NW + k, k)

        @block.sync
        def _(sp):
            sp.sem_inc(S("sub"), 2)
            sp.sem_inc(S("z"), 1)
            sp.sem_inc(S("trb"), 2)
            sp.sem_inc(S("pca"), 1)
            sp.sem_inc(S("pcb"), 1)
            sp.sem_inc(S("pv"), 2)
            sp.sem_inc(S("xt"), 1)
            sp.sem_inc(S("xrow"), 2)
            for L in ATTN:
                sp.sem_inc(S(f"{L}_vps"), 2)
            def load_weights(L):
                for t, src in loads[L]:
                    sp.dma_start(t[tuple(slice(None) for _ in t.shape)], src).then_inc(S(f"{L}_loaded"), 16)

            load_weights("A")
            load_weights("B")
            moe_loads(sp, "C")
            sp.wait_ge(S("C_wl"), 2 * E0)
            settle(sp)
            for u in range(2):
                sp.dma_start(qm[u][64:128].rearrange("p g j q -> p (g j q)"), a["E_qrow"]).then_inc(S("qrow"), 16)
                sp.dma_start(kT[u][64:128].rearrange("p s k -> p (s k)"), a["E_krow"]).then_inc(S("krow"), 16)
            moe_loads(sp, "F")
            with sp.Fori(0, B // 2) as j:
                for u in range(2):
                    sp.wait_ge(S("xrow"), nb("F", j * 2 + u + 3))
                    settle(sp)
                    sp.dma_start(out[bass.ds(j * 2 + u, 1)].rearrange("b p d -> p (b d)"),
                                 xn[u][:, :]).then_inc(S(f"stored{u}"), 16)
            for u in range(2):
                sp.wait_ge(S(f"stored{u}"), 16 * B // 2)
            settle(sp)

        def pe_proj_T(pe, dst, w, src, m=P):
            for c in range(C):
                for k in range(C):
                    mm = pe.matmul(dst[0:m, c * P:(c + 1) * P], w[:, k, c * m:(c + 1) * m], src[:, k, :],
                                   start=(k == 0), stop=(k == C - 1))
            return mm

        def pe_proj_rows(pe, dst, w, src, cols, at=0):
            for k in range(C):
                mm = pe.matmul(dst, src[:, k, :], w[:, k, at:at + cols], start=(k == 0), stop=(k == C - 1))
            return mm

        def pe_attention(pe, L):
            U = UNITS[L]
            loaded(pe, L)
            before_done(pe, L)
            if L == "E":
                pe.wait_ge(S("qrow"), 32)
                pe.wait_ge(S("krow"), 32)

            def proj(i, u):
                pe.wait_ge(S(f"{L}_xs"), i + 1)
                if not (isinstance(i, int) and i == 0):
                    pe.wait_ge(S("xt"), nb(L, i))
                if L == "A":
                    pe_proj_T(pe, MB[:, 0:D], W[L, "wq"], xs[u])
                    pe_proj_T(pe, MB[:, D:2 * D], W[L, "wk"], xs[u]).then_inc(S("A_qkps"), 1)
                if L == "B":
                    pe_proj_T(pe, MB[:, 0:D], W[L, "wfc"], xs[u])
                    pe_proj_T(pe, MB[:, D:2 * D], W[L, "wfc"], cs[u]).then_inc(S("B_fcps"), 1)
                    pe.wait_ge(S("B_fc"), i * 4 + 4)
                    pe_proj_T(pe, MB[:, 0:D], W[L, "wq"], refT[u])
                    pe_proj_T(pe, MB[:, D:2 * D], W[L, "wk"], supT[u]).then_inc(S("B_qkps"), 1)
                if L == "E":
                    for j in range(G1):
                        for k in range(2 * C):
                            mm = pe.matmul(MB[0:64, j * P:(j + 1) * P], W[L, "wq"][:, k, j * 64:(j + 1) * 64],
                                           (cs if k < C else xs)[u][:, k % C, :], start=(k == 0), stop=(k == 2 * C - 1))
                    mm.then_inc(S("E_qps"), 1)
                    pe.wait_ge(S("E_qm"), i * 2 + 2)
                    for s, (wn, src) in enumerate((("wsk", cs), ("wk", xs))):
                        for k in range(C):
                            mm = pe.matmul(MB[0:64, s * P:(s + 1) * P], W[L, wn][:, k, :], src[u][:, k, :],
                                           start=(k == 0), stop=(k == C - 1))
                    mm.then_inc(S("E_kps"), 1)
                if L == "D":
                    pe_proj_rows(pe, MB, W[L, "wqk"], xs[u], 2 * D).then_inc(S("D_qkps"), 1)
                    if not (isinstance(i, int) and i == 0):
                        pe.wait_ge(S("D_v"), i)
                        pe.wait_ge(S("D_gx"), i)
                    pe_proj_rows(pe, ps[:, 0, 0:D], W[L, "wg"], xs[u], D).then_inc(S("D_gps"), 1)
                elif not (isinstance(i, int) and i == 0):
                    pe.wait_ge(S(f"{L}_ot"), i * OTN[L])
                if L == "E":
                    for s, (wn, src) in enumerate((("wsv", cs), ("wv", xs))):
                        mm = pe_proj_rows(pe, OB[:, s * D:(s + 1) * D], W[L, wn], src[u], D)
                    mm.then_inc(S("E_vps"), 1)
                else:
                    pe_proj_rows(pe, OB, W[L, "wv"], (supT if L == "B" else xs)[u], 2 * D).then_inc(S(f"{L}_vps"), 1)

            def scores(b, u, n):
                g = b * U + n
                pe.wait_ge(S("sub"), nu(L, g + 1))
                sl = SLOT[n % 2]
                for h in range(2):
                    if L == "A":
                        pe.matmul(sl[:, h, :], ident16[:, :], causal[:, :], start=True, stop=False)
                    if L == "E":
                        pe.matmul(sl[:, h, :], ident16[:, :], bc(window[:, :], 1, 2), start=True, stop=False,
                                  skip_group_check=True)
                        for q in range(2):
                            mm = pe.matmul(sl[:, h, q * D:(q + 1) * D], qm[u][:, n, 2 * h + q, :],
                                           kT[u][:, :, :], start=False, stop=True, skip_group_check=True)
                    else:
                        mm = pe.matmul(sl[:, h, :], qT[u][:, n, :], kbd[u][:, n, 4 * h:4 * h + 4, :],
                                       start=(L == "B"), stop=True)
                mm.then_inc(S("sps"), 1)

            def transposes(b, n):
                g = b * U + n
                pe.wait_ge(S("exp"), nu(L, g + 1))
                for h, (free, done) in enumerate((("pca", "tra"), ("pcb", "trb"))):
                    pe.wait_ge(S(free), nu(L, g + 1))
                    for q in range(4):
                        at = (q * 2 + h) * P if L == "E" else (h * 4 + q) * P
                        mm = pe.transpose(PT[h][:, q * P:(q + 1) * P], e[n % 2][:, at:at + P], ident[:, :])
                    mm.then_inc(S(done), 1)

            def values(b, u, n):
                g = b * U + n
                pe.wait_ge(S("pca"), nu(L, g + 2))
                pe.wait_ge(S("pcb"), nu(L, g + 2))
                if n == 0:
                    pe.wait_ge(S(f"{L}_v"), b + 1)
                if L == "E":
                    if n == 4:
                        pe.wait_ge(S("E_ot"), b * 2 + 1)
                    r = 32 * (n % 4)
                    for s in range(2):
                        mm = pe.matmul(OB[r:r + VW, :], v[u][:, s * D + n * VW:s * D + (n + 1) * VW],
                                       pT[n % 2][:, s * HALF:(s + 1) * HALF], start=(s == 0), stop=(s == 1),
                                       tile_position=(0, r))
                else:
                    for h in range(8):
                        r, blk, head = 32 * (h % 4), 2 * n + h // 4, 8 * n + h
                        mm = pe.matmul(OB[r:r + VW, blk * P:(blk + 1) * P], v[u][:, head * VW:(head + 1) * VW],
                                       pT[n % 2][:, h * P:(h + 1) * P], start=True, stop=True,
                                       tile_position=(0, r))
                mm.then_inc(S("pv"), 1)

            def core(b, u):
                if L == "D":
                    pe.wait_ge(S("D_f"), b + 1)
                    for c in range(C):
                        mm = pe.transpose(ps[:, 1, c * P:(c + 1) * P], f[u][:, c * P:(c + 1) * P], ident[:, :])
                    mm.then_inc(S("D_qfps"), 1)
                    pe.wait_ge(S("D_v"), b + 1)
                    for n, rows in enumerate((P // 2, P)):
                        for c in range(C):
                            mm = pe.matmul(ps[:, 2 + n, c * D:(c + 1) * D], f[u][0:rows, D + c * P:D + (c + 1) * P],
                                           v[u][0:rows, c * D:(c + 1) * D], start=True, stop=True)
                    mm.then_inc(S("D_gmps"), 1)
                    pe.wait_ge(S("D_qf"), b + 1)
                    pe.wait_ge(S("D_gm"), b * 2 + 2)
                    for n in range(2):
                        r = 64 * n
                        for c in range(C):
                            mm = pe.matmul(ps[r:r + 64, 4, c * D:(c + 1) * D], qfT[:, c, r:r + 64],
                                           gm[:, n, c * D:(c + 1) * D], start=True, stop=True,
                                           tile_position=(0, r))
                    mm.then_inc(S("D_num"), 1)
                    return
                if L == "E":
                    pe.wait_ge(S("E_kT"), b + 1)
                else:
                    pe.wait_ge(S(f"{L}_q"), b * 2 + 2)
                    pe.wait_ge(S(f"{L}_kbd"), b * 2 + 2)
                scores(b, u, 0)
                for n in range(U):
                    if n + 1 < U:
                        scores(b, u, n + 1)
                    transposes(b, n)
                    if n:
                        values(b, u, n - 1)
                values(b, u, U - 1)

            def fin(b, u):
                if L != "D":
                    for r in range(OTN[L]):
                        pe.wait_ge(S(f"{L}_ot"), b * OTN[L] + r + 1)
                        if r == 0:
                            if L == "E":
                                pe.wait_ge(S("E_kT"), b + 2 if not (isinstance(b, int) and b == B - 1) else B)
                            else:
                                last = isinstance(b, int) and b == B - 1
                                pe.wait_ge(S(f"{L}_q"), 2 * B if last else b * 2 + 4)
                                pe.wait_ge(S(f"{L}_kbd"), 2 * B if last else b * 2 + 4)
                        else:
                            pe.wait_ge(S(f"{L}_an"), b * OTN[L] + r)
                        for k in range(4):
                            mm = pe.transpose(MB[:, k * P:(k + 1) * P], oT[:, r, k * P:(k + 1) * P], ident[:, :])
                        mm.then_inc(S(f"{L}_otr"), 1)
                    pe.wait_ge(S(f"{L}_an"), (b + 1) * OTN[L])
                else:
                    last = isinstance(b, int) and b == B - 1
                    pe.wait_ge(S("D_qk"), B if last else b + 2)
                    pe.wait_ge(S("D_an"), b + 1)
                if L == "B":
                    for c in range(C):
                        mm = pe.transpose(MB[:, D + c * P:D + (c + 1) * P], refT[u][:, c, :], ident[:, :])
                    mm.then_inc(S("y"), 1)
                else:
                    for c in range(C):
                        mm = pe.transpose(MB[:, c * P:(c + 1) * P], an[:, c * P:(c + 1) * P], ident[:, :])
                    mm.then_inc(S(f"{L}_atr"), 1)
                    pe.wait_ge(S(f"{L}_at"), b + 1)
                    for c in range(C):
                        mm = pe.matmul(MB[:, D:2 * D], aT[:, c, :], W[L, "wo"][:, c, :], start=(c == 0), stop=(c == C - 1))
                    mm.then_inc(S("y"), 1)
                pe_x(b, u, L)

            def pe_x(b, u, L):
                pe_norm(pe, b, u, L)

            batches(pe, proj, core, fin)

        def pe_norm(pe, b, u, L):
            if L == "F":
                return
            pe.wait_ge(S("xn"), nb(L, b + 1))
            for c in range(C):
                mm = pe.transpose(MB[:, c * P:(c + 1) * P], xn[u][:, c * P:(c + 1) * P], ident[:, :])
            mm.then_inc(S("xtr"), 1)
            if L not in NEXT_IS_MOE:
                return
            nl = 64 if L == "B" else 16
            pe.wait_ge(S(f"{L}_xf"), b + 1)
            pe.wait_ge(S(f"{L}_xl"), b + 1)
            for c in range(C):
                mm = pe.matmul(MB[:, D:D + nl], xf[:, c, :], W[L, "wr"][:, c, :], start=(c == 0), stop=(c == C - 1))
            mm.then_inc(S(f"{L}_lgps"), 1)
            pe.wait_ge(S(f"{L}_cm"), b + 1)
            pe.transpose(MB[:, D:D + P], cm[:, :], ident[:, :]).then_inc(S(f"{L}_cps"), 1)

        def pe_moe(pe, L):
            n_e, I = (E0, I0) if L == "C" else (PARTS1, IH1)
            before_done(pe, L)
            for m in range(4):
                pe.matmul(Y[:, m, :], ident16[:, :], zero16[:, :], start=True, stop=False, skip_group_check=True)

            def gate_up(x, u, t):
                if t == 0:
                    pe.wait_ge(S(f"{L}_wl"), x * 2 + 1)
                if not (isinstance(x, int) and x == 0):
                    pe.wait_ge(S(f"{L}_a1"), x * 2 + t - 1)
                for s in range(2):
                    i = 0
                    for w, xx in ((wh, XH), (wl, XH), (wh, XL)):
                        for c in range(C):
                            mm = pe.matmul(GU[t][s][0:I, :], w[u][:, c * 2 * I + s * I:c * 2 * I + (s + 1) * I],
                                           xx[:, c, t * HALF:(t + 1) * HALF], start=(i == 0), stop=(i == 5))
                            i += 1
                    mm.then_inc(S(f"{L}_gu"), 1)

            def down(x, u, t):
                if t == 0:
                    pe.wait_ge(S(f"{L}_wl"), x * 2 + 2)
                pe.wait_ge(S(f"{L}_al"), x * 2 + t + 1)
                for m in range(C):
                    for w, x_ in ((wh, ah), (wl, ah), (wh, al)):
                        mm = pe.matmul(Y[:, 2 * m + t, :], w[u][0:I, 4 * I + m * P:4 * I + (m + 1) * P],
                                       x_[t][0:I, :], start=False, stop=False, skip_group_check=True)
                mm.then_inc(S(f"{L}_down"), 1)

            for t in range(2):
                gate_up(0, 0, t)
            with pe.Fori(0, n_e // 2 - 1) as j:
                for s in range(2):
                    for t in range(2):
                        gate_up(j * 2 + 1 + s, 1 - s, t)
                        down(j * 2 + s, s, t)
            for t in range(2):
                gate_up(n_e - 1, 1, t)
                down(n_e - 2, 0, t)
            for t in range(2):
                down(n_e - 1, 1, t)

            def fin(b, u):
                pe.wait_ge(S(f"{L}_yt"), b + 1)
                if L == "F":
                    pe.wait_ge(S("z"), nb(L, b + 1))
                else:
                    pe.wait_ge(S("xt"), nb(L, b + 1))
                for c in range(C):
                    mm = pe.transpose(MB[:, D + c * P:D + (c + 1) * P], yT[u][:, c, :], ident[:, :])
                mm.then_inc(S("y"), 1)
                pe_norm(pe, b, u, L)

            fin(0, 0)
            fin(1, 1)
            with pe.Fori(1, B // 2) as j:
                fin(j * 2, 0)
                fin(j * 2 + 1, 1)

        @block.tensor
        def _(pe):
            for L in ATTN:
                pe_attention(pe, L)
                if L in NEXT_IS_MOE:
                    pe_moe(pe, "C" if L == "B" else "F")

        def act_attention(act, L):
            U = UNITS[L]
            scale = 0.25 if L != "E" else float(1.0 / np.sqrt(np.float32(DH1)))
            loaded(act, L)
            before_done(act, L)

            def proj(i, u):
                if L == "B":
                    act.wait_ge(S("B_fcps"), i + 1)
                    for n, dst in enumerate((refT, supT)):
                        for c in range(C):
                            act.activation(dst[u][:, c, :], MB[:, n * D + c * P:n * D + (c + 1) * P], ACT.Relu,
                                           bias=W[L, "bfc"][:, c:c + 1]).then_inc(S("B_fc"), 1)
                if L in ("A", "B"):
                    act.wait_ge(S(f"{L}_qkps"), i + 1)
                    for c in range(C):
                        act.activation(qT[u][:, c, :], MB[:, c * P:(c + 1) * P], ACT.Identity,
                                       bias=W[L, "bq"][:, c:c + 1]).then_inc(S(f"{L}_q"), 1)
                if L == "D":
                    act.wait_ge(S("D_gx"), i + 1)
                    act.activation(eg[u][:, :], gx[:, :], ACT.Exp, scale=-1.0).then_inc(S("D_eg"), 1)
                    act.wait_ge(S("D_rn"), i + 1)
                    act.activation(re[:, :], rn[:, :], ACT.Exp).then_inc(S("D_re"), 1)
                if L == "E":
                    act.wait_ge(S("E_qm"), i * 2 + 1)
                    for g in range(4, KV1):
                        ins = act.activation(qm[u][0:64, g].rearrange("p j q -> p (j q)"), MB[0:64, :], ACT.Copy,
                                             scale=gmask[:, g:g + 1])
                    ins.then_inc(S("E_qm_act"), 1)
                    act.wait_ge(S("E_kps"), i + 1)
                    act.activation(kT[u][0:64].rearrange("p s k -> p (s k)"), MB[0:64, 0:2 * P], ACT.Copy)\
                       .then_inc(S("E_kT"), 1)

            def unit(b, n):
                g = b * U + n
                act.wait_ge(S("sub"), nu(L, g + 3))
                act.activation(e[n % 2][:, :], e[n % 2][:, :], ACT.Exp, scale=scale).then_inc(S("exp"), 1)
                act.wait_ge(S("pv"), nu(L, g + 1))
                for h, (ready, done) in enumerate((("tra", "pca"), ("trb", "pcb"))):
                    act.wait_ge(S(ready), nu(L, g + 1 + 2 * h))
                    act.activation(pT[n % 2][:, h * HALF:(h + 1) * HALF], PT[h], ACT.Copy)\
                       .then_inc(S(done), 1)

            def core(b, u):
                if L == "D":
                    act.wait_ge(S("D_qfps"), b + 1)
                    act.activation(qfT[:, :, :].rearrange("p c q -> p (c q)"), ps[:, 1, 0:D], ACT.Copy)\
                       .then_inc(S("D_qf"), 1)
                    return
                for n in range(U):
                    unit(b, n)
                    if L == "E" and n == 4:
                        act.wait_ge(S("pv"), nu("E", b * U + 4 + 2))
                        act.activation(oT[:, 0, :], OB, ACT.Copy).then_inc(S("E_ot"), 1)
                act.wait_ge(S("pv"), nu(L, b * U + U + 2))
                act.activation(oT[:, OTN[L] - 1, :], OB, ACT.Copy).then_inc(S(f"{L}_ot"), 1)

            def fin(b, u):
                if L != "B":
                    act.wait_ge(S(f"{L}_atr"), b + 1)
                    act.activation(aT[:, :, :].rearrange("p c q -> p (c q)"), MB[:, 0:D], ACT.Copy)\
                       .then_inc(S(f"{L}_at"), 1)
                act_norm(act, b, u, L)

            batches(act, proj, core, fin)

        def act_norm(act, b, u, L):
            act.wait_ge(S("ve"), nb(L, b + 1))
            act.activation(lnv[:, :], ve[:, :], ACT.Ln).then_inc(S("lnv"), 1)
            act.wait_ge(S("lnv"), nb(L, b + 1))
            act.activation(y0[:, :], lnv[:, :], ACT.Exp, scale=-0.5).then_inc(S("y0"), 1)
            if L == "F":
                return
            act.wait_ge(S("xtr"), nb(L, b + 1))
            new = MB[:, 0:D].rearrange("p (c q) -> p c q", c=C)
            if L not in NEXT_IS_MOE:
                act.activation(XT[:, :, tok(b)], new, ACT.Copy).then_inc(S("xt"), 1)
                return
            act.activation(xf[:, :, :], new, ACT.Copy).then_inc(S(f"{L}_xf"), 1)
            act.activation(XH[:, :, tok(b)], new, ACT.Copy).then_inc(S(f"{L}_xh"), 1)
            nl = E0 if L == "B" else E1
            act.wait_ge(S(f"{L}_nmax"), b + 1)
            act.activation(ex[:, 0:nl], lg[:, 0:nl], ACT.Exp, bias=nmax[:, :]).then_inc(S(f"{L}_ex"), 1)
            if L == "E":
                act.activation(sg[:, 0:1], lg[:, 32:33], ACT.Exp, scale=-1.0).then_inc(S("E_sg"), 1)
            act.wait_ge(S(f"{L}_cps"), b + 1)
            act.activation(cT[0:64, tok(b)], MB[0:64, D:D + P], ACT.Copy).then_inc(S(f"{L}_cT"), 1)
            act.wait_ge(S(f"{L}_cT"), b + 1)
            act.activation(nt[:, 2:3], nmax[:, :], ACT.Copy).then_inc(S("xt"), 1)

        def act_moe(act, L):
            n_e, I = (E0, I0) if L == "C" else (PARTS1, IH1)
            before_done(act, L)

            def step(x, u, t):
                act.wait_ge(S(f"{L}_gu"), x * 4 + 2 * t + 1)
                if not (isinstance(x, int) and x == 0):
                    act.wait_ge(S(f"{L}_a1"), x * 2 + t - 1)
                act.activation(sgt[t][0:I, :], GU[t][0][0:I, :], ACT.Silu).then_inc(S(f"{L}_silu"), 1)
                act.wait_ge(S(f"{L}_a2"), x * 2 + t + 1)
                if not (isinstance(x, int) and x == 0):
                    act.wait_ge(S(f"{L}_down"), x * 2 + t - 1)
                act.activation(ah[t][0:I, :], a2[t][0:I, :], ACT.Copy).then_inc(S(f"{L}_ah"), 1)

            for t in range(2):
                step(0, 0, t)
            with act.Fori(1, n_e) as x:
                for t in range(2):
                    step(x, 0, t)

            def fin(b, u):
                if isinstance(b, int) and b == 0:
                    act.wait_ge(S(f"{L}_down"), 2 * n_e)
                if not (isinstance(b, int) and b < 2):
                    act.wait_ge(S("y"), nb(L, b - 1))
                act.activation(yT[u][:, :, :], Y.rearrange("p (c a) t -> p c (a t)", c=C)[:, :, tok(b)], ACT.Copy)\
                   .then_inc(S(f"{L}_yt"), 1)
                act_norm(act, b, u, L)

            fin(0, 0)
            fin(1, 1)
            with act.Fori(1, B // 2) as j:
                fin(j * 2, 0)
                fin(j * 2 + 1, 1)

        @block.scalar
        def _(act):
            for L in ATTN:
                act_attention(act, L)
                if L in NEXT_IS_MOE:
                    act_moe(act, "C" if L == "B" else "F")

        def dve_attention(dve, L):
            U = UNITS[L]
            loaded(dve, L)
            before_done(dve, L)

            def proj(i, u):
                if L in ("A", "B"):
                    dve.wait_ge(S(f"{L}_q"), i * 2 + 2)
                    for c in range(C):
                        dve.scalar_tensor_tensor(kbd[u][:, c], bc(MB[:, D + c * P:D + (c + 1) * P], 1, 8),
                                                 W[L, "bk"][:, c:c + 1], bc(hmask[:, :], 2, P), ALU.add, ALU.mult)\
                           .then_inc(S(f"{L}_kbd"), 1)
                if L == "D":
                    qk3 = qk[:, :].rearrange("p (n two) -> p n two", two=2)
                    rb3 = rb[:, :].rearrange("p (n two) -> p n two", two=2)
                    dve.wait_ge(S("D_qkps"), i + 1)
                    if not (isinstance(i, int) and i == 0):
                        dve.wait_ge(S("D_ra"), i)
                    dve.tensor_tensor(qk[:, :], MB, W[L, "bqk"][:, :], ALU.add).then_inc(S("D_qk"), 1)
                    dve.wait_ge(S("D_gps"), i + 1)
                    if not (isinstance(i, int) and i == 0):
                        dve.wait_ge(S("D_eg"), i)
                    dve.tensor_tensor(gx[:, :], ps[:, 0, 0:D], W[L, "bg"][:, :], ALU.add).then_inc(S("D_gx"), 1)
                    dve.wait_ge(S("D_qk"), i + 1)
                    dve.tensor_tensor(rb3[:, :, 0], qk3[:, :, 1], W[L, "sin_lo"][:, :], ALU.mult).then_inc(S("D_rb"), 1)
                    dve.tensor_tensor(rb3[:, :, 1], qk3[:, :, 0], W[L, "sin_hi"][:, :], ALU.mult).then_inc(S("D_rb"), 1)
                    dve.wait_ge(S("D_vps"), i + 3)
                    dve.tensor_tensor(v[u][:, :], OB, W[L, "bv"][:, :], ALU.add).then_inc(S("D_v"), 1)
                    dve.wait_ge(S("D_ra"), i + 1)
                    dve.wait_ge(S("D_rb"), i * 2 + 2)
                    dve.tensor_tensor(rr[:, :], ra[:, :], rb[:, :], ALU.add).then_inc(S("D_rr"), 1)
                    dve.wait_ge(S("D_re"), i + 1)
                    dve.scalar_tensor_tensor(f[u][:, :], rr[:, :], 0.0, re[:, :], ALU.max, ALU.add)\
                       .then_inc(S("D_f"), 1)
                    return
                if L == "E":
                    dve.wait_ge(S("E_qps"), i + 1)
                    dve.tensor_tensor(qm[u][0:64, 0:4].rearrange("p g j q -> p g (j q)"), bc(MB[0:64, :], 1, 4),
                                      bc(gmask[:, 0:4], 2, G1 * P), ALU.mult).then_inc(S("E_qm"), 1)
                    dve.wait_ge(S("E_qm_act"), i + 1)
                    dve.tensor_copy(nt[0:1, 1:2], gmask[0:1, 0:1]).then_inc(S("E_qm"), 1)
                dve.wait_ge(S(f"{L}_vps"), i + 3)
                ones = W[L, "bv"] if L == "A" else W[L, "ones_v"]
                dve.tensor_tensor(v[u][:, :], OB, ones[:, :], ALU.add).then_inc(S(f"{L}_v"), 1)

            def unit(b, n):
                g = b * U + n
                hn = 4 if L == "E" else 8
                s3 = SLOT[n % 2].rearrange("p a (h k) -> p (a h) k", k=1024 // hn)
                dve.wait_ge(S("sps"), nu(L, g + 1))
                dve.reduce_max(mx[n % 2][:, 0:hn], s3, AX.X).then_inc(S("mx"), 1)
                dve.wait_ge(S("mx"), nu(L, g + 1))
                dve.wait_ge(S("trb"), nu(L, g + 1))
                dve.tensor_tensor(e[n % 2][:, :].rearrange("p (h k) -> p h k", h=hn), s3,
                                  bc(mx[n % 2][:, 0:hn], 2, 1024 // hn), ALU.subtract).then_inc(S("sub"), 1)

            def core(b, u):
                if L == "D":
                    dve.wait_ge(S("D_gmps"), b + 1)
                    for n in range(2):
                        dve.tensor_tensor(gm[:, n, :], ps[:, 2 + n, :], W[L, "blocks"][:, :], ALU.mult)\
                           .then_inc(S("D_gm"), 1)
                    dve.wait_ge(S("D_num"), b + 1)
                    num = ps[:, 4, :].rearrange("p (h w) -> p h w", w=VW)
                    dve.tensor_scalar(den[:, :], num[:, :, DH0], 1e-6, None, ALU.add).then_inc(S("D_den"), 1)
                    dve.wait_ge(S("D_den"), b + 1)
                    dve.wait_ge(S("D_eg"), b + 1)
                    dve.scalar_tensor_tensor(d2[:, :].rearrange("p (h w) -> p h w", w=DH0),
                                             eg[u][:, :].rearrange("p (h w) -> p h w", w=DH0), 1.0,
                                             bc(den[:, :], 2, DH0), ALU.add, ALU.mult).then_inc(S("D_d2"), 1)
                    dve.wait_ge(S("D_d2"), b + 1)
                    dve.reciprocal(r2[:, :], d2[:, :]).then_inc(S("D_r2"), 1)
                    dve.wait_ge(S("D_r2"), b + 1)
                    dve.tensor_tensor(an[:, :].rearrange("p (h w) -> p h w", w=DH0), num[:, :, 0:DH0],
                                      r2[:, :].rearrange("p (h w) -> p h w", w=DH0), ALU.mult).then_inc(S("D_an"), 1)
                    return
                for n in range(U):
                    unit(b, n)

            def fin(b, u):
                if L in ("A", "B"):
                    dve.wait_ge(S(f"{L}_otr"), b + 1)
                    o = MB.rearrange("p (h w) -> p h w", w=VW)
                    dve.reciprocal(rden[:, 0, :], o[:, :, DH0]).then_inc(S(f"{L}_rden"), 1)
                    dve.wait_ge(S(f"{L}_rden"), b + 1)
                    dve.tensor_tensor(an[:, :].rearrange("p (h w) -> p h w", w=DH0), o[:, :, 0:DH0],
                                      bc(rden[:, 0, :], 2, DH0), ALU.mult).then_inc(S(f"{L}_an"), 1)
                if L == "E":
                    for r in range(2):
                        dve.wait_ge(S("E_otr"), b * 2 + r + 1)
                        o = MB.rearrange("p (j g w) -> p j g w", j=G1, w=VW)
                        dve.reciprocal(rden[:, r, :].rearrange("p (j g) -> p j g", j=G1), o[:, :, :, DH1])\
                           .then_inc(S("E_rden"), 1)
                        dve.wait_ge(S("E_rden"), b * 2 + r + 1)
                        a4 = an[:, r * P:(r + 1) * P].rearrange("p (g j w) -> p j g w", g=4, w=DH1)
                        dve.tensor_tensor(a4, o[:, :, :, 0:DH1],
                                          bc(rden[:, r, :].rearrange("p (j g) -> p j g", j=G1), 3, DH1), ALU.mult)\
                           .then_inc(S("E_an"), 1)
                dve.wait_ge(S("y"), nb(L, b + 1))
                dve.wait_ge(S(f"{L}_xb"), b + 1)
                if L == "B":
                    dve.wait_ge(S("B_an"), b + 1)
                    dve.tensor_tensor(z1[:, :], MB[:, D:2 * D], an[:, :], ALU.add).then_inc(S("B_z1"), 1)
                    dve.wait_ge(S("B_z1"), b + 1)
                    dve.tensor_tensor(z[:, :], z1[:, :], xb[:, :], ALU.add).then_inc(S("z"), 1)
                else:
                    dve.tensor_tensor(z[:, :], MB[:, D:2 * D], xb[:, :], ALU.add).then_inc(S("z"), 1)
                dve_norm(dve, b, u, L)

            batches(dve, proj, core, fin)

        def dve_norm(dve, b, u, L):
            st = S("stat")

            def step(ins, k):
                ins.then_inc(st, 1)
                dve.wait_ge(st, nb(L, b) * 6 + k + 1)
                settle(dve)

            dve.wait_ge(S("z"), nb(L, b + 2))
            step(dve.bn_stats(stats[:, :], z[:, :]), 0)
            step(dve.bn_aggr(agg[:, :], stats[:, :]), 1)
            dve.tensor_scalar(ve[:, :], agg[:, 1:2], EPS, None, ALU.add).then_inc(S("ve"), 1)
            dve.wait_ge(S("ve"), nb(L, b + 1))
            dve.wait_ge(S("y0"), nb(L, b + 1))
            step(dve.tensor_tensor(nt[:, 0:1], y0[:, :], y0[:, :], ALU.mult), 2)
            step(dve.tensor_tensor(nt[:, 1:2], nt[:, 0:1], ve[:, :], ALU.mult), 3)
            step(dve.tensor_scalar(nt[:, 0:1], nt[:, 1:2], -0.5, 1.5, ALU.mult, ALU.add), 4)
            step(dve.tensor_tensor(rstd[:, :], nt[:, 0:1], y0[:, :], ALU.mult), 5)
            dve.wait_ge(S("xrow"), nb(L, b + 1))
            if L == "F" and not (isinstance(b, int) and b < 2):
                dve.wait_ge(S(f"stored{u}"), b * 8 - 8 * u)
            dve.tensor_scalar(xn[u][:, :], z[:, :], agg[:, 0:1], rstd[:, :], ALU.subtract, ALU.mult)\
               .then_inc(S("xn"), 1)
            if L not in NEXT_IS_MOE:
                return
            dve.wait_ge(S(f"{L}_xh"), b + 1)
            dve.tensor_tensor(XL[:, :, tok(b)], MB[:, 0:D].rearrange("p (c q) -> p c q", c=C),
                              XH[:, :, tok(b)].bitcast(F32), ALU.subtract).then_inc(S(f"{L}_xl"), 1)
            nl, k = (E0, TOP0) if L == "B" else (E1, TOP1)
            rt = S(f"{L}_route")

            def route(ins, i):
                ins.then_inc(rt, 1)
                dve.wait_ge(rt, b * 7 + i + 1)
                settle(dve)

            dve.wait_ge(S(f"{L}_lgps"), b + 1)
            if L == "B":
                route(dve.tensor_copy(lg[:, 0:nl], MB[:, D:D + nl]), 0)
                route(dve.max(top[:, :], lg[:, 0:nl]), 1)
            else:
                dve.tensor_copy(lg[:, 32:33], MB[:, D + E1:D + E1 + 1]).then_inc(S("E_lgs"), 1)
                route(dve.tensor_copy(lg[:, 0:nl], MB[:, D:D + nl]), 0)
                route(dve.max(top[:, :], lg[:, 0:nl]), 1)
                dve.memset(top[:, k:8], SENT).then_inc(S("E_top"), 1)
                dve.wait_ge(S("E_top"), b + 1)
                dve.wait_ge(S("E_lgs"), b + 1)
            dve.tensor_scalar(nmax[:, :], top[:, 0:1], -1.0, None, ALU.mult).then_inc(S(f"{L}_nmax"), 1)
            wide = nl if L == "B" else 16
            route(dve.match_replace(lrep[:, 0:wide], top[:, :], lg[:, 0:wide], -SENT), 2)
            route(dve.tensor_tensor(msk[:, 0:nl], lrep[:, 0:nl], lg[:, 0:nl], ALU.not_equal), 3)
            dve.wait_ge(S(f"{L}_ex"), b + 1)
            route(dve.tensor_tensor(em[:, 0:nl], ex[:, 0:nl], msk[:, 0:nl], ALU.mult), 4)
            route(dve.reduce_sum(esum[:, :], em[:, 0:nl], AX.X), 5)
            route(dve.reciprocal(einv[:, :], esum[:, :]), 6)
            if L == "E":
                dve.wait_ge(S("E_sg"), b + 1)
                dve.tensor_scalar(sg[:, 1:2], sg[:, 0:1], 1.0, None, ALU.add).then_inc(S("E_sg1"), 1)
                dve.wait_ge(S("E_sg1"), b + 1)
                dve.reciprocal(cm[:, E1:E1 + 1], sg[:, 1:2]).then_inc(S("E_cmsh"), 1)
                dve.wait_ge(S("E_cmsh"), b + 1)
            dve.tensor_scalar(cm[:, 0:nl], em[:, 0:nl], einv[:, :], None, ALU.mult).then_inc(S(f"{L}_cm"), 1)

        def dve_moe(dve, L):
            n_e, I = (E0, I0) if L == "C" else (PARTS1, IH1)
            before_done(dve, L)

            def step(x, k, t):
                g = x * 2 + t
                dve.wait_ge(S(f"{L}_silu"), g + 1)
                dve.wait_ge(S(f"{L}_gu"), g * 2 + 2)
                dve.tensor_tensor(a1[t][0:I, :], sgt[t][0:I, :], GU[t][1][0:I, :], ALU.mult).then_inc(S(f"{L}_a1"), 1)
                dve.wait_ge(S(f"{L}_a1"), g + 1)
                if t == 0:
                    dve.wait_ge(S(f"{L}_w{k}"), (x - k) // NW * 48 + 48 if isinstance(x, int) else turn[0] * 48 + 48)
                dve.tensor_tensor(a2[t][0:I, :], a1[t][0:I, :], wbc[k][0:I, t * HALF:(t + 1) * HALF], ALU.mult)\
                   .then_inc(S(f"{L}_a2"), 1)
                dve.wait_ge(S(f"{L}_ah"), g + 1)
                dve.tensor_tensor(al[t][0:I, :], a2[t][0:I, :], ah[t][0:I, :].bitcast(F32), ALU.subtract)\
                   .then_inc(S(f"{L}_al"), 1)

            turn = [None]
            with dve.Fori(0, n_e // NW) as j:
                turn[0] = j
                for k in range(NW):
                    for t in range(2):
                        step(j * NW + k, k, t)

            def fin(b, u):
                dve.wait_ge(S("y"), nb(L, b + 1))
                dve.wait_ge(S("xn"), nb(L, b))
                dve.tensor_tensor(z[:, :], MB[:, D:2 * D], X[:, bass.ds(b, 1), :].rearrange("p b d -> p (b d)"),
                                  ALU.add).then_inc(S("z"), 1)
                dve_norm(dve, b, u, L)

            fin(0, 0)
            fin(1, 1)
            with dve.Fori(1, B // 2) as j:
                fin(j * 2, 0)
                fin(j * 2 + 1, 1)

        @block.vector
        def _(dve):
            dve.memset(zero16[:, :], 0.0).then_inc(S("zero16"), 1)
            for u in range(2):
                dve.memset(lg[:, :], SENT).then_inc(S("lg_set"), 1)
                dve.wait_ge(S("lg_set"), u + 1)
            dve.memset(cm[:, :], 0.0).then_inc(S("cm_set"), 1)
            dve.wait_ge(S("cm_set"), 1)
            for L in ATTN:
                dve_attention(dve, L)
                if L in NEXT_IS_MOE:
                    dve_moe(dve, "C" if L == "B" else "F")

        def pool_attention(pool, L):
            loaded(pool, L)
            before_done(pool, L)
            def proj(i, u):
                pool.wait_ge(S(f"{L}_vps"), i + 1)
                settle(pool)
                if L in ("B", "E"):
                    pool.tensor_copy(cs[u][:, :, :], CTXT[:, :, tok(i)])
                pool.tensor_copy(xs[u][:, :, :], XT[:, :, tok(i)]).then_inc(S(f"{L}_xs"), 1)
                if L == "D":
                    pool.wait_ge(S("D_qk"), i + 1)
                    settle(pool)
                    pool.tensor_tensor(ra[:, :], qk[:, :], W[L, "cos"][:, :], ALU.mult).then_inc(S("D_ra"), 1)
                    pool.wait_ge(S("D_rr"), i + 1)
                    settle(pool)
                    pool.tensor_scalar(rn[:, :], rr[:, :], 0.0, None, ALU.min).then_inc(S("D_rn"), 1)

            def core(b, u):
                pass

            def fin(b, u):
                pool.wait_ge(S("z"), nb(L, b + 1))
                settle(pool)
                row = X[:, bass.ds(b, 1), :].rearrange("p b d -> p (b d)")
                bias = {"A": "bo", "B": "bv", "D": "bo"}.get(L)
                if bias:
                    pool.tensor_tensor(xb[:, :], row, W[L, bias][:, :], ALU.add).then_inc(S(f"{L}_xb"), 1)
                else:
                    pool.tensor_copy(xb[:, :], row).then_inc(S(f"{L}_xb"), 1)
                keep(pool, b, u, L)

            batches(pool, proj, core, fin)

        def keep(pool, b, u, L):
            pool.wait_ge(S("xn"), nb(L, b + 1))
            settle(pool)
            pool.tensor_copy(X[:, bass.ds(b, 1), :].rearrange("p b d -> p (b d)"), xn[u][:, :])\
                .then_inc(S("xrow"), 1)

        def pool_moe(pool, L):
            n_e, I = (E0, I0) if L == "C" else (PARTS1, IH1)
            before_done(pool, L)
            used = 4 * I + D

            def split(x, u, k, turn):
                pool.wait_ge(S(f"{L}_w{k}"), turn * 48 + 48)
                settle(pool)
                for n, (lo, hi, rows) in enumerate(((0, 4 * I, P), (4 * I, used, I))):
                    if not (isinstance(x, int) and x < 2):
                        pool.wait_ge(S(f"{L}_down") if n else S(f"{L}_gu"), x * 2 - 2 if n else x * 4 - 4)
                        settle(pool)
                    pool.tensor_copy(wh[u][0:rows, lo:hi], wraw[k][0:rows, lo:hi]).then_inc(S(f"{L}_wh"), 1)
                    pool.wait_ge(S(f"{L}_wh"), x * 2 + n + 1)
                    pool.tensor_tensor(wl[u][0:rows, lo:hi], wraw[k][0:rows, lo:hi],
                                       wh[u][0:rows, lo:hi].bitcast(F32), ALU.subtract)\
                        .then_inc(S(f"{L}_wl"), 1)

            for x in range(NW):
                split(x, x % 2, x, 0)
            with pool.Fori(1, n_e // NW) as j:
                for k in range(NW):
                    split(j * NW + k, k % 2, k, j)

            def fin(b, u):
                keep(pool, b, u, L)

            fin(0, 0)
            fin(1, 1)
            with pool.Fori(1, B // 2) as j:
                fin(j * 2, 0)
                fin(j * 2 + 1, 1)

        @block.gpsimd
        def _(pool):
            for L in ATTN:
                pool_attention(pool, L)
                if L in NEXT_IS_MOE:
                    pool_moe(pool, "C" if L == "B" else "F")



def constants():
    def bf16(x):
        return (np.ascontiguousarray(x, np.float32).view(np.uint32) >> 16).astype(np.uint16)

    big = np.float32(-1e30)
    q, k = np.arange(P)[:, None], np.arange(P)[None, :]
    c = {}
    c["head_mask"] = (np.arange(P)[:, None] // DH0 == np.arange(8)[None, :]).astype(np.float32)
    c["causal_bf16"] = bf16(np.tile(np.where(k > q, big, np.float32(0)), (1, 4)))
    delta = q - k
    win = [np.where((delta >= 0) & (delta < w), np.float32(0), big) for w in (64, 32)]
    c["window_bf16"] = bf16(np.concatenate(win, 1))
    c["ident"] = np.eye(P, dtype=np.float32)
    c["ident_bf16"] = bf16(np.eye(P))

    def ones_col(heads, at):
        row = np.zeros((heads, VW), np.float32)
        row[:, at] = 1
        return np.broadcast_to(row.reshape(-1), (P, heads * VW)).copy()

    c["B_ones_v"] = ones_col(H0, DH0)
    c["E_ones_v"] = ones_col(2 * KV1, DH1)
    inv = np.float32(1.0) / np.float32(10000.0) ** (np.arange(0, DH0, 2, dtype=np.float32) / np.float32(DH0))
    ang = np.arange(P, dtype=np.float32)[:, None] * inv[None, :].astype(np.float32)
    cos, sin = np.cos(ang).astype(np.float32), np.sin(ang).astype(np.float32)
    c["D_cos"] = np.tile(np.repeat(cos, 2, 1), (1, 2 * H0))
    c["D_sin_lo"] = np.tile(-sin, (1, 2 * H0))
    c["D_sin_hi"] = np.tile(sin, (1, 2 * H0))
    rows = np.arange(P)[:, None] // DH0
    cols = (np.arange(2 * D)[None, :] % D) // VW
    c["D_blocks"] = (rows == cols).astype(np.float32)
    c["group_mask"] = (np.arange(64)[:, None] // DH1 == np.arange(KV1)[None, :]).astype(np.float32)
    heads = KV1 * G1
    slope = 2.0 ** (-8.0 * np.arange(heads) / heads) * np.sqrt(float(DH1))
    pos = np.arange(P) - 64.0
    qrow = np.zeros((64, heads, P))
    qrow[0] = -slope[:, None] * pos[None, :]
    qrow[1] = slope[:, None]
    c["E_qrow"] = qrow.reshape(64, heads * P).astype(np.float32)
    krow = np.zeros((64, 2, P))
    krow[0] = 1
    krow[1] = pos
    c["E_krow"] = krow.reshape(64, 2 * P).astype(np.float32)
    return c


def kernel(**inputs):
    import concourse.bacc as bacc
    from concourse.bass_utils import run_bass_kernel_spmd

    n = {k: np.asarray(v) for k, v in inputs.items()}

    def chunks(w):
        return w.reshape(-1, P, w.shape[1]).transpose(1, 0, 2)

    def T_layout(x):
        return chunks(x.reshape(T, D).T)

    def cols(b):
        return b.reshape(-1, P).T

    def spread(b):
        return np.broadcast_to(b, (P, b.shape[-1]))

    def heads_wide(w, h):
        r = np.zeros((w.shape[0], h, VW), w.dtype)
        r[:, :, :w.shape[1] // h] = w.reshape(w.shape[0], h, -1)
        return r.reshape(w.shape[0], h * VW)

    def values_bias(b, h):
        r = heads_wide(b[None], h).reshape(h, VW)
        r[:, b.shape[0] // h] = 1
        return spread(r.reshape(-1))

    d = constants()
    d["x_t"], d["ctx_t"] = T_layout(n["x"]), T_layout(n["ctx_2048"])
    d["x_rows"] = n["x"].transpose(1, 0, 2)
    w, b = n["L0_attn_W_in"].T, n["L0_attn_b_in"]
    d["A_wq"], d["A_wk"], d["A_wv"] = chunks(w[:, :D]), chunks(w[:, D:2 * D]), chunks(heads_wide(w[:, 2 * D:], H0))
    d["A_bq"], d["A_bk"], d["A_bv"] = cols(b[:D]), cols(b[D:2 * D]), values_bias(b[2 * D:], H0)
    d["A_wo"], d["A_bo"] = chunks(n["L0_attn_W_out"].T), spread(n["L0_attn_b_out"])
    p = "L0_xattn_"
    d["B_wfc"], d["B_bfc"] = chunks(n[p + "W_fc"].T), cols(n[p + "b_fc"])
    d["B_wq"], d["B_bq"] = chunks(n[p + "W_q"].T), cols(n[p + "b_q"])
    d["B_wk"], d["B_bk"] = chunks(n[p + "W_k"].T), cols(n[p + "b_k"])
    d["B_wv"] = chunks(heads_wide(n[p + "W_v"].reshape(D, D).T, H0))
    d["B_bv"] = spread(n[p + "b_v"])
    d["B_wr"] = chunks(n["L0_ffn_gate_weight"].T)
    d["C_gu"], d["C_down"] = n["L0_ffn_gate_up_weights"], n["L0_ffn_down_weights"]
    p = "L1_attn_"
    d["D_wqk"] = chunks(np.concatenate([n[p + "Wq"].T, n[p + "Wk"].T], 1))
    d["D_bqk"] = spread(np.concatenate([n[p + "bq"], n[p + "bk"]]))
    d["D_wv"], d["D_bv"] = chunks(heads_wide(n[p + "Wv"].T, H0)), values_bias(n[p + "bv"], H0)
    d["D_wg"], d["D_bg"] = chunks(n[p + "Wg"].T), spread(n[p + "bg"])
    d["D_wo"], d["D_bo"] = chunks(n[p + "Wo"].T), spread(n[p + "bo"])
    p = "L1_xattn_"
    d["E_wq"] = chunks(n[p + "Wq"].reshape(2 * D, KV1, G1, DH1).transpose(0, 2, 1, 3).reshape(2 * D, D))
    d["E_wk"], d["E_wsk"] = chunks(n[p + "Wk"]), chunks(n[p + "Wsk"])
    d["E_wv"], d["E_wsv"] = chunks(heads_wide(n[p + "Wv"], KV1)), chunks(heads_wide(n[p + "Wsv"], KV1))
    d["E_wo"] = chunks(n[p + "Wo"])
    p = "L1_ffn_"
    wr = np.zeros((D, 16), np.float32)
    wr[:, :E1], wr[:, E1] = n[p + "router_weight"].T, n[p + "shared_gate_w"][0]
    d["E_wr"] = chunks(wr)
    k = I1 // IH1
    gu = n[p + "gate_up_proj"].reshape(E1, 2, k, IH1, D).transpose(0, 2, 4, 1, 3).reshape(E1 * k, D, 2 * IH1)
    sh = np.stack([n[p + "sh_gate_w"], n[p + "sh_up_w"]]).reshape(2, ISH // IH1, IH1, D)
    sh = sh.transpose(1, 3, 0, 2).reshape(ISH // IH1, D, 2 * IH1)
    d["F_gu"] = np.concatenate([gu, sh])
    dn = n[p + "down_proj"].reshape(E1, D, k, IH1).transpose(0, 2, 3, 1).reshape(E1 * k, IH1, D)
    d["F_down"] = np.concatenate([dn, n[p + "sh_down_w"].T.reshape(ISH // IH1, IH1, D)])

    nc = bacc.Bacc("TRN2", target_bir_lowering=False, num_devices=1)
    arrays, args = {}, {}
    for name, x in d.items():
        arrays[f"in_{name}"] = np.ascontiguousarray(x)
        args[name] = nc.dram_tensor(f"in_{name}", x.shape, mybir.dt.from_np(x.dtype), kind="ExternalInput").ap()
    out = nc.dram_tensor("out", (B, P, D), F32, kind="ExternalOutput").ap()
    build(nc, args, out)
    r = run_bass_kernel_spmd(nc, [arrays], core_ids=[0])
    return r.results[0]["out"]
```

```python
from contextlib import ExitStack

import numpy as np

import concourse.bass as bass
from concourse import mybir

F32 = mybir.dt.float32
F32R = mybir.dt.float32r
BF16 = mybir.dt.bfloat16
ALU = mybir.AluOpType
ACT = mybir.ActivationFunctionType
AX = mybir.AxisListType

P = 128
B = 8
T = B * P
D = 256
C = D // P
VW = 32
DH0, H0 = 16, 16
DH1, KV1, G1 = 8, 8, 4
HALF = 512
EPS = 1e-5
E0, I0, TOP0 = 64, 96, 8
E1, I1, TOP1 = 8, 176, 2
ISH = 704
UNITS_OF = {"C": E0 * I0, "F": E1 * I1 + ISH}
BLOCKS = {L: -(-n // P) for L, n in UNITS_OF.items()}
RUN = {"C": 32, "F": 16}
SENT = -3.0e38


def build(nc, a, out):
    ctx = ExitStack()
    with ctx:
        def sb(name, shape, dt=F32):
            return ctx.enter_context(nc.sbuf_tensor(name, shape, dt))

        sems = {}

        def S(name):
            if name not in sems:
                sems[name] = ctx.enter_context(nc.semaphore(name))
            return sems[name]

        loads = {}

        def const(layer, name, dt=F32):
            src = a[name]
            t = sb("c_" + name, list(src.shape), dt)
            loads.setdefault(layer, []).append((t[:, :].bitcast(src.dtype) if dt == BF16 else t, src))
            return t

        arena = sb("arena", [P, 9856])
        filled = {"AB": 0, "DE": 0}

        def weight(layer, name):
            src = a[f"{layer}_{name}"]
            both = "AB" if layer in "AB" else "DE"
            n = int(np.prod(src.shape[1:]))
            t = arena[:, filled[both]:filled[both] + n]
            filled[both] += n
            assert filled[both] <= arena.shape[1]
            if len(src.shape) == 3:
                t = t.rearrange("p (c n) -> p c n", c=src.shape[1])
            loads.setdefault(layer, []).append((t, src))
            W[layer, name] = t

        W = {}

        XT = const("A", "x_t")
        X = const("A", "x_rows")
        hmask = const("A", "head_mask")
        causal = const("A", "causal_bf16", BF16)
        ident16 = const("A", "ident_bf16", BF16)
        ident = const("A", "ident")
        CTXT = const("B", "ctx_t")
        for layer, names in (("A", "wq wk wv bq bk bv wo bo"),
                             ("B", "wfc bfc wq wk wv bq bk bv ones_v wr"),
                             ("D", "wqk wv wg bqk bv bg wo bo cos sin_lo sin_hi blocks"),
                             ("E", "wq wk wsk wv wsv wo ones_v wr")):
            for n in names.split():
                weight(layer, n)
        gmask = const("E", "group_mask")
        window = const("E", "window_bf16", BF16)

        xs = [sb(f"xs{u}", [P, C, P]) for u in range(2)]
        cs = [sb(f"cs{u}", [P, C, P]) for u in range(2)]
        refT = [sb(f"refT{u}", [P, C, P]) for u in range(2)]
        supT = [sb(f"supT{u}", [P, C, P]) for u in range(2)]
        qT = [sb(f"qT{u}", [P, C, P]) for u in range(2)]
        kbd = [sb(f"kbd{u}", [P, C, 8, P]) for u in range(2)]
        qm = [sb(f"qm{u}", [P, KV1, G1, P]) for u in range(2)]
        kT = [sb(f"kT{u}", [P, 2, P]) for u in range(2)]
        v = [sb(f"v{u}", [P, 2 * D]) for u in range(2)]
        e = [sb(f"e{u}", [P, 1024]) for u in range(2)]
        pT = [sb(f"pT{u}", [P, 1024]) for u in range(2)]
        mx = [sb(f"mx{u}", [P, 8]) for u in range(2)]
        oT = sb("oT", [P, 2, HALF])
        rden = sb("rden", [P, 2, 16])
        an = sb("an", [P, D])
        aT = sb("aT", [P, C, P])
        xb = sb("xb", [P, D])
        z1 = sb("zsum", [P, D])
        z = [sb(f"z{u}", [P, D]) for u in range(2)]
        stats = sb("stats", [P, 6])
        agg = [sb(f"agg{u}", [P, 2]) for u in range(2)]
        ve = sb("ve", [P, 1])
        y0 = sb("y0", [P, 1])
        nt = sb("nt", [P, 3])
        rstd = [sb(f"rstd{u}", [P, 1]) for u in range(2)]
        minus_half = sb("minus_half", [P, 1])
        xn = [sb(f"xn{u}", [P, D]) for u in range(2)]
        qk = e[0][:, 0:512]
        ra = e[0][:, 512:1024]
        rb = e[1][:, 0:512]
        rr = e[1][:, 512:1024]
        rn = pT[0][:, 0:512]
        re = pT[0][:, 512:1024]
        f = [sb(f"f{u}", [P, 2 * D]) for u in range(2)]
        gx = refT[0][:, :, :].rearrange("p c q -> p (c q)")
        eg = [supT[u][:, :, :].rearrange("p c q -> p (c q)") for u in range(2)]
        qfT = cs[0]
        qs = refT[0][:, :, :].rearrange("p c q -> p (c q)")
        qs2 = refT[1][:, :, :].rearrange("p c q -> p (c q)")
        gm = oT
        den = sb("den", [P, 16])
        d2 = sb("d2", [P, D])
        r2 = sb("r2", [P, D])
        lg = qT[0][:, :, :].rearrange("p c q -> p (c q)")
        lg64 = pT[0][:, 0:B * E0]
        lrep = pT[0][:, 512:1024]
        msk = pT[1][:, 0:512]
        ex = pT[1][:, 512:1024]
        em = e[0][:, 0:512]
        cm = e[0][:, 512:1024]
        top = sb("top", [P, B, 8])
        esum = sb("esum", [P, B])
        einv = sb("einv", [P, B])
        sg = sb("sg", [P, B])
        sg1 = sb("sg1", [P, B])
        cT = sb("cT", [64, T])
        XH = sb("XH", [P, C, T], F32R)
        XL = sb("XL", [P, C, T], F32R)
        WCOLS = C * 2 * P + D
        NW = 4
        qm_flat = [m[:, :, :, :].rearrange("p g j q -> p (g j q)") for m in qm]
        wraw = [qm_flat[k // 2][:, (k % 2) * WCOLS:(k % 2 + 1) * WCOLS] for k in range(NW)]
        wh = [sb(f"wh{u}", [P, WCOLS], F32R) for u in range(2)]
        wl = [sb(f"wl{u}", [P, WCOLS], F32R) for u in range(2)]
        wbc = [kbd[k // 2][:, k % 2].rearrange("p h k -> p (h k)") for k in range(NW)]
        sgt = [e[u][:, 0:HALF] for u in range(2)]
        a1 = [e[u][:, HALF:2 * HALF] for u in range(2)]
        a2 = [pT[u][:, 0:HALF] for u in range(2)]
        ah = [sb(f"ah{u}", [P, HALF], F32R) for u in range(2)]
        al = [sb(f"al{u}", [P, HALF], F32R) for u in range(2)]
        zero16 = sb("zero16", [P, HALF], BF16)
        yT = xs

        combine = {L: nc.dram_tensor(f"combine_{L}", [BLOCKS[L] * P // RUN[L], T], F32).ap() for L in "CF"}
        shared_row = nc.dram_tensor("shared_row", [1, T], F32).ap()

        ps = ctx.enter_context(nc.psum_tensor("ps", [P, 8, HALF], F32))
        SLOT = [ps[:, 2 * s:2 * s + 2, :] for s in range(2)]
        PT = [ps[:, 4 + s, :] for s in range(2)]
        OB = ps[:, 6, :]
        MB = ps[:, 7, :]
        Y = ps[:, 0:4, :]
        GU = [[ps[:, 4 + 2 * t + s, :] for s in range(2)] for t in range(2)]

        def tok(b):
            return bass.ds(b * P, P)

        def bc(ap, axis, n):
            x = ap.unsqueeze(axis)
            shape = list(x.shape)
            shape[axis] = n
            return x.to_broadcast(shape)

        ATTN = ("A", "B", "D", "E")
        UNITS = {"A": 2, "B": 2, "E": 8, "D": 0}
        ORDER = "ABCDEF"

        def nb(L, n):
            return ORDER.index(L) * B + n

        def nu(L, n):
            return sum(UNITS[M] * B for M in ORDER[:ORDER.index(L)] if M in UNITS) + n

        BEFORE = {"B": "A", "C": "B", "D": "C", "E": "D", "F": "E"}
        NEXT_IS_MOE = ("B", "E")
        OTN = {"A": 1, "B": 1, "E": 2}

        def loaded(eng, layer):
            eng.wait_ge(S(f"{layer}_loaded"), 16 * len(loads[layer]))

        def settle(eng):
            eng.sem_inc(S("settled"), 1)

        def before_done(eng, L):
            if L in BEFORE:
                p = BEFORE[L]
                eng.wait_ge(S("xt"), nb(L, 1))
                eng.wait_ge(S("xrow"), nb(L, 2))
                if p in NEXT_IS_MOE:
                    eng.wait_ge(S(f"{p}_xl"), 1)
                    eng.wait_ge(S(f"{p}_cT"), 2 if p == "B" else 1)

        def turns(eng, turn):
            turn(0, 0, True, False, False)
            turn(1, 1, True, True, False)
            with eng.Fori(0, B // 2 - 1) as j:
                turn(j * 2 + 2, 0, True, True, True)
                turn(j * 2 + 3, 1, True, True, True)
            turn(B, 0, False, True, True)
            turn(B + 1, 1, False, False, True)

        def norm_turns(eng, turn):
            turn(0, 0, True, False)
            turn(1, 1, True, True)
            with eng.Fori(1, B // 2) as j:
                turn(j * 2, 0, True, True)
                turn(j * 2 + 1, 1, True, True)
            turn(B, 0, False, True)

        def first(i):
            return isinstance(i, int) and i == 0

        block = ctx.enter_context(nc.Block())

        def moe_loads(sp, L):
            def weights(x, k):
                sp.dma_start(wraw[k], a[f"{L}_w"][bass.ds(x, 1)].rearrange("o p n -> p (o n)"))\
                  .then_inc(S(f"{L}_w{k}"), 16)

            def token_weights(x, k):
                runs = P // RUN[L]
                src = combine[L][bass.ds(x * runs, runs)]
                sp.dma_start(wbc[k][:, :], bc(src, 1, RUN[L])).then_inc(S(f"{L}_t{k}"), 16)

            if L == "F":
                sp.wait_ge(S("sps"), nu("E", B * UNITS["E"]))
                settle(sp)
            for k in range(NW):
                weights(k, k)
            sp.wait_ge(S(f"{BEFORE[L]}_cT"), 2 if L == "C" else 1)
            settle(sp)
            n_e, runs = (E0, I0 // RUN[L]) if L == "C" else (E1, I1 // RUN[L])
            rows = combine[L][0:n_e * runs].rearrange("(e k) t -> k e t", k=runs)
            for k in range(runs):
                sp.dma_start(rows[k], cT[0:n_e, :]).then_inc(S(f"{L}_out"), 16)
            if L == "F":
                sp.dma_start(shared_row, cT[E1:E1 + 1, :]).then_inc(S("shared_out"), 16)
                sp.wait_ge(S("shared_out"), 16)
                settle(sp)
                rest = combine[L].shape[0] - n_e * runs
                sp.dma_start(combine[L][n_e * runs:], shared_row.to_broadcast([rest, T])).then_inc(S(f"{L}_out"), 16)
            sp.wait_ge(S(f"{L}_out"), 16 * (runs + (L == "F")))
            settle(sp)
            for k in range(NW):
                token_weights(k, k)
            if L == "C":
                for M in ("D", "E"):
                    for t, src in loads[M]:
                        sp.dma_start(t[tuple(slice(None) for _ in t.shape)], src).then_inc(S(f"{M}_loaded"), 16)

            def refill(j, k):
                done = (j - 1) * (2 * NW) + 2 * k + 2
                sp.wait_ge(S(f"{L}_wl"), done)
                settle(sp)
                weights(j * NW + k, k)
                sp.wait_ge(S(f"{L}_a2"), done)
                settle(sp)
                token_weights(j * NW + k, k)

            with sp.Fori(1, BLOCKS[L] // NW) as j:
                for k in range(NW):
                    refill(j, k)
            for k in range(BLOCKS[L] % NW):
                refill(BLOCKS[L] // NW, k)

        @block.sync
        def _(sp):
            sp.sem_inc(S("sub"), 2)
            sp.sem_inc(S("z"), 1)
            sp.sem_inc(S("trb"), 2)
            sp.sem_inc(S("pca"), 1)
            sp.sem_inc(S("pcb"), 1)
            sp.sem_inc(S("pv"), 2)
            sp.sem_inc(S("xt"), 1)
            sp.sem_inc(S("xrow"), 2)
            for u in range(2):
                sp.sem_inc(S(f"stored{u}"), 16)
            for L in ATTN:
                sp.sem_inc(S(f"{L}_vps"), 2)

            def load_weights(L):
                for t, src in loads[L]:
                    sp.dma_start(t[tuple(slice(None) for _ in t.shape)], src).then_inc(S(f"{L}_loaded"), 16)

            load_weights("A")
            load_weights("B")
            moe_loads(sp, "C")
            sp.wait_ge(S("C_wl"), 2 * BLOCKS["C"])
            settle(sp)
            for u in range(2):
                sp.dma_start(qm[u][64:128].rearrange("p g j q -> p (g j q)"), a["E_qrow"]).then_inc(S("qrow"), 16)
                sp.dma_start(kT[u][64:128].rearrange("p s k -> p (s k)"), a["E_krow"]).then_inc(S("krow"), 16)
            moe_loads(sp, "F")
            with sp.Fori(0, B // 2) as j:
                for u in range(2):
                    sp.wait_ge(S("xrow"), nb("F", j * 2 + u + 3))
                    settle(sp)
                    sp.dma_start(out[bass.ds(j * 2 + u, 1)].rearrange("b p d -> p (b d)"),
                                 xn[u][:, :]).then_inc(S(f"stored{u}"), 16)
            for u in range(2):
                sp.wait_ge(S(f"stored{u}"), 16 + 16 * B // 2)
            settle(sp)

        def pe_T(pe, dst, w, src):
            for c in range(C):
                for k in range(C):
                    mm = pe.matmul(dst[:, c * P:(c + 1) * P], w[:, k, c * P:(c + 1) * P], src[:, k, :],
                                   start=(k == 0), stop=(k == C - 1))
            return mm

        def pe_rows(pe, dst, w, src):
            for k in range(C):
                mm = pe.matmul(dst, src[:, k, :], w[:, k, :], start=(k == 0), stop=(k == C - 1))
            return mm

        def pe_attention(pe, L):
            U = UNITS[L]
            loaded(pe, L)
            before_done(pe, L)
            if L == "E":
                pe.wait_ge(S("qrow"), 32)
                pe.wait_ge(S("krow"), 32)

            def slot(s, n):
                return SLOT[(1 - s + n) % 2] if L != "E" else SLOT[(0, 1, 0, 1, 0, 1, 1, 0)[n]]

            def project(i, s):
                pe.wait_ge(S(f"{L}_xs"), i + 1)
                if not first(i):
                    pe.wait_ge(S("sub"), nu(L, i * 2 + 1 if L != "E" else i * 8 - 1))
                sl = SLOT[(s + 1) % 2] if L != "E" else SLOT[0]
                if L == "A":
                    pe_T(pe, sl[:, 0, 0:D], W[L, "wq"], xs[s])
                    pe_T(pe, sl[:, 0, D:2 * D], W[L, "wk"], xs[s]).then_inc(S("A_qkps"), 1)
                    pe_rows(pe, sl[:, 1, :], W[L, "wv"], xs[s]).then_inc(S("A_vps"), 1)
                if L == "B":
                    pe_T(pe, sl[:, 0, 0:D], W[L, "wfc"], xs[s])
                    pe_T(pe, sl[:, 0, D:2 * D], W[L, "wfc"], cs[s]).then_inc(S("B_fcps"), 1)
                if L == "E":
                    for j in range(G1):
                        for k in range(2 * C):
                            mm = pe.matmul(sl[0:64, 0, j * P:(j + 1) * P], W[L, "wq"][:, k, j * 64:(j + 1) * 64],
                                           (cs if k < C else xs)[s][:, k % C, :], start=(k == 0), stop=(k == 2 * C - 1))
                    mm.then_inc(S("E_qps"), 1)
                    for n, (wn, src) in enumerate((("wsk", cs), ("wk", xs))):
                        for k in range(C):
                            mm = pe.matmul(sl[0:64, 1, n * P:(n + 1) * P], W[L, wn][:, k, :], src[s][:, k, :],
                                           start=(k == 0), stop=(k == C - 1))
                    mm.then_inc(S("E_kps"), 1)

            def project2(i, s):
                if L == "B":
                    sl = SLOT[(s + 1) % 2]
                    pe.wait_ge(S("B_fc"), i * 4 + 4)
                    pe_T(pe, sl[:, 1, 0:D], W[L, "wq"], refT[s])
                    pe_T(pe, sl[:, 1, D:2 * D], W[L, "wk"], supT[s]).then_inc(S("B_qkps"), 1)
                    pe_rows(pe, sl[:, 0, :], W[L, "wv"], supT[s]).then_inc(S("B_vps"), 1)
                if L == "E":
                    if not first(i):
                        pe.wait_ge(S("sub"), nu(L, i * 8 + 1))
                    for n, (wn, src) in enumerate((("wsv", cs), ("wv", xs))):
                        mm = pe_rows(pe, SLOT[1][:, 0, n * D:(n + 1) * D], W[L, wn], src[s])
                    mm.then_inc(S("E_vps"), 1)

            def scores(b, s, n, also_p):
                g = b * U + n
                u = 1 - s
                sl = slot(s, n)
                if n == 0:
                    if L == "E":
                        pe.wait_ge(S("E_kT"), b + 1)
                        pe.wait_ge(S("E_qm"), b + 1)
                        pe.wait_ge(S("E_qmp"), b + 1)
                    else:
                        pe.wait_ge(S(f"{L}_q"), b * 2 + 2)
                        pe.wait_ge(S(f"{L}_kbd"), b * 2 + 2)
                    pe.wait_ge(S("sub"), nu(L, g + 2))
                elif n == 1:
                    pe.wait_ge(S(f"{L}_v"), b + 1)
                elif n == 6:
                    pe.wait_ge(S("sub"), nu(L, g + 2))
                elif n == 7 and also_p:
                    pe.wait_ge(S("E_qs"), b + 2)
                    pe.wait_ge(S("E_kT"), b + 2)
                elif n == 7:
                    pe.wait_ge(S("sub"), nu(L, g))
                else:
                    pe.wait_ge(S("sub"), nu(L, g + 1))
                for h in range(2):
                    if L == "A":
                        pe.matmul(sl[:, h, :], ident16[:, :], causal[:, :], start=True, stop=False)
                    if L == "E":
                        pe.matmul(sl[:, h, :], ident16[:, :], bc(window[:, :], 1, 2), start=True, stop=False,
                                  skip_group_check=True)
                        for q in range(2):
                            mm = pe.matmul(sl[:, h, q * D:(q + 1) * D], qm[u][:, n, 2 * h + q, :],
                                           kT[u][:, :, :], start=False, stop=True, skip_group_check=True)
                    else:
                        mm = pe.matmul(sl[:, h, :], qT[u][:, n, :], kbd[u][:, n, 4 * h:4 * h + 4, :],
                                       start=(L == "B"), stop=True)
                mm.then_inc(S("sps"), 1)

            def transposes(b, n):
                g = b * U + n
                pe.wait_ge(S("exp"), nu(L, g + 1))
                for h, (free, done) in enumerate((("pca", "tra"), ("pcb", "trb"))):
                    pe.wait_ge(S(free), nu(L, g + 1))
                    for q in range(4):
                        at = (q * 2 + h) * P if L == "E" else (h * 4 + q) * P
                        mm = pe.transpose(PT[h][:, q * P:(q + 1) * P], e[n % 2][:, at:at + P], ident[:, :])
                    mm.then_inc(S(done), 1)

            def values(b, s, n):
                g = b * U + n
                u = 1 - s
                pe.wait_ge(S("pca"), nu(L, g + 2))
                pe.wait_ge(S("pcb"), nu(L, g + 2))
                if n == 0:
                    if not (L == "A" and isinstance(b, int) and b == 0):
                        pe.wait_ge(S("ot"), {"A": 0, "B": B, "E": 2 * B}[L] + b * OTN[L])
                    if U == 1:
                        pe.wait_ge(S(f"{L}_v"), b + 1)
                if L == "E":
                    if n == 4:
                        pe.wait_ge(S("ot"), 2 * B + b * 2 + 1)
                    r = 32 * (n % 4)
                    for k in range(2):
                        mm = pe.matmul(OB[r:r + VW, :], v[u][:, k * D + n * VW:k * D + (n + 1) * VW],
                                       pT[n % 2][:, k * HALF:(k + 1) * HALF], start=(k == 0), stop=(k == 1),
                                       tile_position=(0, r))
                else:
                    for h in range(8):
                        r, blk, head = 32 * (h % 4), 2 * n + h // 4, 8 * n + h
                        mm = pe.matmul(OB[r:r + VW, blk * P:(blk + 1) * P], v[u][:, head * VW:(head + 1) * VW],
                                       pT[n % 2][:, h * P:(h + 1) * P], start=True, stop=True,
                                       tile_position=(0, r))
                mm.then_inc(S("pv"), 1)

            def out_rows(c, r):
                pe.wait_ge(S("ot"), {"A": 0, "B": B, "E": 2 * B}[L] + c * OTN[L] + r + 1)
                if r == 0:
                    pe.wait_ge(S("xt"), nb(L, c + 1))
                else:
                    pe.wait_ge(S(f"{L}_an"), c * 2 + 1)
                for k in range(4):
                    mm = pe.transpose(MB[:, k * P:(k + 1) * P], oT[:, r, k * P:(k + 1) * P], ident[:, :])
                mm.then_inc(S(f"{L}_otr"), 1)

            def out_T(c):
                if L == "D":
                    pe.wait_ge(S("xt"), nb(L, c + 1))
                pe.wait_ge(S(f"{L}_an"), (c + 1) * (2 if L == "E" else 1))
                for k in range(C):
                    mm = pe.transpose(MB[:, k * P:(k + 1) * P], an[:, k * P:(k + 1) * P], ident[:, :])
                mm.then_inc(S(f"{L}_atr"), 1)

            def out_project(c):
                pe.wait_ge(S(f"{L}_at"), c + 1)
                pe_rows(pe, MB[:, D:2 * D], W[L, "wo"], aT).then_inc(S("y"), 1)

            def ref_rows(c, s):
                pe.wait_ge(S("B_an"), c + 1)
                for k in range(C):
                    mm = pe.transpose(MB[:, D + k * P:D + (k + 1) * P], refT[s][:, k, :], ident[:, :])
                mm.then_inc(S("y"), 1)

            def x_T(c, s):
                pe.wait_ge(S("xn"), nb(L, c + 1))
                for k in range(C):
                    mm = pe.transpose(MB[:, k * P:(k + 1) * P], xn[s][:, k * P:(k + 1) * P], ident[:, :])
                mm.then_inc(S("xtr"), 1)

            def linear_project(i, s):
                pe.wait_ge(S("D_xs"), i + 1)
                if not first(i):
                    pe.wait_ge(S("D_qk"), i)
                    pe.wait_ge(S("D_gx"), i)
                    pe.wait_ge(S("D_v"), i)
                pe_rows(pe, ps[:, 0, :], W[L, "wqk"], xs[s]).then_inc(S("D_qkps"), 1)
                pe_rows(pe, ps[:, 1, 0:D], W[L, "wg"], xs[s]).then_inc(S("D_gps"), 1)
                pe_rows(pe, ps[:, 2, :], W[L, "wv"], xs[s]).then_inc(S("D_vps"), 1)

            def linear_sums(b, u):
                pe.wait_ge(S("D_f"), b + 1)
                for c in range(C):
                    mm = pe.transpose(ps[:, 3, c * P:(c + 1) * P], f[u][:, c * P:(c + 1) * P], ident[:, :])
                mm.then_inc(S("D_qfps"), 1)
                pe.wait_ge(S("D_v"), b + 1)
                for n, rows in enumerate((P // 2, P)):
                    for c in range(C):
                        mm = pe.matmul(ps[:, 4 + n, c * D:(c + 1) * D], f[u][0:rows, D + c * P:D + (c + 1) * P],
                                       v[u][0:rows, c * D:(c + 1) * D], start=True, stop=True)
                mm.then_inc(S("D_gmps"), 1)

            def linear_out(b):
                pe.wait_ge(S("D_qf"), b + 1)
                pe.wait_ge(S("D_gm"), b * 2 + 2)
                for n in range(2):
                    r = 64 * n
                    for c in range(C):
                        mm = pe.matmul(ps[r:r + 64, 6, c * D:(c + 1) * D], qfT[:, c, r:r + 64],
                                       gm[:, n, c * D:(c + 1) * D], start=True, stop=True,
                                       tile_position=(0, r))
                mm.then_inc(S("D_num"), 1)

            def turn_two(i, s, p, c, f):
                if c:
                    scores(i - 1, s, 0, p)
                if f:
                    out_rows(i - 2, 0)
                if c:
                    scores(i - 1, s, 1, p)
                if f and L == "B":
                    ref_rows(i - 2, s)
                if p:
                    project(i, s)
                if f and L == "A":
                    out_T(i - 2)
                if c:
                    transposes(i - 1, 0)
                if p:
                    project2(i, s)
                if f and L == "A":
                    out_project(i - 2)
                if c:
                    transposes(i - 1, 1)
                    values(i - 1, s, 0)
                    values(i - 1, s, 1)
                if f:
                    x_T(i - 2, s)

            def turn_groups(i, s, p, c, f):
                for n in range(U + 3):
                    if n == 6 and p:
                        project(i, s)
                    if n == 8 and p:
                        project2(i, s)
                    if c and n < U:
                        scores(i - 1, s, n, p)
                    if f and n in (1, 2):
                        out_rows(i - 2, n - 1)
                    if f and n == 3:
                        out_T(i - 2)
                    if f and n == 4:
                        out_project(i - 2)
                    if f and n == 7:
                        x_T(i - 2, s)
                    if c and 2 <= n < U + 2:
                        transposes(i - 1, n - 2)
                    if c and n >= 3:
                        values(i - 1, s, n - 3)

            def turn_linear(i, s, p, c, f):
                if p:
                    linear_project(i, s)
                if f:
                    out_T(i - 2)
                if c:
                    linear_sums(i - 1, 1 - s)
                if f:
                    out_project(i - 2)
                if c:
                    linear_out(i - 1)
                if f:
                    x_T(i - 2, s)

            turns(pe, {"A": turn_two, "B": turn_two, "D": turn_linear, "E": turn_groups}[L])

        def pe_router(pe, L):
            w = 16 if L == "E" else E0
            pe.wait_ge(S("xt"), nb(L, B + 1))
            for b in range(B):
                for c in range(C):
                    mm = pe.matmul(ps[:, 0, b * w:(b + 1) * w], XT[:, c, b * P:(b + 1) * P], W[L, "wr"][:, c, :],
                                   start=(c == 0), stop=(c == C - 1))
            mm.then_inc(S(f"{L}_lgps"), 1)
            pe.wait_ge(S(f"{L}_cm"), 2 if L == "E" else 1)
            for h in range(2):
                for b in range(4):
                    at = (4 * h + b) * w
                    mm = pe.transpose(ps[0:w, 2 + h, b * P:(b + 1) * P], cm[:, at:at + w], ident[:, :])
                mm.then_inc(S(f"{L}_cps"), 1)

        def pe_moe(pe, L):
            n = BLOCKS[L]
            before_done(pe, L)
            pe.wait_ge(S("zero16"), 1)
            for m in range(4):
                pe.matmul(Y[:, m, :], ident16[:, :], zero16[:, :], start=True, stop=False, skip_group_check=True)

            def gate_up(x, u, t):
                if t == 0:
                    pe.wait_ge(S(f"{L}_wl"), x * 2 + 1)
                if not first(x):
                    pe.wait_ge(S(f"{L}_a1"), x * 2 + t - 1)
                for s in range(2):
                    i = 0
                    for w, xx in ((wh, XH), (wl, XH), (wh, XL)):
                        for c in range(C):
                            mm = pe.matmul(GU[t][s], w[u][:, (c * 2 + s) * P:(c * 2 + s + 1) * P],
                                           xx[:, c, t * HALF:(t + 1) * HALF], start=(i == 0), stop=(i == 5))
                            i += 1
                    mm.then_inc(S(f"{L}_gu"), 1)

            def down(x, u, t):
                if t == 0:
                    pe.wait_ge(S(f"{L}_wl"), x * 2 + 2)
                pe.wait_ge(S(f"{L}_al"), x * 2 + t + 1)
                for m in range(C):
                    for w, x_ in ((wh, ah), (wl, ah), (wh, al)):
                        mm = pe.matmul(Y[:, 2 * m + t, :], w[u][:, (4 + m) * P:(5 + m) * P],
                                       x_[t][:, :], start=False, stop=False, skip_group_check=True)
                mm.then_inc(S(f"{L}_down"), 1)

            for t in range(2):
                gate_up(0, 0, t)
            with pe.Fori(0, (n - 1) // 2) as j:
                for s in range(2):
                    for t in range(2):
                        gate_up(j * 2 + 1 + s, 1 - s, t)
                        down(j * 2 + s, s, t)
            if n % 2 == 0:
                for t in range(2):
                    gate_up(n - 1, 1, t)
                    down(n - 2, 0, t)
            for t in range(2):
                down(n - 1, (n - 1) % 2, t)

            def turn(i, s, begin, end):
                if begin:
                    pe.wait_ge(S(f"{L}_yt"), i + 1)
                    pe.wait_ge(S("z"), nb(L, i))
                    for c in range(C):
                        mm = pe.transpose(ps[:, 4 + 2 * s, c * P:(c + 1) * P], yT[s][:, c, :], ident[:, :])
                    mm.then_inc(S("y"), 1)
                if end and L != "F":
                    pe.wait_ge(S("xn"), nb(L, i))
                    pe.wait_ge(S("xt"), nb(L, i - 1))
                    for c in range(C):
                        mm = pe.transpose(ps[:, 5 + 2 * s, c * P:(c + 1) * P], xn[1 - s][:, c * P:(c + 1) * P],
                                          ident[:, :])
                    mm.then_inc(S("xtr"), 1)

            norm_turns(pe, turn)

        @block.tensor
        def _(pe):
            pe_attention(pe, "A")
            pe_attention(pe, "B")
            pe_router(pe, "B")
            pe_moe(pe, "C")
            pe_attention(pe, "D")
            pe_attention(pe, "E")
            pe_router(pe, "E")
            pe_moe(pe, "F")

        def act_x(act, L, b, bank):
            act.wait_ge(S("xtr"), nb(L, b + 1))
            act.activation(XT[:, :, tok(b)], bank[:, 0:D].rearrange("p (c q) -> p c q", c=C), ACT.Copy)\
               .then_inc(S("xt"), 1)

        def act_attention(act, L):
            U = UNITS[L]
            scale = 0.25 if L != "E" else float(1.0 / np.sqrt(np.float32(DH1)))
            loaded(act, L)
            before_done(act, L)

            def relu(i, s):
                act.wait_ge(S("B_fcps"), i + 1)
                for n, dst in enumerate((refT, supT)):
                    for c in range(C):
                        at = n * D + c * P
                        act.activation(dst[s][:, c, :], SLOT[(s + 1) % 2][:, 0, at:at + P], ACT.Relu,
                                       bias=W[L, "bfc"][:, c:c + 1]).then_inc(S("B_fc"), 1)

            def queries(i, s):
                if L == "E":
                    act.wait_ge(S("E_qps"), i + 1)
                    if not first(i):
                        act.wait_ge(S("E_qm"), i)
                        act.wait_ge(S("E_qmp"), i)
                    act.activation(qs[0:64, :], SLOT[0][0:64, 0, 0:D], ACT.Copy)
                    act.activation(qs2[0:64, :], SLOT[0][0:64, 0, D:2 * D], ACT.Copy).then_inc(S("E_qs"), 1)
                    act.wait_ge(S("E_kps"), i + 1)
                    act.activation(kT[s][0:64].rearrange("p s k -> p (s k)"), SLOT[0][0:64, 1, 0:2 * P], ACT.Copy)\
                       .then_inc(S("E_kT"), 1)
                    return
                act.wait_ge(S(f"{L}_qkps"), i + 1)
                for c in range(C):
                    act.activation(qT[s][:, c, :], SLOT[(s + 1) % 2][:, 0 if L == "A" else 1, c * P:(c + 1) * P],
                                   ACT.Identity, bias=W[L, "bq"][:, c:c + 1]).then_inc(S(f"{L}_q"), 1)

            def exps(b, n):
                act.wait_ge(S("sub"), nu(L, b * U + n + 3))
                act.activation(e[n % 2][:, :], e[n % 2][:, :], ACT.Exp, scale=scale).then_inc(S("exp"), 1)

            def copies(b, n):
                g = b * U + n
                act.wait_ge(S("pv"), nu(L, g + 1))
                for h, (ready, done) in enumerate((("tra", "pca"), ("trb", "pcb"))):
                    act.wait_ge(S(ready), nu(L, g + 1 + 2 * h))
                    act.activation(pT[n % 2][:, h * HALF:(h + 1) * HALF], PT[h], ACT.Copy).then_inc(S(done), 1)

            def outputs(b, r):
                act.wait_ge(S("pv"), nu(L, b * U + (r + 1) * U // OTN[L] + 2))
                act.activation(oT[:, r, :], OB, ACT.Copy).then_inc(S("ot"), 1)

            def out_T(c):
                act.wait_ge(S(f"{L}_atr"), c + 1)
                act.activation(aT[:, :, :].rearrange("p c q -> p (c q)"), MB[:, 0:D], ACT.Copy)\
                   .then_inc(S(f"{L}_at"), 1)

            def turn_two(i, s, p, c, f):
                if c:
                    exps(i - 1, 0)
                    exps(i - 1, 1)
                if p and L == "B":
                    relu(i, s)
                if p and L == "A":
                    queries(i, s)
                if f and L == "A":
                    out_T(i - 2)
                if c:
                    copies(i - 1, 0)
                if p and L == "B":
                    queries(i, s)
                if c:
                    copies(i - 1, 1)
                    outputs(i - 1, 0)
                if f:
                    act_x(act, L, i - 2, MB)

            def turn_groups(i, s, p, c, f):
                for n in range(U + 3):
                    if n == 6 and p:
                        queries(i, s)
                    if n == 7 and c:
                        outputs(i - 1, 0)
                    if c and 2 <= n < U + 2:
                        copies(i - 1, n - 2)
                    if c and n < U:
                        exps(i - 1, n)
                    if f and n == 3:
                        out_T(i - 2)
                    if f and n == 7:
                        act_x(act, L, i - 2, MB)
                if c:
                    outputs(i - 1, 1)

            def turn_linear(i, s, p, c, f):
                if f:
                    out_T(i - 2)
                if c:
                    act.wait_ge(S("D_qfps"), i)
                    act.activation(qfT[:, :, :].rearrange("p c q -> p (c q)"), ps[:, 3, 0:D], ACT.Copy)\
                       .then_inc(S("D_qf"), 1)
                if p:
                    act.wait_ge(S("D_gx"), i + 1)
                    act.activation(eg[s][:, :], gx[:, :], ACT.Exp, scale=-1.0).then_inc(S("D_eg"), 1)
                    act.wait_ge(S("D_rn"), i + 1)
                    act.activation(re[:, :], rn[:, :], ACT.Exp).then_inc(S("D_re"), 1)
                if f:
                    act_x(act, L, i - 2, MB)

            turns(act, {"A": turn_two, "B": turn_two, "D": turn_linear, "E": turn_groups}[L])

        def act_router(act, L):
            n_e = E0 if L == "B" else E1
            act.wait_ge(S("xt"), nb(L, B + 1))
            act.activation(XH[:, :, :], XT[:, :, :], ACT.Copy).then_inc(S(f"{L}_xh"), 1)
            act.wait_ge(S(f"{L}_lgm"), 1)
            act.activation(ex[:, 0:B * n_e], ex[:, 0:B * n_e], ACT.Exp).then_inc(S(f"{L}_ex"), 1)
            if L == "E":
                act.activation(sg[:, :], lg[:, 0:B * 16].rearrange("p (b n) -> p b n", n=16)[:, :, 15], ACT.Exp,
                               scale=-1.0).then_inc(S("E_sg"), 1)
            w = 16 if L == "E" else E0
            act.wait_ge(S(f"{L}_cps"), 2)
            if L == "B":
                for h in range(2):
                    act.activation(cT[0:w, h * HALF:(h + 1) * HALF], ps[0:w, 2 + h, :], ACT.Copy)\
                       .then_inc(S("B_cT"), 1)
            else:
                act.activation(cT[0:w, :], ps[0:w, 2:4, :].rearrange("p a t -> p (a t)"), ACT.Copy)\
                   .then_inc(S("E_cT"), 1)

        def act_moe(act, L):
            n = BLOCKS[L]
            before_done(act, L)

            def step(x, t):
                act.wait_ge(S(f"{L}_gu"), x * 4 + 2 * t + 1)
                if not first(x):
                    act.wait_ge(S(f"{L}_a1"), x * 2 + t - 1)
                act.activation(sgt[t], GU[t][0], ACT.Silu).then_inc(S(f"{L}_silu"), 1)
                act.wait_ge(S(f"{L}_a2"), x * 2 + t + 1)
                if not first(x):
                    act.wait_ge(S(f"{L}_down"), x * 2 + t - 1)
                act.activation(ah[t][:, :], a2[t], ACT.Copy).then_inc(S(f"{L}_ah"), 1)

            for t in range(2):
                step(0, t)
            with act.Fori(1, n) as x:
                for t in range(2):
                    step(x, t)
            act.wait_ge(S(f"{L}_down"), 2 * n)

            def turn(i, s, begin, end):
                if begin:
                    if not (isinstance(i, int) and i < 2):
                        act.wait_ge(S("y"), nb(L, i - 1))
                    act.activation(yT[s][:, :, :], Y.rearrange("p (c a) t -> p c (a t)", c=C)[:, :, tok(i)], ACT.Copy)\
                       .then_inc(S(f"{L}_yt"), 1)
                if end and L != "F":
                    act_x(act, L, i - 1, ps[:, 5 + 2 * s, :])

            norm_turns(act, turn)

        @block.scalar
        def _(act):
            act_attention(act, "A")
            act_attention(act, "B")
            act_router(act, "B")
            act_moe(act, "C")
            act_attention(act, "D")
            act_attention(act, "E")
            act_router(act, "E")
            act_moe(act, "F")

        def dve_stats(dve, L, b, u):
            dve.wait_ge(S("z"), nb(L, b + 2))
            dve.bn_stats(stats[:, :], z[u][:, :]).then_inc(S("stats"), 1)
            dve.wait_ge(S("stats"), nb(L, b + 1))
            settle(dve)
            dve.bn_aggr(agg[u][:, :], stats[:, :]).then_inc(S("agg"), 1)

        def dve_x(dve, L, b, u):
            dve.wait_ge(S("rstd"), nb(L, b + 1))
            dve.wait_ge(S("xrow"), nb(L, b + 1))
            if L == "F":
                dve.wait_ge(S(f"stored{u}"), b * 8 - 8 * u + 16)
            dve.tensor_scalar(xn[u][:, :], z[u][:, :], agg[u][:, 0:1], rstd[u][:, :], ALU.subtract, ALU.mult)\
               .then_inc(S("xn"), 1)

        def dve_attention(dve, L):
            U = UNITS[L]
            loaded(dve, L)
            before_done(dve, L)

            def keys(i, s):
                if L == "E":
                    dve.wait_ge(S("E_qs"), i + 1)
                    for h, q in enumerate((qs, qs2)):
                        ins = dve.tensor_tensor(qm[s][0:64, 0:4, 2 * h:2 * h + 2].rearrange("p g j q -> p g (j q)"),
                                                bc(q[0:64, :], 1, 4), bc(gmask[:, 0:4], 2, D), ALU.mult)
                    ins.then_inc(S("E_qm"), 1)
                    return
                dve.wait_ge(S(f"{L}_q"), i * 2 + 2)
                for c in range(C):
                    at = D + c * P
                    dve.scalar_tensor_tensor(kbd[s][:, c], bc(SLOT[(s + 1) % 2][:, 0 if L == "A" else 1, at:at + P], 1, 8),
                                             W[L, "bk"][:, c:c + 1], bc(hmask[:, :], 2, P), ALU.add, ALU.mult)\
                       .then_inc(S(f"{L}_kbd"), 1)

            def values(i, s):
                src = {"A": SLOT[(s + 1) % 2][:, 1, :], "B": SLOT[(s + 1) % 2][:, 0, :], "E": SLOT[1][:, 0, :]}[L]
                dve.wait_ge(S(f"{L}_vps"), i + 3)
                ones = W[L, "bv"] if L == "A" else W[L, "ones_v"]
                dve.tensor_tensor(v[s][:, :], src, ones[:, :], ALU.add).then_inc(S(f"{L}_v"), 1)

            def unit(b, s, n):
                g = b * U + n
                hn = 4 if L == "E" else 8
                sl = SLOT[(1 - s + n) % 2] if L != "E" else SLOT[(0, 1, 0, 1, 0, 1, 1, 0)[n]]
                s3 = sl.rearrange("p a (h k) -> p (a h) k", k=1024 // hn)
                dve.wait_ge(S("sps"), nu(L, g + 1))
                dve.reduce_max(mx[n % 2][:, 0:hn], s3, AX.X).then_inc(S("mx"), 1)
                dve.wait_ge(S("mx"), nu(L, g + 1))
                dve.wait_ge(S("trb"), nu(L, g + 1))
                dve.tensor_tensor(e[n % 2][:, :].rearrange("p (h k) -> p h k", h=hn), s3,
                                  bc(mx[n % 2][:, 0:hn], 2, 1024 // hn), ALU.subtract).then_inc(S("sub"), 1)

            def normalize(c, r):
                if L != "E":
                    dve.wait_ge(S(f"{L}_otr"), c + 1)
                    o = MB.rearrange("p (h w) -> p h w", w=VW)
                    dve.reciprocal(rden[:, 0, :], o[:, :, DH0]).then_inc(S(f"{L}_rden"), 1)
                    dve.wait_ge(S(f"{L}_rden"), c + 1)
                    dve.tensor_tensor(an[:, :].rearrange("p (h w) -> p h w", w=DH0), o[:, :, 0:DH0],
                                      bc(rden[:, 0, :], 2, DH0), ALU.mult).then_inc(S(f"{L}_an"), 1)
                    return
                dve.wait_ge(S("E_otr"), c * 2 + r + 1)
                o = MB.rearrange("p (j g w) -> p j g w", j=G1, w=VW)
                dve.reciprocal(rden[:, r, :].rearrange("p (j g) -> p j g", j=G1), o[:, :, :, DH1])\
                    .then_inc(S("E_rden"), 1)
                dve.wait_ge(S("E_rden"), c * 2 + r + 1)
                a4 = an[:, r * P:(r + 1) * P].rearrange("p (g j w) -> p j g w", g=4, w=DH1)
                dve.tensor_tensor(a4, o[:, :, :, 0:DH1],
                                  bc(rden[:, r, :].rearrange("p (j g) -> p j g", j=G1), 3, DH1), ALU.mult)\
                    .then_inc(S("E_an"), 1)

            def residual(c, s):
                dve.wait_ge(S("y"), nb(L, c + 1))
                dve.wait_ge(S("xb"), c + 1 + B * ATTN.index(L))
                if L == "B":
                    dve.wait_ge(S("B_an"), c + 1)
                    dve.tensor_tensor(z1[:, :], MB[:, D:2 * D], an[:, :], ALU.add).then_inc(S("B_z1"), 1)
                    dve.wait_ge(S("B_z1"), c + 1)
                    dve.tensor_tensor(z[s][:, :], z1[:, :], xb[:, :], ALU.add).then_inc(S("z"), 1)
                else:
                    dve.tensor_tensor(z[s][:, :], MB[:, D:2 * D], xb[:, :], ALU.add).then_inc(S("z"), 1)
                dve_stats(dve, L, c, s)

            def linear_in(i, s):
                qk3 = qk[:, :].rearrange("p (n two) -> p n two", two=2)
                rb3 = rb[:, :].rearrange("p (n two) -> p n two", two=2)
                dve.wait_ge(S("D_qkps"), i + 1)
                if not first(i):
                    dve.wait_ge(S("D_ra"), i)
                dve.tensor_tensor(qk[:, :], ps[:, 0, :], W[L, "bqk"][:, :], ALU.add).then_inc(S("D_qk"), 1)
                dve.wait_ge(S("D_gps"), i + 1)
                if not first(i):
                    dve.wait_ge(S("D_eg"), i)
                dve.tensor_tensor(gx[:, :], ps[:, 1, 0:D], W[L, "bg"][:, :], ALU.add).then_inc(S("D_gx"), 1)
                dve.wait_ge(S("D_qk"), i + 1)
                dve.tensor_tensor(rb3[:, :, 0], qk3[:, :, 1], W[L, "sin_lo"][:, :], ALU.mult).then_inc(S("D_rb"), 1)
                dve.tensor_tensor(rb3[:, :, 1], qk3[:, :, 0], W[L, "sin_hi"][:, :], ALU.mult).then_inc(S("D_rb"), 1)
                dve.wait_ge(S("D_vps"), i + 3)
                dve.tensor_tensor(v[s][:, :], ps[:, 2, :], W[L, "bv"][:, :], ALU.add).then_inc(S("D_v"), 1)
                dve.wait_ge(S("D_ra"), i + 1)
                dve.wait_ge(S("D_rb"), i * 2 + 2)
                dve.tensor_tensor(rr[:, :], ra[:, :], rb[:, :], ALU.add).then_inc(S("D_rr"), 1)

            def linear_features(i, s):
                dve.wait_ge(S("D_re"), i + 1)
                dve.scalar_tensor_tensor(f[s][:, :], rr[:, :], 0.0, re[:, :], ALU.max, ALU.add)\
                    .then_inc(S("D_f"), 1)

            def linear_masks(b):
                dve.wait_ge(S("D_gmps"), b + 1)
                for n in range(2):
                    dve.tensor_tensor(gm[:, n, :], ps[:, 4 + n, :], W[L, "blocks"][:, :], ALU.mult)\
                        .then_inc(S("D_gm"), 1)

            def linear_out(b, u):
                dve.wait_ge(S("D_num"), b + 1)
                num = ps[:, 6, :].rearrange("p (h w) -> p h w", w=VW)
                dve.tensor_scalar(den[:, :], num[:, :, DH0], 1e-6, None, ALU.add).then_inc(S("D_den"), 1)
                dve.wait_ge(S("D_den"), b + 1)
                dve.wait_ge(S("D_eg"), b + 1)
                dve.scalar_tensor_tensor(d2[:, :].rearrange("p (h w) -> p h w", w=DH0),
                                         eg[u][:, :].rearrange("p (h w) -> p h w", w=DH0), 1.0,
                                         bc(den[:, :], 2, DH0), ALU.add, ALU.mult).then_inc(S("D_d2"), 1)
                dve.wait_ge(S("D_d2"), b + 1)
                dve.reciprocal(r2[:, :], d2[:, :]).then_inc(S("D_r2"), 1)
                dve.wait_ge(S("D_r2"), b + 1)
                dve.tensor_tensor(an[:, :].rearrange("p (h w) -> p h w", w=DH0), num[:, :, 0:DH0],
                                  r2[:, :].rearrange("p (h w) -> p h w", w=DH0), ALU.mult).then_inc(S("D_an"), 1)

            def turn_two(i, s, p, c, f):
                if c:
                    unit(i - 1, s, 0)
                if f:
                    normalize(i - 2, 0)
                if c:
                    unit(i - 1, s, 1)
                if f and L == "B":
                    residual(i - 2, s)
                    dve_x(dve, L, i - 2, s)
                if p:
                    keys(i, s)
                    values(i, s)
                if f and L == "A":
                    residual(i - 2, s)
                    dve_x(dve, L, i - 2, s)

            def turn_groups(i, s, p, c, f):
                for n in range(U + 1):
                    if c and n < U:
                        unit(i - 1, s, n)
                    if f and n in (1, 2):
                        normalize(i - 2, n - 1)
                    if f and n == 4:
                        residual(i - 2, s)
                    if f and n == 5:
                        dve_x(dve, L, i - 2, s)
                    if p and n == 7:
                        keys(i, s)
                    if p and n == 8:
                        values(i, s)

            def turn_linear(i, s, p, c, f):
                if c:
                    linear_masks(i - 1)
                if p:
                    linear_in(i, s)
                if f:
                    residual(i - 2, s)
                if c:
                    linear_out(i - 1, 1 - s)
                if f:
                    dve_x(dve, L, i - 2, s)
                if p:
                    linear_features(i, s)

            turns(dve, {"A": turn_two, "B": turn_two, "D": turn_linear, "E": turn_groups}[L])

        def dve_router(dve, L):
            n_e, k = (E0, TOP0) if L == "B" else (E1, TOP1)
            w = 16 if L == "E" else E0
            l3 = (lg[:, 0:B * 16] if L == "E" else lg64[:, :]).rearrange("p (b n) -> p b n", n=w)
            rep3, ex3, em3, msk3, cm3 = (x[:, 0:B * (w if x in (lrep, cm) else n_e)].rearrange(
                "p (b n) -> p b n", b=B) for x in (lrep, ex, em, msk, cm))
            rt = S(f"{L}_route")
            done = [0]

            def then(ins):
                done[0] += 1
                ins.then_inc(rt, 1)
                dve.wait_ge(rt, done[0])

            dve.wait_ge(S(f"{L}_lgps"), 1)
            lps = ps[:, 0, 0:B * w].rearrange("p (b n) -> p b n", n=w)
            if L == "B":
                then(dve.tensor_copy(l3, lps))
            else:
                dve.memset(l3[:, :, n_e:15], SENT)
                dve.tensor_copy(l3[:, :, 15:16], lps[:, :, 15:16])
                then(dve.tensor_copy(l3[:, :, 0:n_e], lps[:, :, 0:n_e]))
            for b in range(B):
                ins = dve.max(top[:, b, :], l3[:, b, 0:n_e])
            then(ins)
            dve.tensor_tensor(ex3, l3[:, :, 0:n_e], bc(top[:, :, 0], 2, n_e), ALU.subtract)\
               .then_inc(S(f"{L}_lgm"), 1)
            if k < 8:
                dve.wait_ge(S(f"{L}_lgm"), 1)
                then(dve.memset(top[:, :, k:8], SENT))
            for b in range(B):
                ins = dve.match_replace(rep3[:, b, :], top[:, b, :], l3[:, b, :], -SENT)
            then(ins)
            then(dve.tensor_tensor(msk3, rep3[:, :, 0:n_e], l3[:, :, 0:n_e], ALU.not_equal))
            dve.wait_ge(S(f"{L}_ex"), 1)
            then(dve.tensor_tensor(em3, ex3, msk3, ALU.mult))
            then(dve.reduce_sum(esum[:, :], em3, AX.X))
            then(dve.reciprocal(einv[:, :], esum[:, :]))
            if L == "E":
                then(dve.memset(cm[:, 0:B * w], 0.0))
                dve.wait_ge(S("E_sg"), 1)
                then(dve.tensor_scalar(sg1[:, :], sg[:, :], 1.0, None, ALU.add))
                dve.reciprocal(cm3[:, :, n_e], sg1[:, :]).then_inc(S("E_cm"), 1)
            dve.tensor_tensor(cm3[:, :, 0:n_e], em3, bc(einv[:, :], 2, n_e), ALU.mult).then_inc(S(f"{L}_cm"), 1)
            dve.wait_ge(S(f"{L}_xh"), 1)
            dve.tensor_tensor(XL[:, :, :], XT[:, :, :], XH[:, :, :].bitcast(F32), ALU.subtract)\
               .then_inc(S(f"{L}_xl"), 1)

        def dve_moe(dve, L):
            before_done(dve, L)

            def step(x, k, t, j):
                g = x * 2 + t
                dve.wait_ge(S(f"{L}_silu"), g + 1)
                dve.wait_ge(S(f"{L}_gu"), g * 2 + 2)
                dve.tensor_tensor(a1[t], sgt[t], GU[t][1], ALU.mult).then_inc(S(f"{L}_a1"), 1)
                dve.wait_ge(S(f"{L}_a1"), g + 1)
                if t == 0:
                    dve.wait_ge(S(f"{L}_t{k}"), j * 16 + 16)
                dve.tensor_tensor(a2[t], a1[t], wbc[k][:, t * HALF:(t + 1) * HALF], ALU.mult)\
                   .then_inc(S(f"{L}_a2"), 1)
                dve.wait_ge(S(f"{L}_ah"), g + 1)
                dve.tensor_tensor(al[t][:, :], a2[t], ah[t][:, :].bitcast(F32), ALU.subtract)\
                   .then_inc(S(f"{L}_al"), 1)

            with dve.Fori(0, BLOCKS[L] // NW) as j:
                for k in range(NW):
                    for t in range(2):
                        step(j * NW + k, k, t, j)
            j = BLOCKS[L] // NW
            for k in range(BLOCKS[L] % NW):
                for t in range(2):
                    step(j * NW + k, k, t, j)

            def turn(i, s, begin, end):
                if begin:
                    dve.wait_ge(S("y"), nb(L, i + 1))
                    dve.wait_ge(S("xn"), nb(L, i - 1))
                    dve.tensor_tensor(z[s][:, :], ps[:, 4 + 2 * s, 0:D], X[:, bass.ds(i, 1), :].rearrange("p b d -> p (b d)"),
                                      ALU.add).then_inc(S("z"), 1)
                    dve_stats(dve, L, i, s)
                if end:
                    dve_x(dve, L, i - 1, 1 - s)

            norm_turns(dve, turn)

        @block.vector
        def _(dve):
            dve.memset(zero16[:, :], 0.0).then_inc(S("zero16"), 1)
            dve_attention(dve, "A")
            dve_attention(dve, "B")
            dve_router(dve, "B")
            dve_moe(dve, "C")
            dve_attention(dve, "D")
            dve_attention(dve, "E")
            dve_router(dve, "E")
            dve_moe(dve, "F")

        def pool_rstd(pool, L, b, u):
            st = S("newton")

            def then(ins, k):
                ins.then_inc(st, 1)
                pool.wait_ge(st, nb(L, b) * 5 + k)
                settle(pool)

            pool.wait_ge(S("agg"), nb(L, b + 1))
            settle(pool)
            then(pool.tensor_scalar(ve[:, :], agg[u][:, 1:2], EPS, None, ALU.add), 1)
            then(pool.tensor_tensor(y0[:, :], ve[:, :], minus_half[:, :], ALU.pow), 2)
            then(pool.tensor_tensor(nt[:, 0:1], y0[:, :], y0[:, :], ALU.mult), 3)
            then(pool.tensor_tensor(nt[:, 1:2], nt[:, 0:1], ve[:, :], ALU.mult), 4)
            then(pool.tensor_scalar(nt[:, 2:3], nt[:, 1:2], -0.5, 1.5, ALU.mult, ALU.add), 5)
            pool.tensor_tensor(rstd[u][:, :], nt[:, 2:3], y0[:, :], ALU.mult).then_inc(S("rstd"), 1)

        def pool_keep(pool, L, b, u):
            pool.wait_ge(S("xn"), nb(L, b + 1))
            settle(pool)
            pool.tensor_copy(X[:, bass.ds(b, 1), :].rearrange("p b d -> p (b d)"), xn[u][:, :])\
                .then_inc(S("xrow"), 1)

        def pool_attention(pool, L):
            loaded(pool, L)
            before_done(pool, L)

            def stage(i, s):
                pool.wait_ge(S(f"{L}_vps"), i + 1)
                settle(pool)
                if L in ("B", "E"):
                    pool.tensor_copy(cs[s][:, :, :], CTXT[:, :, tok(i)])
                pool.tensor_copy(xs[s][:, :, :], XT[:, :, tok(i)]).then_inc(S(f"{L}_xs"), 1)

            def residual(c):
                pool.wait_ge(S("z"), nb(L, c + 1))
                settle(pool)
                row = X[:, bass.ds(c, 1), :].rearrange("p b d -> p (b d)")
                bias = {"A": "bo", "B": "bv", "D": "bo"}.get(L)
                if bias:
                    pool.tensor_tensor(xb[:, :], row, W[L, bias][:, :], ALU.add).then_inc(S("xb"), 1)
                else:
                    pool.tensor_copy(xb[:, :], row).then_inc(S("xb"), 1)

            def rotary(i):
                pool.wait_ge(S("D_qk"), i + 1)
                pool.tensor_tensor(ra[:, :], qk[:, :], W[L, "cos"][:, :], ALU.mult).then_inc(S("D_ra"), 1)

            def negative(i):
                pool.wait_ge(S("D_rr"), i + 1)
                settle(pool)
                pool.tensor_scalar(rn[:, :], rr[:, :], 0.0, None, ALU.min).then_inc(S("D_rn"), 1)

            def masks(i, s):
                pool.wait_ge(S("E_qs"), i + 1)
                settle(pool)
                for h, q in enumerate((qs, qs2)):
                    for g in range(4, KV1):
                        ins = pool.tensor_scalar(qm[s][0:64, g, 2 * h:2 * h + 2].rearrange("p j q -> p (j q)"),
                                                 q[0:64, :], gmask[:, g:g + 1], None, ALU.mult)
                ins.then_inc(S("E_qmp"), 1)

            def turn(i, s, p, c, f):
                if p:
                    stage(i, s)
                if f:
                    residual(i - 2)
                if p and L == "D":
                    rotary(i)
                if f:
                    if L == "D":
                        if p:
                            negative(i)
                        pool_rstd(pool, L, i - 2, s)
                    else:
                        pool_rstd(pool, L, i - 2, s)
                    pool_keep(pool, L, i - 2, s)
                elif p and L == "D":
                    negative(i)
                if p and L == "E":
                    masks(i, s)

            turns(pool, turn)

        def pool_moe(pool, L):
            n = BLOCKS[L]

            def split(x, u, k, j):
                pool.wait_ge(S(f"{L}_w{k}"), j * 16 + 16)
                settle(pool)
                for h, (lo, hi) in enumerate(((0, 4 * P), (4 * P, WCOLS))):
                    if not (isinstance(x, int) and x < 2):
                        pool.wait_ge(S(f"{L}_down") if h else S(f"{L}_gu"), x * 2 - 2 if h else x * 4 - 4)
                        settle(pool)
                    pool.tensor_copy(wh[u][:, lo:hi], wraw[k][:, lo:hi]).then_inc(S(f"{L}_wh"), 1)
                    pool.wait_ge(S(f"{L}_wh"), x * 2 + h + 1)
                    pool.tensor_tensor(wl[u][:, lo:hi], wraw[k][:, lo:hi], wh[u][:, lo:hi].bitcast(F32),
                                       ALU.subtract).then_inc(S(f"{L}_wl"), 1)

            for k in range(NW):
                split(k, k % 2, k, 0)
            with pool.Fori(1, n // NW) as j:
                for k in range(NW):
                    split(j * NW + k, k % 2, k, j)
            for k in range(n % NW):
                split(n // NW * NW + k, k % 2, k, n // NW)

            def turn(i, s, begin, end):
                if begin:
                    pool_rstd(pool, L, i, s)
                if end:
                    pool_keep(pool, L, i - 1, 1 - s)

            norm_turns(pool, turn)

        @block.gpsimd
        def _(pool):
            pool.memset(minus_half[:, :], -0.5).then_inc(S("half"), 1)
            pool.wait_ge(S("half"), 1)
            for L, part in (("A", pool_attention), ("B", pool_attention), ("C", pool_moe),
                            ("D", pool_attention), ("E", pool_attention), ("F", pool_moe)):
                part(pool, L)


def constants():
    def bf16(x):
        return (np.ascontiguousarray(x, np.float32).view(np.uint32) >> 16).astype(np.uint16)

    big = np.float32(-1e30)
    q, k = np.arange(P)[:, None], np.arange(P)[None, :]
    c = {}
    c["head_mask"] = (np.arange(P)[:, None] // DH0 == np.arange(8)[None, :]).astype(np.float32)
    c["causal_bf16"] = bf16(np.tile(np.where(k > q, big, np.float32(0)), (1, 4)))
    delta = q - k
    win = [np.where((delta >= 0) & (delta < w), np.float32(0), big) for w in (64, 32)]
    c["window_bf16"] = bf16(np.concatenate(win, 1))
    c["ident"] = np.eye(P, dtype=np.float32)
    c["ident_bf16"] = bf16(np.eye(P))

    def ones_col(heads, at):
        row = np.zeros((heads, VW), np.float32)
        row[:, at] = 1
        return np.broadcast_to(row.reshape(-1), (P, heads * VW)).copy()

    c["B_ones_v"] = ones_col(H0, DH0)
    c["E_ones_v"] = ones_col(2 * KV1, DH1)
    inv = np.float32(1.0) / np.float32(10000.0) ** (np.arange(0, DH0, 2, dtype=np.float32) / np.float32(DH0))
    ang = np.arange(P, dtype=np.float32)[:, None] * inv[None, :].astype(np.float32)
    cos, sin = np.cos(ang).astype(np.float32), np.sin(ang).astype(np.float32)
    c["D_cos"] = np.tile(np.repeat(cos, 2, 1), (1, 2 * H0))
    c["D_sin_lo"] = np.tile(-sin, (1, 2 * H0))
    c["D_sin_hi"] = np.tile(sin, (1, 2 * H0))
    rows = np.arange(P)[:, None] // DH0
    cols = (np.arange(2 * D)[None, :] % D) // VW
    c["D_blocks"] = (rows == cols).astype(np.float32)
    c["group_mask"] = (np.arange(64)[:, None] // DH1 == np.arange(KV1)[None, :]).astype(np.float32)
    heads = KV1 * G1
    slope = 2.0 ** (-8.0 * np.arange(heads) / heads) * np.sqrt(float(DH1))
    pos = np.arange(P) - 64.0
    qrow = np.zeros((64, heads, P))
    qrow[0] = -slope[:, None] * pos[None, :]
    qrow[1] = slope[:, None]
    c["E_qrow"] = qrow.reshape(64, heads * P).astype(np.float32)
    krow = np.zeros((64, 2, P))
    krow[0] = 1
    krow[1] = pos
    c["E_krow"] = krow.reshape(64, 2 * P).astype(np.float32)
    return c


def kernel(**inputs):
    import concourse.bacc as bacc
    from concourse.bass_utils import run_bass_kernel_spmd

    n = {k: np.asarray(v) for k, v in inputs.items()}

    def chunks(w):
        return w.reshape(-1, P, w.shape[1]).transpose(1, 0, 2)

    def T_layout(x):
        return chunks(x.reshape(T, D).T)

    def cols(b):
        return b.reshape(-1, P).T

    def spread(b):
        return np.broadcast_to(b, (P, b.shape[-1]))

    def heads_wide(w, h):
        r = np.zeros((w.shape[0], h, VW), w.dtype)
        r[:, :, :w.shape[1] // h] = w.reshape(w.shape[0], h, -1)
        return r.reshape(w.shape[0], h * VW)

    def values_bias(b, h):
        r = heads_wide(b[None], h).reshape(h, VW)
        r[:, b.shape[0] // h] = 1
        return spread(r.reshape(-1))

    def blocks(layer, gu, down):
        nb = BLOCKS[layer]
        pad = nb * P - down.shape[0]
        gu = np.concatenate([gu, np.zeros((D, 2, pad), gu.dtype)], 2)
        down = np.concatenate([down, np.zeros((pad, D), down.dtype)])
        gu = gu.reshape(C, P, 2, nb, P).transpose(3, 1, 0, 2, 4).reshape(nb, P, C * 2 * P)
        return np.concatenate([gu, down.reshape(nb, P, D)], 2)

    d = constants()
    d["x_t"], d["ctx_t"] = T_layout(n["x"]), T_layout(n["ctx_2048"])
    d["x_rows"] = n["x"].transpose(1, 0, 2)
    w, b = n["L0_attn_W_in"].T, n["L0_attn_b_in"]
    d["A_wq"], d["A_wk"], d["A_wv"] = chunks(w[:, :D]), chunks(w[:, D:2 * D]), chunks(heads_wide(w[:, 2 * D:], H0))
    d["A_bq"], d["A_bk"], d["A_bv"] = cols(b[:D]), cols(b[D:2 * D]), values_bias(b[2 * D:], H0)
    d["A_wo"], d["A_bo"] = chunks(n["L0_attn_W_out"].T), spread(n["L0_attn_b_out"])
    p = "L0_xattn_"
    d["B_wfc"], d["B_bfc"] = chunks(n[p + "W_fc"].T), cols(n[p + "b_fc"])
    d["B_wq"], d["B_bq"] = chunks(n[p + "W_q"].T), cols(n[p + "b_q"])
    d["B_wk"], d["B_bk"] = chunks(n[p + "W_k"].T), cols(n[p + "b_k"])
    d["B_wv"] = chunks(heads_wide(n[p + "W_v"].reshape(D, D).T, H0))
    d["B_bv"] = spread(n[p + "b_v"])
    d["B_wr"] = chunks(n["L0_ffn_gate_weight"].T)
    gu = n["L0_ffn_gate_up_weights"].reshape(E0, D, 2, I0).transpose(1, 2, 0, 3).reshape(D, 2, E0 * I0)
    d["C_w"] = blocks("C", gu, n["L0_ffn_down_weights"].reshape(E0 * I0, D))
    p = "L1_attn_"
    d["D_wqk"] = chunks(np.concatenate([n[p + "Wq"].T, n[p + "Wk"].T], 1))
    d["D_bqk"] = spread(np.concatenate([n[p + "bq"], n[p + "bk"]]))
    d["D_wv"], d["D_bv"] = chunks(heads_wide(n[p + "Wv"].T, H0)), values_bias(n[p + "bv"], H0)
    d["D_wg"], d["D_bg"] = chunks(n[p + "Wg"].T), spread(n[p + "bg"])
    d["D_wo"], d["D_bo"] = chunks(n[p + "Wo"].T), spread(n[p + "bo"])
    p = "L1_xattn_"
    d["E_wq"] = chunks(n[p + "Wq"].reshape(2 * D, KV1, G1, DH1).transpose(0, 2, 1, 3).reshape(2 * D, D))
    d["E_wk"], d["E_wsk"] = chunks(n[p + "Wk"]), chunks(n[p + "Wsk"])
    d["E_wv"], d["E_wsv"] = chunks(heads_wide(n[p + "Wv"], KV1)), chunks(heads_wide(n[p + "Wsv"], KV1))
    d["E_wo"] = chunks(n[p + "Wo"])
    p = "L1_ffn_"
    wr = np.zeros((D, 16), np.float32)
    wr[:, :E1], wr[:, 15] = n[p + "router_weight"].T, n[p + "shared_gate_w"][0]
    d["E_wr"] = chunks(wr)
    gu = n[p + "gate_up_proj"].reshape(E1, 2, I1, D).transpose(3, 1, 0, 2).reshape(D, 2, E1 * I1)
    sh = np.stack([n[p + "sh_gate_w"].T, n[p + "sh_up_w"].T], 1)
    down = [n[p + "down_proj"].transpose(0, 2, 1).reshape(E1 * I1, D), n[p + "sh_down_w"].T]
    d["F_w"] = blocks("F", np.concatenate([gu, sh], 2), np.concatenate(down))

    nc = bacc.Bacc("TRN2", target_bir_lowering=False, num_devices=1)
    arrays, args = {}, {}
    for name, x in d.items():
        arrays[f"in_{name}"] = np.ascontiguousarray(x)
        args[name] = nc.dram_tensor(f"in_{name}", x.shape, mybir.dt.from_np(x.dtype), kind="ExternalInput").ap()
    out = nc.dram_tensor("out", (B, P, D), F32, kind="ExternalOutput").ap()
    build(nc, args, out)
    r = run_bass_kernel_spmd(nc, [arrays], core_ids=[0])
    return r.results[0]["out"]
```

```python
from contextlib import ExitStack

import numpy as np

import concourse.bass as bass
from concourse import mybir

F32 = mybir.dt.float32
F32R = mybir.dt.float32r
BF16 = mybir.dt.bfloat16
ALU = mybir.AluOpType
ACT = mybir.ActivationFunctionType
AX = mybir.AxisListType

P = 128
B = 8
T = B * P
D = 256
C = D // P
VW = 32
DH0, H0 = 16, 16
DH1, KV1, G1 = 8, 8, 4
HALF = 512
EPS = 1e-5
E0, I0, TOP0 = 64, 96, 8
E1, I1, TOP1 = 8, 176, 2
ISH = 704
UNITS_OF = {"C": E0 * I0, "F": E1 * I1 + ISH}
BLOCKS = {L: -(-n // P) for L, n in UNITS_OF.items()}
RUN = {"C": 32, "F": 16}
KR = 100
SENT = -3.0e38


def build(nc, a, out):
    ctx = ExitStack()
    with ctx:
        def sb(name, shape, dt=F32):
            return ctx.enter_context(nc.sbuf_tensor(name, shape, dt))

        sems = {}

        def S(name):
            if name not in sems:
                sems[name] = ctx.enter_context(nc.semaphore(name))
            return sems[name]

        loads = {}

        def const(layer, name, dt=F32):
            src = a[name]
            t = sb("c_" + name, list(src.shape), dt)
            loads.setdefault(layer, []).append((t[:, :].bitcast(src.dtype) if dt == BF16 else t, src))
            return t

        arena = sb("arena", [P, 9856])
        filled = {"AB": 0, "DE": 0}

        def weight(layer, name):
            src = a[f"{layer}_{name}"]
            both = "AB" if layer in "AB" else "DE"
            n = int(np.prod(src.shape[1:]))
            t = arena[:, filled[both]:filled[both] + n]
            filled[both] += n
            assert filled[both] <= arena.shape[1]
            if len(src.shape) == 3:
                t = t.rearrange("p (c n) -> p c n", c=src.shape[1])
            loads.setdefault(layer, []).append((t, src))
            W[layer, name] = t

        W = {}

        XT = const("A", "x_t")
        hmask = const("A", "head_mask")
        causal = const("A2", "causal_bf16", BF16)
        ident16 = const("A2", "ident_bf16", BF16)
        ident = const("A2", "ident")
        X = const("A2", "x_rows")
        CTXT = const("B", "ctx_t")
        for layer, names in (("A", "wq wk wv bq bk bv wo bo"),
                             ("B", "wfc bfc wq wk wv bq bk bv wr"),
                             ("D", "wqk wv wg bqk bv bg wo bo cos sin_lo sin_hi blocks"),
                             ("E", "wq wk wsk wv wsv wo ones_v wr")):
            for n in names.split():
                weight(layer, n)
        gmask = const("E", "group_mask")
        window = const("E", "window_bf16", BF16)

        xs = [sb(f"xs{u}", [P, C, P]) for u in range(2)]
        cs = [sb(f"cs{u}", [P, C, P]) for u in range(2)]
        refT = [sb(f"refT{u}", [P, C, P]) for u in range(2)]
        supT = [sb(f"supT{u}", [P, C, P]) for u in range(2)]
        qT = [sb(f"qT{u}", [P, C, P]) for u in range(2)]
        kbd = [sb(f"kbd{u}", [P, C, 8, P]) for u in range(2)]
        shared = [sb(f"shared{u}", [P, KV1 * G1 * P], F32R) for u in range(2)]
        qm = [m[:, :].rearrange("p (g j q) -> p g j q", g=KV1, j=G1) for m in shared]
        kT = [[sb(f"kT{u}{t}", [P, 2, P], F32R) for t in range(2)] for u in range(2)]
        v = [sb(f"v{u}", [P, 2 * D]) for u in range(2)]
        e = [sb(f"e{u}", [P, 1024]) for u in range(2)]
        pT = [sb(f"pT{u}", [P, 1024]) for u in range(2)]
        mx = [sb(f"mx{u}", [P, 8]) for u in range(2)]
        for u in range(2):
            loads["A"].append((v[u], a["A_ones_v"]))
        v3 = [x[:, :].rearrange("p (h w) -> p h w", w=VW)[:, :, 0:DH0] for x in v]
        oT = sb("oT", [P, 2, HALF])
        rden = sb("rden", [P, 2, 16])
        an = sb("an", [P, D])
        aT = sb("aT", [P, C, P])
        xb = sb("xb", [P, D])
        z1 = sb("zsum", [P, D])
        z = [sb(f"z{u}", [P, D]) for u in range(2)]
        stats = sb("stats", [P, 6])
        agg = [sb(f"agg{u}", [P, 2]) for u in range(2)]
        newton8 = sb("newton8", [P, 5, 8])
        stats8 = sb("stats8", [P, B, 6])
        agg8 = sb("agg8", [P, B, 2])
        rstd8 = sb("rstd8", [P, B])
        rstd = [sb(f"rstd{u}", [P, 1]) for u in range(2)]
        minus_half = sb("minus_half", [P, 4])
        xn = [sb(f"xn{u}", [P, D]) for u in range(2)]
        qk = e[0][:, 0:512]
        ra = e[0][:, 512:1024]
        rb = e[1][:, 0:512]
        rr = e[1][:, 512:1024]
        rn = pT[0][:, 0:512]
        re = pT[0][:, 512:1024]
        f = [sb(f"f{u}", [P, 2 * D]) for u in range(2)]
        gx = refT[0][:, :, :].rearrange("p c q -> p (c q)")
        eg = [supT[u][:, :, :].rearrange("p c q -> p (c q)") for u in range(2)]
        qfT = qT[0]
        qst = [f[t][:, :].bitcast(F32R) for t in range(2)]
        flat = kbd[0][:, :, :, :].rearrange("p c h k -> p (c h k)").bitcast(F32R)
        qh, ql = flat[:, 0:D], flat[:, D:2 * D]
        kh, kl = flat[0:64, 2 * D:3 * D], flat[0:64, 3 * D:4 * D]
        gm = oT
        den = sb("den", [P, 16])
        d2 = sb("d2", [P, D])
        r2 = sb("r2", [P, D])
        lg = qT[0][:, :, :].rearrange("p c q -> p (c q)")
        lg64 = pT[0][:, 0:B * E0]
        lrep = pT[0][:, 512:1024]
        msk = pT[1][:, 0:512]
        ex = pT[1][:, 512:1024]
        em = e[0][:, 0:512]
        cm = e[0][:, 512:1024]
        top = sb("top", [P, B, 8])
        esum = sb("esum", [P, B])
        einv = sb("einv", [P, B])
        sg = sb("sg", [P, B])
        sg1 = sb("sg1", [P, B])
        cT = sb("cT", [64, T])
        XH, XL = (shared[0][:, k * C * T:(k + 1) * C * T].rearrange("p (c t) -> p c t", c=C) for k in range(2))
        WCOLS = C * 2 * P + D
        NW = 4
        wraw = [sb(f"wraw{k}", [P, WCOLS]) for k in range(NW)]
        wh, wl = ([shared[1][:, (2 * k + u) * WCOLS:(2 * k + u + 1) * WCOLS] for u in range(2)] for k in range(2))
        wbc = [kbd[k // 2][:, k % 2].rearrange("p h k -> p (h k)") for k in range(NW)]
        sgt = [e[u][:, 0:HALF] for u in range(2)]
        a1 = [e[u][:, HALF:2 * HALF] for u in range(2)]
        a2 = [pT[u][:, 0:HALF] for u in range(2)]
        ah = [shared[1][:, 4 * WCOLS + u * HALF:4 * WCOLS + (u + 1) * HALF] for u in range(2)]
        al = [sb(f"al{u}", [P, HALF], F32R) for u in range(2)]
        zero16 = sb("zero16", [P, HALF], BF16)
        ysb = e
        zsb = pT

        combine = {L: nc.dram_tensor(f"combine_{L}", [BLOCKS[L] * P // RUN[L], T], F32).ap() for L in "CF"}
        shared_row = nc.dram_tensor("shared_row", [1, T], F32).ap()

        ps = ctx.enter_context(nc.psum_tensor("ps", [P, 8, HALF], F32))
        SLOT = [ps[:, 2 * s:2 * s + 2, :] for s in range(2)]
        PT = [ps[:, 4 + s, :] for s in range(2)]
        OB = ps[:, 6, :]
        MB = ps[:, 7, :]
        Y = ps[:, 0:4, :]
        GU = [[ps[:, 4 + 2 * t + s, :] for s in range(2)] for t in range(2)]

        def tok(b):
            return bass.ds(b * P, P)

        def bc(ap, axis, n):
            x = ap.unsqueeze(axis)
            shape = list(x.shape)
            shape[axis] = n
            return x.to_broadcast(shape)

        ATTN = ("A", "B", "D", "E")
        UNITS = {"A": 2, "B": 2, "E": 8, "D": 0}
        ORDER = "ABCDEF"

        def nb(L, n):
            return ORDER.index(L) * B + n

        def nu(L, n):
            return sum(UNITS[M] * B for M in ORDER[:ORDER.index(L)] if M in UNITS) + n

        def nh(L, n):
            return (L == "F") * 2 * BLOCKS["C"] + n

        EARLY = 5
        BEFORE = {"B": "A", "C": "B", "D": "C", "E": "D", "F": "E"}
        NEXT_IS_MOE = ("B", "E")
        OTN = {"A": 1, "B": 1, "E": 2}

        def loaded(eng, layer):
            eng.wait_ge(S(f"{layer}_loaded"), 16 * len(loads[layer]))

        def settle(eng):
            eng.sem_inc(S("settled"), 1)

        def before_done(eng, L):
            if L in BEFORE:
                p = BEFORE[L]
                eng.wait_ge(S("xt"), nb(L, 1))
                eng.wait_ge(S("xrow"), nb(L, 2))
                if p in NEXT_IS_MOE:
                    eng.wait_ge(S(f"{p}_cT"), 2 if p == "B" else 1)

        def two_layers(eng, part, turn_L, turn_M, L, M):
            def turn(fn, x, i, s, *have):
                fn(s, *((x, i - k) if h else None for k, h in enumerate(have)))

            def loop(fn, x):
                with eng.Fori(0, B // 2 - 1) as j:
                    turn(fn, x, j * 2 + 2, 0, True, True, True)
                    turn(fn, x, j * 2 + 3, 1, True, True, True)

            x = part(eng, L)
            turn(turn_L, x, 0, 0, True, False, False)
            turn(turn_L, x, 1, 1, True, True, False)
            loop(turn_L, x)
            y = part(eng, M)
            turn_L(0, (y, 0), (x, B - 1), (x, B - 2))
            turn_M(1, (y, 1), (y, 0), (x, B - 1))
            loop(turn_M, y)
            turn(turn_M, y, B, 0, False, True, True)
            turn(turn_M, y, B + 1, 1, False, False, True)

        def first(i):
            return isinstance(i, int) and i == 0

        block = ctx.enter_context(nc.Block())

        def moe_loads(sp, L):
            def weights(x, k):
                sp.dma_start(wraw[k][:, :], a[f"{L}_w"][bass.ds(x, 1)].rearrange("o p n -> p (o n)"))\
                  .then_inc(S(f"{L}_w{k}"), 16)

            def token_weights(x, k):
                runs = P // RUN[L]
                src = combine[L][bass.ds(x * runs, runs)]
                sp.dma_start(wbc[k][:, :], bc(src, 1, RUN[L])).then_inc(S(f"{L}_t{k}"), 16)

            for k in range(NW):
                weights(k, k)
            sp.wait_ge(S(f"{BEFORE[L]}_cT"), 2 if L == "C" else 1)
            settle(sp)
            n_e, runs = (E0, I0 // RUN[L]) if L == "C" else (E1, I1 // RUN[L])
            rows = combine[L][0:n_e * runs].rearrange("(k e) t -> k e t", e=n_e)
            sp.dma_start(rows[0], cT[0:n_e, :]).then_inc(S(f"{L}_out0"), 16)
            if L == "F":
                sp.dma_start(shared_row, cT[E1:E1 + 1, :]).then_inc(S("shared_out"), 16)
            for k in range(1, runs):
                sp.dma_start(rows[k], cT[0:n_e, :]).then_inc(S(f"{L}_out"), 16)
            sp.wait_ge(S(f"{L}_out0"), 16)
            for k in range(NW):
                per = P // RUN[L]
                at = k * per % n_e
                sp.dma_start(wbc[k][:, :], bc(combine[L][at:at + per], 1, RUN[L])).then_inc(S(f"{L}_t{k}"), 16)
            if L == "F":
                sp.wait_ge(S("shared_out"), 16)
                rest = combine[L].shape[0] - n_e * runs
                sp.dma_start(combine[L][n_e * runs:], shared_row.to_broadcast([rest, T])).then_inc(S(f"{L}_out"), 16)
            sp.wait_ge(S(f"{L}_out"), 16 * (runs - (L == "C")))
            settle(sp)
            if L == "C":
                for M in ("D", "E"):
                    for t, src in loads[M]:
                        sp.dma_start(t[tuple(slice(None) for _ in t.shape)], src).then_inc(S(f"{M}_loaded"), 16)

            def refill(j, k):
                done = (j - 1) * (2 * NW) + 2 * k + 2
                sp.wait_ge(S(f"{L}_wl"), done)
                settle(sp)
                weights(j * NW + k, k)
                sp.wait_ge(S(f"{L}_a2"), done)
                settle(sp)
                token_weights(j * NW + k, k)

            with sp.Fori(1, BLOCKS[L] // NW) as j:
                for k in range(NW):
                    refill(j, k)
            for k in range(BLOCKS[L] % NW):
                refill(BLOCKS[L] // NW, k)

        @block.sync
        def _(sp):
            sp.sem_inc(S("sub"), 2)
            sp.sem_inc(S("z"), 1)
            sp.sem_inc(S("trb"), 2)
            sp.sem_inc(S("pca"), 1)
            sp.sem_inc(S("pcb"), 1)
            sp.sem_inc(S("pv"), 2)
            sp.sem_inc(S("xt"), 1)
            sp.sem_inc(S("xrow"), 2)
            for L in ATTN:
                sp.sem_inc(S(f"{L}_vps"), 2)

            def load_weights(L):
                for t, src in loads[L]:
                    sp.dma_start(t[tuple(slice(None) for _ in t.shape)], src).then_inc(S(f"{L}_loaded"), 16)

            load_weights("A")
            load_weights("A2")
            load_weights("B")
            moe_loads(sp, "C")
            with sp.Fori(0, B // 2) as j:
                for u in range(2):
                    for t in range(2):
                        for n, part in ((0, qh), (2, qh), (1, ql)):
                            if t == 0 and n < 2:
                                sp.wait_ge(S("E_qh" if n == 0 else "E_ql"), j * 2 + u + 1)
                                settle(sp)
                            to = qst[t][32 * n:32 * n + 32].bitcast(F32).rearrange("p (c o q) -> p c o q", c=2, o=2)
                            for o in range(2):
                                r = 64 * o + 32 * t
                                sp.dma_start(to[:, :, o], part[r:r + 32].bitcast(F32).rearrange(
                                    "p (c q) -> p c q", c=2)).then_inc(S(f"E_q{t}st"), 16)
            moe_loads(sp, "F")
            for h in range(2):
                sp.wait_ge(S("xn"), nb("F", 4 * h + 4))
                sp.dma_start(out[4 * h:4 * h + 4].rearrange("b p d -> p b d"), X[:, 4 * h:4 * h + 4, :])\
                  .then_inc(S("stored"), 16)
            sp.wait_ge(S("stored"), 32)

        def pe_T(pe, dst, w, src):
            for c in range(C):
                for k in range(C):
                    mm = pe.matmul(dst[:, c * P:(c + 1) * P], w[:, k, c * P:(c + 1) * P], src[:, k, :],
                                   start=(k == 0), stop=(k == C - 1))
            return mm

        def pe_rows(pe, dst, w, src):
            for k in range(C):
                mm = pe.matmul(dst, src[:, k, :], w[:, k, :], start=(k == 0), stop=(k == C - 1))
            return mm

        def pe_attention(pe, L):
            U = UNITS[L]
            loaded(pe, L)
            if L == "D":
                before_done(pe, L)
            if L == "E":
                pe.wait_ge(S("alibi_rows"), 96)

            def slot(s, n):
                return SLOT[(1 - s + n) % 2] if L != "E" else SLOT[(s + (1, 0, 1, 0, 1, 1, 1, 0)[n]) % 2]

            def queries(i, s, half):
                if half == 0:
                    pe.wait_ge(S("E_xs"), i + 1)
                    if first(i):
                        pe.wait_ge(S("D_qk"), B)
                        pe.wait_ge(S("D_gx"), B)
                    else:
                        pe.wait_ge(S("sub"), nu(L, i * 8 - 2))
                cols = slice(half * P, (half + 1) * P)
                for k in range(2 * C):
                    mm = pe.matmul(SLOT[s][:, 0, cols], W[L, "wq"][:, k, cols],
                                   (cs if k < C else xs)[s][:, k % C, :], start=(k == 0), stop=(k == 2 * C - 1))
                if half == 1:
                    mm.then_inc(S("E_qps"), 1)

            def project(i, s):
                pe.wait_ge(S(f"{L}_xs"), i + 1)
                if L == "B" or not first(i):
                    pe.wait_ge(S("sub"), nu(L, i * 2 + 1))
                sl = SLOT[(s + 1) % 2]
                if L == "A":
                    pe_T(pe, sl[:, 0, 0:D], W[L, "wq"], xs[s])
                    pe_T(pe, sl[:, 0, D:2 * D], W[L, "wk"], xs[s]).then_inc(S("A_qkps"), 1)
                if L == "B":
                    pe_T(pe, sl[:, 0, 0:D], W[L, "wfc"], xs[s])
                    pe_T(pe, sl[:, 0, D:2 * D], W[L, "wfc"], cs[s]).then_inc(S("B_fcps"), 1)

            def project2(i, s):
                if L == "A":
                    pe_rows(pe, SLOT[(s + 1) % 2][:, 1, 0:D], W[L, "wv"], xs[s]).then_inc(S("A_vps"), 1)
                if L == "B":
                    sl = SLOT[(s + 1) % 2]
                    pe.wait_ge(S("B_fc"), i * 4 + 4)
                    pe_T(pe, sl[:, 1, 0:D], W[L, "wq"], refT[s])
                    pe_T(pe, sl[:, 1, D:2 * D], W[L, "wk"], supT[s]).then_inc(S("B_qkps"), 1)
                    pe_rows(pe, sl[:, 0, 0:D], W[L, "wv"], supT[s]).then_inc(S("B_vps"), 1)
                if L == "E":
                    for n, (wn, src) in enumerate((("wsk", cs), ("wk", xs))):
                        for k in range(C):
                            mm = pe.matmul(SLOT[s][0:64, 1, n * P:(n + 1) * P], W[L, wn][:, k, :], src[s][:, k, :],
                                           start=(k == 0), stop=(k == C - 1))
                    for n, (wn, src) in enumerate((("wsv", cs), ("wv", xs))):
                        at = D + n * 64
                        mm = pe_rows(pe, SLOT[s][:, 1, at:at + 64], W[L, wn], src[s])
                    mm.then_inc(S("E_vps"), 1)

            def scores(b, s, n, also_p):
                g = b * U + n
                u = 1 - s
                sl = slot(s, n)
                if n == 0 and L == "A" and first(b):
                    loaded(pe, "A2")
                if n == 0 and L == "E" and first(b):
                    pe.wait_ge(S("D_v"), B)
                    pe.wait_ge(S("D_qf"), B)
                    pe.wait_ge(S("D_gm"), 2 * B)
                    pe.wait_ge(S("D_an"), B)
                if n == 0 and L == "E":
                    pe.wait_ge(S("E_k0st"), b * 48 + 48)
                    pe.wait_ge(S("E_qm"), b * 2 + 1)
                    pe.wait_ge(S("E_v"), b + 1)
                elif L != "E":
                    pe.wait_ge(S(f"{L}_q"), b * 2 + n + 1)
                    pe.wait_ge(S(f"{L}_kbd"), b * 2 + n + 1)
                if n == 2:
                    pe.wait_ge(S("E_qm"), b * 2 + 2)
                if n == 4:
                    pe.wait_ge(S("E_k1st"), b * 48 + 48)
                    pe.wait_ge(S("E_qma"), b + 1)
                if n in (0, 5, 6):
                    pe.wait_ge(S("sub"), nu(L, g + 2))
                elif n == 1 and L != "E":
                    pe.wait_ge(S(f"{L}_v"), b + 1)
                elif n == 7 and also_p:
                    pe.wait_ge(S("E_ql"), b + 2)
                    pe.wait_ge(S("E_kl"), b + 2)
                    pe.wait_ge(S("E_v"), b + 2)
                else:
                    pe.wait_ge(S("sub"), nu(L, g + 1))
                for h in range(2):
                    if L == "A":
                        pe.matmul(sl[:, h, :], ident16[:, :], causal[:, :], start=True, stop=False)
                    if L == "E":
                        pe.matmul(sl[:, h, :], ident16[:, :], bc(window[:, :], 1, 2), start=True, stop=False,
                                  skip_group_check=True)
                        for q in range(2):
                            mm = pe.matmul(sl[:, h, q * D:(q + 1) * D], qm[u][0:KR, n, 2 * h + q, :],
                                           kT[u][n // 4][0:KR], start=False, stop=True, skip_group_check=True)
                    else:
                        mm = pe.matmul(sl[:, h, :], qT[u][:, n, :], kbd[u][:, n, 4 * h:4 * h + 4, :],
                                       start=(L == "B"), stop=True)
                mm.then_inc(S("sps"), 1)

            def transposes(b, n):
                g = b * U + n
                pe.wait_ge(S("exp"), nu(L, g + 1))
                for h, (free, done) in enumerate((("pca", "tra"), ("pcb", "trb"))):
                    pe.wait_ge(S(free), nu(L, g + 1))
                    for q in range(4):
                        at = (q * 2 + h) * P if L == "E" else (h * 4 + q) * P
                        mm = pe.transpose(PT[h][:, q * P:(q + 1) * P], e[n % 2][:, at:at + P], ident[:, :])
                    mm.then_inc(S(done), 1)

            def values(b, s, n):
                g = b * U + n
                u = 1 - s
                pe.wait_ge(S("pca"), nu(L, g + 2))
                pe.wait_ge(S("pcb"), nu(L, g + 2))
                if n == 0:
                    if not (L == "A" and isinstance(b, int) and b == 0):
                        pe.wait_ge(S("ot"), {"A": 0, "B": B, "E": 2 * B}[L] + b * OTN[L])
                    if U == 1:
                        pe.wait_ge(S(f"{L}_v"), b + 1)
                if L == "E":
                    if n == 4:
                        pe.wait_ge(S("ot"), 2 * B + b * 2 + 1)
                    r = 32 * (n % 4)
                    for k in range(2):
                        mm = pe.matmul(OB[r:r + VW, :], v[u][:, k * D + n * VW:k * D + (n + 1) * VW],
                                       pT[n % 2][:, k * HALF:(k + 1) * HALF], start=(k == 0), stop=(k == 1),
                                       tile_position=(0, r))
                else:
                    for h in range(8):
                        r, blk, head = 32 * (h % 4), 2 * n + h // 4, 8 * n + h
                        mm = pe.matmul(OB[r:r + VW, blk * P:(blk + 1) * P], v[u][:, head * VW:(head + 1) * VW],
                                       pT[n % 2][:, h * P:(h + 1) * P], start=True, stop=True,
                                       tile_position=(0, r))
                mm.then_inc(S("pv"), 1)

            def out_rows(c, r):
                pe.wait_ge(S("ot"), {"A": 0, "B": B, "E": 2 * B}[L] + c * OTN[L] + r + 1)
                if r == 0:
                    pe.wait_ge(S("xt"), nb(L, c + 1))
                else:
                    pe.wait_ge(S(f"{L}_an"), c * 2 + 1)
                for k in range(4):
                    mm = pe.transpose(MB[:, k * P:(k + 1) * P], oT[:, r, k * P:(k + 1) * P], ident[:, :])
                mm.then_inc(S(f"{L}_otr"), 1)

            def out_T(c):
                if L == "D":
                    pe.wait_ge(S("xt"), nb(L, c + 1))
                pe.wait_ge(S(f"{L}_an"), (c + 1) * (2 if L == "E" else 1))
                for k in range(C):
                    mm = pe.transpose(MB[:, k * P:(k + 1) * P], an[:, k * P:(k + 1) * P], ident[:, :])
                mm.then_inc(S(f"{L}_atr"), 1)

            def out_project(c):
                pe.wait_ge(S(f"{L}_at"), c + 1)
                pe_rows(pe, MB[:, D:2 * D], W[L, "wo"], aT).then_inc(S("y"), 1)

            def ref_rows(c, s):
                pe.wait_ge(S("B_an"), c + 1)
                for k in range(C):
                    mm = pe.transpose(MB[:, D + k * P:D + (k + 1) * P], refT[s][:, k, :], ident[:, :])
                mm.then_inc(S("y"), 1)

            def x_T(c, s):
                pe.wait_ge(S("xn"), nb(L, c + 1))
                for k in range(C):
                    mm = pe.transpose(MB[:, k * P:(k + 1) * P], xn[s][:, k * P:(k + 1) * P], ident[:, :])
                mm.then_inc(S("xtr"), 1)

            def linear_project(i, s):
                pe.wait_ge(S("D_xs"), i + 1)
                if not first(i):
                    pe.wait_ge(S("D_qk"), i)
                    pe.wait_ge(S("D_gx"), i)
                    pe.wait_ge(S("D_v"), i)
                pe_rows(pe, ps[:, 0, :], W[L, "wqk"], xs[s]).then_inc(S("D_qkps"), 1)
                pe_rows(pe, ps[:, 1, 0:D], W[L, "wg"], xs[s]).then_inc(S("D_gps"), 1)
                pe_rows(pe, ps[:, 2, 0:D], W[L, "wv"], xs[s]).then_inc(S("D_vps"), 1)

            def linear_sums(b, u):
                pe.wait_ge(S("D_f"), b + 1)
                for c in range(C):
                    mm = pe.transpose(ps[:, 3, c * P:(c + 1) * P], f[u][:, c * P:(c + 1) * P], ident[:, :])
                mm.then_inc(S("D_qfps"), 1)
                pe.wait_ge(S("D_v"), b + 1)
                for n, rows in enumerate((P // 2, P)):
                    for c in range(C):
                        mm = pe.matmul(ps[:, 4 + n, c * D:(c + 1) * D], f[u][0:rows, D + c * P:D + (c + 1) * P],
                                       v[u][0:rows, c * D:(c + 1) * D], start=True, stop=True)
                mm.then_inc(S("D_gmps"), 1)

            def linear_out(b):
                pe.wait_ge(S("D_qf"), b + 1)
                pe.wait_ge(S("D_gm"), b * 2 + 2)
                for n in range(2):
                    r = 64 * n
                    for c in range(C):
                        mm = pe.matmul(ps[r:r + 64, 6, c * D:(c + 1) * D], qfT[:, c, r:r + 64],
                                       gm[:, n, c * D:(c + 1) * D], start=True, stop=True,
                                       tile_position=(0, r))
                mm.then_inc(S("D_num"), 1)

            return dict(L=L, project=project, project2=project2, scores=scores,
                                   transposes=transposes, values=values, out_rows=out_rows, out_T=out_T,
                                   out_project=out_project, ref_rows=ref_rows, x_T=x_T,
                                   linear_project=linear_project, linear_sums=linear_sums,
                                   linear_out=linear_out, queries=queries)

        def pe_two(s, p, c, f):
            (P_, pb), (C_, cb), (F_, fb) = (x or (None, None) for x in (p, c, f))
            if f:
                F_["out_rows"](fb, 0)
            if c:
                C_["scores"](cb, s, 1, bool(p))
            if f and F_["L"] == "B":
                F_["ref_rows"](fb, s)
            if f and F_["L"] == "A":
                F_["out_T"](fb)
            if p:
                P_["project"](pb, s)
            if f and F_["L"] == "A":
                F_["out_project"](fb)
            if p and P_["L"] == "A":
                P_["project2"](pb, s)
            if c:
                C_["transposes"](cb, 0)
            if p and P_["L"] == "B":
                P_["project2"](pb, s)
            if c:
                C_["transposes"](cb, 1)
                C_["values"](cb, s, 0)
            if p:
                P_["scores"](pb, 1 - s, 0, False)
            if c:
                C_["values"](cb, s, 1)
            if f:
                if not c:
                    pe_logits(nc.tensor, F_["L"], range(EARLY))
                F_["x_T"](fb, s)

        def pe_groups(s, p, c, f):
            (P_, pb), (C_, cb), (F_, fb) = (x or (None, None) for x in (p, c, f))
            before = f and F_["L"] == "E"
            U = UNITS["E"]
            for n in range(U):
                if c:
                    C_["scores"](cb, s, n, bool(p))
                if n < 2 and before:
                    F_["transposes"](fb, n + U - 2)
                if n >= 2 and c:
                    C_["transposes"](cb, n - 2)
                if n == 5 and p:
                    P_["project2"](pb, s)
                if n < 3 and before:
                    F_["values"](fb, 1 - s, n + U - 3)
                if n >= 3 and c:
                    C_["values"](cb, s, n - 3)
                if n == 4 and p:
                    P_["queries"](pb, s, 0)
                    P_["queries"](pb, s, 1)
                if before and n in (1, 3):
                    F_["out_rows"](fb, n // 2)
                if f and n == 5:
                    F_["out_T"](fb)
                if f and n == 6:
                    F_["out_project"](fb)
                if f and n == 7:
                    if not c:
                        pe_logits(nc.tensor, F_["L"], range(EARLY))
                    F_["x_T"](fb, s)

        def pe_linear(s, p, c, f):
            (P_, pb), (C_, cb), (F_, fb) = (x or (None, None) for x in (p, c, f))
            if f:
                F_["out_T"](fb)
            if c:
                C_["linear_sums"](cb, 1 - s)
            if f:
                F_["out_project"](fb)
            if c:
                C_["linear_out"](cb)
            if p and P_["L"] == "D":
                P_["linear_project"](pb, s)
            if p and P_["L"] == "E":
                P_["queries"](pb, s, 0)
                P_["queries"](pb, s, 1)
                P_["project2"](pb, s)
            if f:
                F_["x_T"](fb, s)

        def pe_logits(pe, L, batches):
            w = 16 if L == "E" else E0
            for b in batches:
                pe.wait_ge(S("xt"), nb(L, b + 2))
                for c in range(C):
                    mm = pe.matmul(ps[:, 0, b * w:(b + 1) * w], XT[:, c, b * P:(b + 1) * P], W[L, "wr"][:, c, :],
                                   start=(c == 0), stop=(c == C - 1))
                mm.then_inc(S(f"{L}_lgps"), 1)

        def pe_combine_T(pe, L):
            w = 16 if L == "E" else E0
            pe.wait_ge(S(f"{L}_cm"), 2 if L == "E" else 1)
            for h in range(2):
                for b in range(4):
                    at = (4 * h + b) * w
                    mm = pe.transpose(ps[0:w, 2 + h, b * P:(b + 1) * P], cm[:, at:at + w], ident[:, :])
                mm.then_inc(S(f"{L}_cps"), 1)

        def pe_moe(pe, L):
            n = BLOCKS[L]

            def gate_up(x, u, t):
                if t == 0:
                    pe.wait_ge(S(f"{L}_wl"), x * 2 + 1)
                if not first(x):
                    pe.wait_ge(S(f"{L}_a1"), x * 2 + t - 1)
                for s in range(2):
                    i = 0
                    for w, xx in ((wh, XH), (wl, XH), (wh, XL)):
                        for c in range(C):
                            mm = pe.matmul(GU[t][s], w[u][:, (c * 2 + s) * P:(c * 2 + s + 1) * P],
                                           xx[:, c, t * HALF:(t + 1) * HALF], start=(i == 0), stop=(i == 5))
                            i += 1
                    mm.then_inc(S(f"{L}_gu"), 1)

            def down(x, u, t):
                if t == 0:
                    pe.wait_ge(S(f"{L}_wl"), x * 2 + 2)
                pe.wait_ge(S("al"), nh(L, x * 2 + t + 1))
                for m in range(C):
                    for w, x_ in ((wh, ah), (wl, ah), (wh, al)):
                        mm = pe.matmul(Y[:, 2 * m + t, :], w[u][:, (4 + m) * P:(5 + m) * P],
                                       x_[t][:, :], start=False, stop=False, skip_group_check=True)
                mm.then_inc(S(f"{L}_down"), 1)

            pe_combine_T(pe, BEFORE[L])
            pe.wait_ge(S(f"{BEFORE[L]}_xl"), 1)
            for t in range(2):
                gate_up(0, 0, t)
            before_done(pe, L)
            pe.wait_ge(S("zero16"), 1)
            for m in range(4):
                pe.matmul(Y[:, m, :], ident16[:, :], zero16[:, :], start=True, stop=False, skip_group_check=True)
            with pe.Fori(0, (n - 1) // 2) as j:
                for s in range(2):
                    for t in range(2):
                        gate_up(j * 2 + 1 + s, 1 - s, t)
                        down(j * 2 + s, s, t)
            if n % 2 == 0:
                for t in range(2):
                    gate_up(n - 1, 1, t)
                    down(n - 2, 0, t)
            for t in range(2):
                down(n - 1, (n - 1) % 2, t)

            for b in range(B):
                if b % 4 == 0:
                    pe.wait_ge(S(f"{L}_yt"), b // 2 + 2)
                for c in range(C):
                    at = (b % 2) * D + c * P
                    mm = pe.transpose(ps[:, 4 + b // 2, at:at + P], ysb[c][:, b * P:(b + 1) * P], ident[:, :])
                mm.then_inc(S("y"), 1)
            if L == "C":
                for b in range(B):
                    pe.wait_ge(S("xn"), nb(L, b + 1))
                    for c in range(C):
                        mm = pe.transpose(ps[:, 2 * c + b // 4, (b % 4) * P:(b % 4 + 1) * P],
                                          X[:, b, c * P:(c + 1) * P], ident[:, :])
                    mm.then_inc(S("xtr"), 1)

        @block.tensor
        def _(pe):
            two_layers(pe, pe_attention, pe_two, pe_two, "A", "B")
            pe_logits(pe, "B", range(EARLY, B))
            pe_moe(pe, "C")
            two_layers(pe, pe_attention, pe_linear, pe_groups, "D", "E")
            pe_logits(pe, "E", range(EARLY, B))
            pe_moe(pe, "F")

        def act_x(act, L, b, bank):
            act.wait_ge(S("xtr"), nb(L, b + 1))
            act.activation(XT[:, :, tok(b)], bank[:, 0:D].rearrange("p (c q) -> p c q", c=C), ACT.Copy)\
               .then_inc(S("xt"), 1)

        def act_attention(act, L):
            U = UNITS[L]
            scale = 0.25 if L != "E" else float(1.0 / np.sqrt(np.float32(DH1)))
            loaded(act, L)
            if L == "D":
                before_done(act, L)

            def relu(i, s):
                act.wait_ge(S("B_fcps"), i + 1)
                for n, dst in enumerate((refT, supT)):
                    for c in range(C):
                        at = n * D + c * P
                        act.activation(dst[s][:, c, :], SLOT[(s + 1) % 2][:, 0, at:at + P], ACT.Relu,
                                       bias=W[L, "bfc"][:, c:c + 1]).then_inc(S("B_fc"), 1)

            def queries(i, s):
                act.wait_ge(S(f"{L}_qkps"), i + 1)
                for c in range(C):
                    act.activation(qT[s][:, c, :], SLOT[(s + 1) % 2][:, 0 if L == "A" else 1, c * P:(c + 1) * P],
                                   ACT.Identity, bias=W[L, "bq"][:, c:c + 1]).then_inc(S(f"{L}_q"), 1)

            def high_queries(i, s):
                act.wait_ge(S("E_qps"), i + 1)
                if not first(i):
                    act.wait_ge(S("E_qm"), i * 2)
                    act.wait_ge(S("E_qma"), i)
                act.activation(qh[:, :], SLOT[s][:, 0, 0:D], ACT.Copy).then_inc(S("E_qh"), 1)

            def high_keys_and_values(i, s):
                act.wait_ge(S("E_vps"), i + 3)
                act.wait_ge(S("E_vone"), 2)
                act.activation(v[s][:, :].rearrange("p (h w) -> p h w", w=VW)[:, :, 0:DH1],
                               SLOT[s][:, 1, D:D + P].rearrange("p (h w) -> p h w", w=DH1), ACT.Copy)\
                   .then_inc(S("E_v"), 1)
                act.activation(kh[:, :], SLOT[s][0:64, 1, 0:2 * P], ACT.Copy).then_inc(S("E_kh"), 1)

            def masks(i, s):
                act.wait_ge(S("E_q1st"), i * 96 + 96)
                for g in range(4):
                    ins = act.activation(qm[s][0:96, 4 + g].rearrange("p j q -> p (j q)"), qst[1][0:96, :].bitcast(F32),
                                         ACT.Copy, scale=gmask[:, g:g + 1])
                ins.then_inc(S("E_qma"), 1)

            def exps(b, n):
                act.wait_ge(S("sub"), nu(L, b * U + n + 3))
                act.activation(e[n % 2][:, :], e[n % 2][:, :], ACT.Exp, scale=scale).then_inc(S("exp"), 1)

            def copies(b, n):
                g = b * U + n
                act.wait_ge(S("pv"), nu(L, g + 1))
                for h, (ready, done) in enumerate((("tra", "pca"), ("trb", "pcb"))):
                    act.wait_ge(S(ready), nu(L, g + 1 + 2 * h))
                    act.activation(pT[n % 2][:, h * HALF:(h + 1) * HALF], PT[h], ACT.Copy).then_inc(S(done), 1)

            def outputs(b, r):
                act.wait_ge(S("pv"), nu(L, b * U + (r + 1) * U // OTN[L] + 2))
                act.activation(oT[:, r, :], OB, ACT.Copy).then_inc(S("ot"), 1)

            def out_T(c):
                act.wait_ge(S(f"{L}_atr"), c + 1)
                act.activation(aT[:, :, :].rearrange("p c q -> p (c q)"), MB[:, 0:D], ACT.Copy)\
                   .then_inc(S(f"{L}_at"), 1)

            def query_features(b):
                act.wait_ge(S("D_qfps"), b + 1)
                act.activation(qfT[:, :, :].rearrange("p c q -> p (c q)"), ps[:, 3, 0:D], ACT.Copy)\
                   .then_inc(S("D_qf"), 1)

            def exponentials(i, s):
                act.wait_ge(S("D_gx"), i + 1)
                act.activation(eg[s][:, :], gx[:, :], ACT.Exp, scale=-1.0).then_inc(S("D_eg"), 1)
                act.wait_ge(S("D_rr"), i + 1)
                act.activation(rn[:, :], rr[:, :], ACT.Relu, scale=-1.0).then_inc(S("D_rn"), 1)
                act.wait_ge(S("D_rn"), i + 1)
                act.activation(re[:, :], rn[:, :], ACT.Exp, scale=-1.0).then_inc(S("D_re"), 1)

            return dict(L=L, relu=relu, queries=queries, high_queries=high_queries,
                                   high_keys_and_values=high_keys_and_values, masks=masks, exps=exps,
                                   copies=copies, outputs=outputs, out_T=out_T, query_features=query_features,
                                   exponentials=exponentials)

        def act_two(s, p, c, f):
            (P_, pb), (C_, cb), (F_, fb) = (x or (None, None) for x in (p, c, f))
            if c:
                C_["exps"](cb, 0)
            if f and F_["L"] == "A":
                F_["out_T"](fb)
            if p and P_["L"] == "B":
                P_["relu"](pb, s)
            if c:
                C_["exps"](cb, 1)
            if p and P_["L"] == "A":
                P_["queries"](pb, s)
            if c:
                C_["copies"](cb, 0)
            if p and P_["L"] == "B":
                P_["queries"](pb, s)
            if c:
                C_["copies"](cb, 1)
                C_["outputs"](cb, 0)
            if f:
                act_x(nc.scalar, F_["L"], fb, MB)

        def act_groups(s, p, c, f):
            (P_, pb), (C_, cb), (F_, fb) = (x or (None, None) for x in (p, c, f))
            before = f and F_["L"] == "E"
            U = UNITS["E"]
            for n in range(U):
                if n == 7 and c:
                    C_["outputs"](cb, 0)
                if n < 2 and before:
                    F_["copies"](fb, n + U - 2)
                if n >= 2 and c:
                    C_["copies"](cb, n - 2)
                if n == 2 and before:
                    F_["outputs"](fb, 1)
                if n == 5 and p:
                    P_["high_queries"](pb, s)
                if c:
                    C_["exps"](cb, n)
                if n == 5 and p:
                    P_["high_keys_and_values"](pb, s)
                if f and n == 5:
                    F_["out_T"](fb)
                if n == 7 and p:
                    P_["masks"](pb, s)
                if f and n == 7:
                    act_x(nc.scalar, F_["L"], fb, MB)

        def act_linear(s, p, c, f):
            (P_, pb), (C_, cb), (F_, fb) = (x or (None, None) for x in (p, c, f))
            if f:
                F_["out_T"](fb)
            if c:
                C_["query_features"](cb)
            if p and P_["L"] == "D":
                P_["exponentials"](pb, s)
            if p and P_["L"] == "E":
                P_["high_queries"](pb, s)
                P_["high_keys_and_values"](pb, s)
                P_["masks"](pb, s)
            if f:
                act_x(nc.scalar, F_["L"], fb, MB)

        def act_router(act, L):
            n_e = E0 if L == "B" else E1
            act.wait_ge(S("xt"), nb(L, B + 1))
            act.activation(XH[:, :, :], XT[:, :, :], ACT.Copy).then_inc(S(f"{L}_xh"), 1)
            act.wait_ge(S(f"{L}_lgm"), 1)
            act.activation(ex[:, 0:B * n_e], ex[:, 0:B * n_e], ACT.Exp).then_inc(S(f"{L}_ex"), 1)
            if L == "E":
                act.activation(sg[:, :], lg[:, 0:B * 16].rearrange("p (b n) -> p b n", n=16)[:, :, 15], ACT.Exp,
                               scale=-1.0).then_inc(S("E_sg"), 1)
            w = 16 if L == "E" else E0
            act.wait_ge(S(f"{L}_cps"), 2)
            if L == "B":
                for h in range(2):
                    act.activation(cT[0:w, h * HALF:(h + 1) * HALF], ps[0:w, 2 + h, :], ACT.Copy)\
                       .then_inc(S("B_cT"), 1)
            else:
                act.activation(cT[0:w, :], ps[0:w, 2:4, :].rearrange("p a t -> p (a t)"), ACT.Copy)\
                   .then_inc(S("E_cT"), 1)

        def act_moe(act, L):
            n = BLOCKS[L]
            before_done(act, L)

            def step(x, t):
                act.wait_ge(S(f"{L}_gu"), x * 4 + 2 * t + 1)
                if not first(x):
                    act.wait_ge(S(f"{L}_a1"), x * 2 + t - 1)
                act.activation(sgt[t], GU[t][0], ACT.Silu).then_inc(S("silu"), 1)
                act.wait_ge(S(f"{L}_a2"), x * 2 + t + 1)
                if not first(x):
                    act.wait_ge(S(f"{L}_down"), x * 2 + t - 1)
                act.activation(ah[t][:, :], a2[t], ACT.Copy).then_inc(S("ah"), 1)

            for t in range(2):
                step(0, t)
            with act.Fori(1, n) as x:
                for t in range(2):
                    step(x, t)
            act.wait_ge(S(f"{L}_down"), 2 * n)

            for h in range(2):
                for c in range(C):
                    act.activation(ysb[c][:, h * HALF:(h + 1) * HALF], Y[:, 2 * c + h, :], ACT.Copy)\
                       .then_inc(S(f"{L}_yt"), 1)
            if L == "C":
                for h in range(2):
                    act.wait_ge(S("xtr"), nb(L, 4 * h + 4))
                    for c in range(C):
                        act.activation(XT[:, c, h * HALF:(h + 1) * HALF], ps[:, 2 * c + h, :], ACT.Copy)\
                           .then_inc(S("xt"), 2)

        @block.scalar
        def _(act):
            two_layers(act, act_attention, act_two, act_two, "A", "B")
            act_router(act, "B")
            act_moe(act, "C")
            two_layers(act, act_attention, act_linear, act_groups, "D", "E")
            act_router(act, "E")
            act_moe(act, "F")

        def dve_stats(dve, L, b, u):
            dve.wait_ge(S("z"), nb(L, b + 2))
            dve.bn_stats(stats[:, :], z[u][:, :]).then_inc(S("stats"), 1)
            dve.wait_ge(S("stats"), nb(L, b + 1))
            settle(dve)
            dve.bn_aggr(agg[u][:, :], stats[:, :]).then_inc(S("agg"), 1)

        def dve_x(dve, L, b, u):
            dve.wait_ge(S("rstd"), nb(L, b + 1))
            dve.wait_ge(S("xrow"), nb(L, b + 1))
            dve.tensor_scalar(xn[u][:, :], z[u][:, :], agg[u][:, 0:1], rstd[u][:, :], ALU.subtract, ALU.mult)\
               .then_inc(S("xn"), 1)

        def dve_attention(dve, L):
            U = UNITS[L]
            loaded(dve, L)
            if L == "D":
                before_done(dve, L)

            def keys(i, s):
                dve.wait_ge(S(f"{L}_q"), i * 2 + 2)
                for c in range(C):
                    at = D + c * P
                    dve.scalar_tensor_tensor(kbd[s][:, c], bc(SLOT[(s + 1) % 2][:, 0 if L == "A" else 1, at:at + P], 1, 8),
                                             W[L, "bk"][:, c:c + 1], bc(hmask[:, :], 2, P), ALU.add, ALU.mult)\
                       .then_inc(S(f"{L}_kbd"), 1)

            def low_parts(i, s):
                for x, high, low, src in (("q", qh, ql, SLOT[s][:, 0, 0:D]), ("k", kh, kl, SLOT[s][0:64, 1, 0:2 * P])):
                    dve.wait_ge(S(f"E_{x}h"), i + 1)
                    if x == "q" and not first(i):
                        dve.wait_ge(S("E_qma"), i)
                        dve.wait_ge(S("E_qm"), i * 2)
                    dve.tensor_tensor(low[:, :], src, high[:, :].bitcast(F32), ALU.subtract).then_inc(S(f"E_{x}l"), 1)

            def masks(i, s):
                dve.wait_ge(S("E_q0st"), i * 96 + 96)
                for g in (0, 2):
                    dve.tensor_tensor(qm[s][0:96, g:g + 2].rearrange("p g j q -> p g (j q)"),
                                      bc(qst[0][0:96, :].bitcast(F32), 1, 2), bc(gmask[:, g:g + 2], 2, HALF),
                                      ALU.mult).then_inc(S("E_qm"), 1)

            def values(i, s):
                src = SLOT[(s + 1) % 2][:, 1 if L == "A" else 0, 0:D].rearrange("p (h w) -> p h w", w=DH0)
                dve.wait_ge(S(f"{L}_vps"), i + 3)
                if L == "A":
                    dve.tensor_tensor(v3[s], src, W[L, "bv"].rearrange("p (h w) -> p h w", w=DH0), ALU.add)\
                       .then_inc(S("A_v"), 1)
                else:
                    dve.tensor_copy(v3[s], src).then_inc(S("B_v"), 1)

            def unit(b, s, n):
                g = b * U + n
                hn = 4 if L == "E" else 8
                sl = SLOT[(1 - s + n) % 2] if L != "E" else SLOT[(s + (1, 0, 1, 0, 1, 1, 1, 0)[n]) % 2]
                s3 = sl.rearrange("p a (h k) -> p (a h) k", k=1024 // hn)
                dve.wait_ge(S("sps"), nu(L, g + 1))
                dve.reduce_max(mx[n % 2][:, 0:hn], s3, AX.X).then_inc(S("mx"), 1)
                dve.wait_ge(S("mx"), nu(L, g + 1))
                dve.wait_ge(S("trb"), nu(L, g + 1))
                dve.tensor_tensor(e[n % 2][:, :].rearrange("p (h k) -> p h k", h=hn), s3,
                                  bc(mx[n % 2][:, 0:hn], 2, 1024 // hn), ALU.subtract).then_inc(S("sub"), 1)

            def normalize(c, r):
                if L != "E":
                    dve.wait_ge(S(f"{L}_otr"), c + 1)
                    o = MB.rearrange("p (h w) -> p h w", w=VW)
                    dve.reciprocal(rden[:, 0, :], o[:, :, DH0]).then_inc(S(f"{L}_rden"), 1)
                    dve.wait_ge(S(f"{L}_rden"), c + 1)
                    dve.tensor_tensor(an[:, :].rearrange("p (h w) -> p h w", w=DH0), o[:, :, 0:DH0],
                                      bc(rden[:, 0, :], 2, DH0), ALU.mult).then_inc(S(f"{L}_an"), 1)
                    return
                dve.wait_ge(S("E_otr"), c * 2 + r + 1)
                o = MB.rearrange("p (j g w) -> p j g w", j=G1, w=VW)
                dve.reciprocal(rden[:, r, :].rearrange("p (j g) -> p j g", j=G1), o[:, :, :, DH1])\
                    .then_inc(S("E_rden"), 1)
                dve.wait_ge(S("E_rden"), c * 2 + r + 1)
                a4 = an[:, r * P:(r + 1) * P].rearrange("p (g j w) -> p j g w", g=4, w=DH1)
                dve.tensor_tensor(a4, o[:, :, :, 0:DH1],
                                  bc(rden[:, r, :].rearrange("p (j g) -> p j g", j=G1), 3, DH1), ALU.mult)\
                    .then_inc(S("E_an"), 1)

            def residual(c, s):
                dve.wait_ge(S("y"), nb(L, c + 1))
                dve.wait_ge(S("xb"), c + 1 + B * ATTN.index(L))
                if L == "B":
                    dve.wait_ge(S("B_an"), c + 1)
                    dve.tensor_tensor(z1[:, :], MB[:, D:2 * D], an[:, :], ALU.add).then_inc(S("B_z1"), 1)
                    dve.wait_ge(S("B_z1"), c + 1)
                    dve.tensor_tensor(z[s][:, :], z1[:, :], xb[:, :], ALU.add).then_inc(S("z"), 1)
                else:
                    dve.tensor_tensor(z[s][:, :], MB[:, D:2 * D], xb[:, :], ALU.add).then_inc(S("z"), 1)
                dve_stats(dve, L, c, s)

            def linear_in(i, s):
                qk3 = qk[:, :].rearrange("p (n two) -> p n two", two=2)
                rb3 = rb[:, :].rearrange("p (n two) -> p n two", two=2)
                dve.wait_ge(S("D_qkps"), i + 1)
                if not first(i):
                    dve.wait_ge(S("D_ra"), i)
                dve.tensor_tensor(qk[:, :], ps[:, 0, :], W[L, "bqk"][:, :], ALU.add).then_inc(S("D_qk"), 1)
                dve.wait_ge(S("D_gps"), i + 1)
                if not first(i):
                    dve.wait_ge(S("D_eg"), i)
                dve.tensor_tensor(gx[:, :], ps[:, 1, 0:D], W[L, "bg"][:, :], ALU.add).then_inc(S("D_gx"), 1)
                dve.wait_ge(S("D_qk"), i + 1)
                dve.tensor_tensor(rb3[:, :, 0], qk3[:, :, 1], W[L, "sin_lo"][:, :], ALU.mult).then_inc(S("D_rb"), 1)
                dve.tensor_tensor(rb3[:, :, 1], qk3[:, :, 0], W[L, "sin_hi"][:, :], ALU.mult).then_inc(S("D_rb"), 1)
                dve.wait_ge(S("D_vps"), i + 3)
                dve.tensor_tensor(v3[s], ps[:, 2, 0:D].rearrange("p (h w) -> p h w", w=DH0),
                                  W[L, "bv"].rearrange("p (h w) -> p h w", w=DH0), ALU.add).then_inc(S("D_v"), 1)
                dve.wait_ge(S("D_ra"), i + 1)
                dve.wait_ge(S("D_rb"), i * 2 + 2)
                dve.tensor_tensor(rr[:, :], ra[:, :], rb[:, :], ALU.add).then_inc(S("D_rr"), 1)

            def linear_features(i, s):
                dve.wait_ge(S("D_re"), i + 1)
                dve.scalar_tensor_tensor(f[s][:, :], rr[:, :], 0.0, re[:, :], ALU.max, ALU.add)\
                    .then_inc(S("D_f"), 1)

            def linear_masks(b):
                dve.wait_ge(S("D_gmps"), b + 1)
                for n in range(2):
                    dve.tensor_tensor(gm[:, n, :], ps[:, 4 + n, :], W[L, "blocks"][:, :], ALU.mult)\
                        .then_inc(S("D_gm"), 1)

            def linear_out(b, u):
                dve.wait_ge(S("D_num"), b + 1)
                num = ps[:, 6, :].rearrange("p (h w) -> p h w", w=VW)
                dve.tensor_scalar(den[:, :], num[:, :, DH0], 1e-6, None, ALU.add).then_inc(S("D_den"), 1)
                dve.wait_ge(S("D_den"), b + 1)
                dve.wait_ge(S("D_eg"), b + 1)
                dve.scalar_tensor_tensor(d2[:, :].rearrange("p (h w) -> p h w", w=DH0),
                                         eg[u][:, :].rearrange("p (h w) -> p h w", w=DH0), 1.0,
                                         bc(den[:, :], 2, DH0), ALU.add, ALU.mult).then_inc(S("D_d2"), 1)
                dve.wait_ge(S("D_d2"), b + 1)
                dve.reciprocal(r2[:, :], d2[:, :]).then_inc(S("D_r2"), 1)
                dve.wait_ge(S("D_r2"), b + 1)
                dve.tensor_tensor(an[:, :].rearrange("p (h w) -> p h w", w=DH0), num[:, :, 0:DH0],
                                  r2[:, :].rearrange("p (h w) -> p h w", w=DH0), ALU.mult).then_inc(S("D_an"), 1)

            def ones():
                for u in range(2):
                    dve.tensor_copy(v[u][:, :], W[L, "ones_v"][:, :]).then_inc(S("E_vone"), 1)

            return dict(L=L, ones=ones, keys=keys, low_parts=low_parts, masks=masks, values=values, unit=unit,
                                   normalize=normalize, residual=residual, linear_in=linear_in,
                                   linear_features=linear_features, linear_masks=linear_masks,
                                   linear_out=linear_out)

        def dve_two(s, p, c, f):
            (P_, pb), (C_, cb), (F_, fb) = (x or (None, None) for x in (p, c, f))
            if c:
                C_["unit"](cb, s, 0)
            if f:
                F_["normalize"](fb, 0)
            if c:
                C_["unit"](cb, s, 1)
            if f:
                F_["residual"](fb, s)
            if p:
                P_["keys"](pb, s)
            if f:
                dve_x(nc.vector, F_["L"], fb, s)
            if p:
                P_["values"](pb, s)

        def dve_groups(s, p, c, f):
            (P_, pb), (C_, cb), (F_, fb) = (x or (None, None) for x in (p, c, f))
            for n in range(UNITS["E"]):
                if c:
                    C_["unit"](cb, s, n)
                if f and F_["L"] == "E" and n in (1, 4):
                    F_["normalize"](fb, n // 3)
                if p and n == 5:
                    P_["low_parts"](pb, s)
                if f and n == 6:
                    F_["residual"](fb, s)
                if f and n == 7:
                    dve_x(nc.vector, F_["L"], fb, s)
                if p and n == 7:
                    P_["masks"](pb, s)

        def dve_linear(s, p, c, f):
            (P_, pb), (C_, cb), (F_, fb) = (x or (None, None) for x in (p, c, f))
            if c:
                C_["linear_masks"](cb)
            if f:
                F_["residual"](fb, s)
            if c:
                C_["linear_out"](cb, 1 - s)
            if p and P_["L"] == "D":
                P_["linear_in"](pb, s)
            if f:
                dve_x(nc.vector, F_["L"], fb, s)
            if p and P_["L"] == "D":
                P_["linear_features"](pb, s)
            if p and P_["L"] == "E":
                P_["ones"]()
                P_["low_parts"](pb, s)
                P_["masks"](pb, s)

        def dve_router(dve, L):
            n_e, k = (E0, TOP0) if L == "B" else (E1, TOP1)
            w = 16 if L == "E" else E0
            l3 = (lg[:, 0:B * 16] if L == "E" else lg64[:, :]).rearrange("p (b n) -> p b n", n=w)
            rep3, ex3, em3, msk3, cm3 = (x[:, 0:B * (w if x in (lrep, cm) else n_e)].rearrange(
                "p (b n) -> p b n", b=B) for x in (lrep, ex, em, msk, cm))
            rt = S(f"{L}_route")
            done = [0]

            def then(ins):
                done[0] += 1
                ins.then_inc(rt, 1)
                dve.wait_ge(rt, done[0])

            dve.wait_ge(S(f"{L}_lgps"), B)
            lps = ps[:, 0, 0:B * w].rearrange("p (b n) -> p b n", n=w)
            if L == "B":
                then(dve.tensor_copy(l3, lps))
            else:
                dve.memset(l3[:, :, n_e:15], SENT)
                dve.tensor_copy(l3[:, :, 15:16], lps[:, :, 15:16])
                then(dve.tensor_copy(l3[:, :, 0:n_e], lps[:, :, 0:n_e]))
            for b in range(B):
                ins = dve.max(top[:, b, :], l3[:, b, 0:n_e])
            then(ins)
            dve.tensor_tensor(ex3, l3[:, :, 0:n_e], bc(top[:, :, 0], 2, n_e), ALU.subtract)\
               .then_inc(S(f"{L}_lgm"), 1)
            if k < 8:
                dve.wait_ge(S(f"{L}_lgm"), 1)
                then(dve.memset(top[:, :, k:8], SENT))
            for b in range(B):
                ins = dve.match_replace(rep3[:, b, :], top[:, b, :], l3[:, b, :], -SENT)
            then(ins)
            then(dve.tensor_tensor(msk3, rep3[:, :, 0:n_e], l3[:, :, 0:n_e], ALU.not_equal))
            dve.wait_ge(S(f"{L}_ex"), 1)
            then(dve.tensor_tensor(em3, ex3, msk3, ALU.mult))
            then(dve.reduce_sum(esum[:, :], em3, AX.X))
            then(dve.reciprocal(einv[:, :], esum[:, :]))
            if L == "E":
                then(dve.memset(cm[:, 0:B * w], 0.0))
                dve.wait_ge(S("E_sg"), 1)
                then(dve.tensor_scalar(sg1[:, :], sg[:, :], 1.0, None, ALU.add))
                dve.reciprocal(cm3[:, :, n_e], sg1[:, :]).then_inc(S("E_cm"), 1)
            dve.tensor_tensor(cm3[:, :, 0:n_e], em3, bc(einv[:, :], 2, n_e), ALU.mult).then_inc(S(f"{L}_cm"), 1)

        def dve_moe(dve, L):
            before_done(dve, L)

            def step(x, k, t, j):
                g = x * 2 + t
                dve.wait_ge(S("silu"), nh(L, g + 1))
                dve.wait_ge(S(f"{L}_gu"), g * 2 + 2)
                dve.tensor_tensor(a1[t], sgt[t], GU[t][1], ALU.mult).then_inc(S(f"{L}_a1"), 1)
                dve.wait_ge(S(f"{L}_a1"), g + 1)
                if t == 0:
                    dve.wait_ge(S(f"{L}_t{k}"), j * 16 + 16)
                dve.tensor_tensor(a2[t], a1[t], wbc[k][:, t * HALF:(t + 1) * HALF], ALU.mult)\
                   .then_inc(S(f"{L}_a2"), 1)
                dve.wait_ge(S("ah"), nh(L, g + 1))
                dve.tensor_tensor(al[t][:, :], a2[t], ah[t][:, :].bitcast(F32), ALU.subtract)\
                   .then_inc(S("al"), 1)

            with dve.Fori(0, BLOCKS[L] // NW) as j:
                for k in range(NW):
                    for t in range(2):
                        step(j * NW + k, k, t, j)
            j = BLOCKS[L] // NW
            for k in range(BLOCKS[L] % NW):
                for t in range(2):
                    step(j * NW + k, k, t, j)

            for h in range(2):
                for q in (2 * h, 2 * h + 1):
                    dve.wait_ge(S("y"), nb(L, 2 * q + 2))
                    dve.tensor_tensor(zsb[h][:, (q % 2) * HALF:(q % 2 + 1) * HALF], ps[:, 4 + q, :],
                                      X[:, 2 * q:2 * q + 2, :].rearrange("p b d -> p (b d)"), ALU.add)\
                       .then_inc(S("z"), 2)
                for b in range(4 * h, 4 * h + 4):
                    dve.wait_ge(S("z"), nb(L, b // 2 * 2 + 3))
                    dve.bn_stats(stats8[:, b, :], zsb[h][:, (b % 4) * D:(b % 4 + 1) * D]).then_inc(S("stats"), 1)
                for b in range(4 * h, 4 * h + 4):
                    dve.wait_ge(S("stats"), nb(L, b + 1))
                    dve.bn_aggr(agg8[:, b, :], stats8[:, b, :]).then_inc(S("agg"), 1)
            for b in range(B):
                dve.wait_ge(S("agg"), nb(L, b + 1))
                dve.wait_ge(S("rstd"), nb(L, b // 4 * 4 + 4))
                dve.tensor_scalar(X[:, b, :], zsb[b // 4][:, (b % 4) * D:(b % 4 + 1) * D], agg8[:, b, 0:1],
                                  rstd8[:, b:b + 1], ALU.subtract, ALU.mult).then_inc(S("xn"), 1)

        @block.vector
        def _(dve):
            dve.memset(zero16[:, :], 0.0).then_inc(S("zero16"), 1)
            two_layers(dve, dve_attention, dve_two, dve_two, "A", "B")
            dve_router(dve, "B")
            dve_moe(dve, "C")
            two_layers(dve, dve_attention, dve_linear, dve_groups, "D", "E")
            dve_router(dve, "E")
            dve_moe(dve, "F")

        def newton(pool, L, b, n, var, tmp, y):
            st = S("newton")
            v_, p_, t0, t1, t2 = (tmp[:, k] for k in range(5))

            def then(ins, k):
                ins.then_inc(st, n)
                pool.wait_ge(st, nb(L, b) * 5 + n * k)
                if not isinstance(b, int):
                    settle(pool)

            then(pool.tensor_scalar(v_, var, EPS, None, ALU.add), 1)
            then(pool.tensor_tensor(p_, v_, minus_half[:, 0:n], ALU.pow), 2)
            then(pool.tensor_tensor(t0, p_, p_, ALU.mult), 3)
            then(pool.tensor_tensor(t1, t0, v_, ALU.mult), 4)
            then(pool.tensor_scalar(t2, t1, -0.5, 1.5, ALU.mult, ALU.add), 5)
            pool.tensor_tensor(y, t2, p_, ALU.mult).then_inc(S("rstd"), n)

        def pool_rstd(pool, L, b, u):
            pool.wait_ge(S("agg"), nb(L, b + 1))
            settle(pool)
            newton(pool, L, b, 1, agg[u][:, 1:2], newton8[:, :, 0:1], rstd[u][:, :])

        def pool_keep(pool, L, b, u):
            pool.wait_ge(S("xn"), nb(L, b + 1))
            settle(pool)
            pool.tensor_copy(X[:, bass.ds(b, 1), :].rearrange("p b d -> p (b d)"), xn[u][:, :])\
                .then_inc(S("xrow"), 1)

        def pool_attention(pool, L):
            loaded(pool, L)
            if L == "D":
                before_done(pool, L)

            def alibi_rows():
                for u in range(2):
                    pool.dma_start(shared[u][96:KR, :], a["E_qrow"].bitcast(F32R)).then_inc(S("alibi_rows"), 16)
                    for t in range(2):
                        pool.dma_start(kT[u][t][96:KR].rearrange("p s k -> p (s k)"), a["E_krow"].bitcast(F32R))\
                            .then_inc(S("alibi_rows"), 16)

            if L in ("B", "E"):
                pool.wait_ge(S(f"{BEFORE[L]}_vps"), B + 2)

            def stage(i, s):
                pool.wait_ge(S(f"{L}_vps"), i + 1)
                settle(pool)
                if L == "A" and isinstance(i, int) and i == 1:
                    loaded(pool, "A2")
                if L in ("B", "E"):
                    pool.wait_ge(S("xt"), nb(BEFORE[L], i + 2))
                    settle(pool)
                if L in ("B", "E"):
                    pool.tensor_copy(cs[s][:, :, :], CTXT[:, :, tok(i)])
                pool.tensor_copy(xs[s][:, :, :], XT[:, :, tok(i)]).then_inc(S(f"{L}_xs"), 1)

            def residual(c):
                pool.wait_ge(S("z"), nb(L, c + 1))
                settle(pool)
                if L in ("B", "E"):
                    pool.wait_ge(S("xrow"), nb(BEFORE[L], c + 3))
                    settle(pool)
                row = X[:, bass.ds(c, 1), :].rearrange("p b d -> p (b d)")
                bias = {"A": "bo", "B": "bv", "D": "bo"}.get(L)
                if bias:
                    pool.tensor_tensor(xb[:, :], row, W[L, bias][:, :], ALU.add).then_inc(S("xb"), 1)
                else:
                    pool.tensor_copy(xb[:, :], row).then_inc(S("xb"), 1)

            def rotary(i):
                pool.wait_ge(S("D_qk"), i + 1)
                pool.tensor_tensor(ra[:, :], qk[:, :], W[L, "cos"][:, :], ALU.mult).then_inc(S("D_ra"), 1)

            def spread_keys(i, s, t):
                pool.wait_ge(S("E_kl"), i + 1)
                settle(pool)
                for n, part in enumerate((kh, kh, kl)):
                    pool.dma_start(kT[s][t][32 * n:32 * n + 32].rearrange("p s k -> p (s k)"),
                                   part[32 * t:32 * t + 32]).then_inc(S(f"E_k{t}st"), 16)

            return dict(L=L, alibi_rows=alibi_rows, stage=stage, residual=residual, rotary=rotary, spread_keys=spread_keys)

        def pool_turn(s, p, c, f):
            (P_, pb), (F_, fb) = (x or (None, None) for x in (p, f))
            if p:
                P_["stage"](pb, s)
            if f:
                F_["residual"](fb)
            if f and F_["L"] == "D":
                pool_rstd(nc.gpsimd, F_["L"], fb, s)
            if p and P_["L"] == "E":
                P_["spread_keys"](pb, s, 0)
            if p and P_["L"] == "D":
                P_["rotary"](pb)
            if c and not f and P_["L"] == "D":
                P_["alibi_rows"]()
            if f and F_["L"] == "D":
                pool_keep(nc.gpsimd, F_["L"], fb, s)
            if f and F_["L"] != "D":
                pool_rstd(nc.gpsimd, F_["L"], fb, s)
                pool_keep(nc.gpsimd, F_["L"], fb, s)
            if p and P_["L"] == "E":
                P_["spread_keys"](pb, s, 1)

        def pool_moe(pool, L):
            n = BLOCKS[L]
            if L == "F":
                pool.wait_ge(S("sps"), nu("E", B * UNITS["E"]))
                settle(pool)

            def split(x, u, k, j):
                pool.wait_ge(S(f"{L}_w{k}"), j * 16 + 16)
                settle(pool)
                for h, (lo, hi) in enumerate(((0, 4 * P), (4 * P, WCOLS))):
                    if not (isinstance(x, int) and x < 2):
                        pool.wait_ge(S(f"{L}_down") if h else S(f"{L}_gu"), x * 2 - 2 if h else x * 4 - 4)
                        settle(pool)
                    pool.tensor_copy(wh[u][:, lo:hi], wraw[k][:, lo:hi]).then_inc(S(f"{L}_wh"), 1)
                    pool.wait_ge(S(f"{L}_wh"), x * 2 + h + 1)
                    pool.tensor_tensor(wl[u][:, lo:hi], wraw[k][:, lo:hi], wh[u][:, lo:hi].bitcast(F32),
                                       ALU.subtract).then_inc(S(f"{L}_wl"), 1)

            for k in range(NW):
                split(k, k % 2, k, 0)
                if k == 0:
                    x_before = BEFORE[L]
                    pool.wait_ge(S(f"{x_before}_xh"), 1)
                    pool.tensor_tensor(XL[:, :, :], XT[:, :, :], XH[:, :, :].bitcast(F32), ALU.subtract)\
                        .then_inc(S(f"{x_before}_xl"), 1)
            with pool.Fori(1, n // NW) as j:
                for k in range(NW):
                    split(j * NW + k, k % 2, k, j)
            for k in range(n % NW):
                split(n // NW * NW + k, k % 2, k, n // NW)

            for h in range(2):
                four = slice(4 * h, 4 * h + 4)
                pool.wait_ge(S("agg"), nb(L, 4 * h + 4))
                newton(pool, L, 4 * h, 4, agg8[:, four, 1], newton8[:, :, four], rstd8[:, four])
            if L == "C":
                pool.wait_ge(S("xn"), nb(L, B))
                pool.sem_inc(S("xrow"), B)

        @block.gpsimd
        def _(pool):
            pool.memset(minus_half[:, :], -0.5).then_inc(S("half"), 1)
            pool.wait_ge(S("half"), 1)
            two_layers(pool, pool_attention, pool_turn, pool_turn, "A", "B")
            pool_moe(pool, "C")
            two_layers(pool, pool_attention, pool_turn, pool_turn, "D", "E")
            pool_moe(pool, "F")


def constants():
    def bf16(x):
        return (np.ascontiguousarray(x, np.float32).view(np.uint32) >> 16).astype(np.uint16)

    big = np.float32(-1e30)
    q, k = np.arange(P)[:, None], np.arange(P)[None, :]
    c = {}
    c["head_mask"] = (np.arange(P)[:, None] // DH0 == np.arange(8)[None, :]).astype(np.float32)
    c["causal_bf16"] = bf16(np.tile(np.where(k > q, big, np.float32(0)), (1, 4)))
    delta = q - k
    win = [np.where((delta >= 0) & (delta < w), np.float32(0), big) for w in (64, 32)]
    c["window_bf16"] = bf16(np.concatenate(win, 1))
    c["ident"] = np.eye(P, dtype=np.float32)
    c["ident_bf16"] = bf16(np.eye(P))

    def ones_col(heads, at):
        row = np.zeros((heads, VW), np.float32)
        row[:, at] = 1
        return np.broadcast_to(row.reshape(-1), (P, heads * VW)).copy()

    c["A_ones_v"] = ones_col(H0, DH0)
    c["E_ones_v"] = ones_col(2 * KV1, DH1)
    inv = np.float32(1.0) / np.float32(10000.0) ** (np.arange(0, DH0, 2, dtype=np.float32) / np.float32(DH0))
    ang = np.arange(P, dtype=np.float32)[:, None] * inv[None, :].astype(np.float32)
    cos, sin = np.cos(ang).astype(np.float32), np.sin(ang).astype(np.float32)
    c["D_cos"] = np.tile(np.repeat(cos, 2, 1), (1, 2 * H0))
    c["D_sin_lo"] = np.tile(-sin, (1, 2 * H0))
    c["D_sin_hi"] = np.tile(sin, (1, 2 * H0))
    rows = np.arange(P)[:, None] // DH0
    cols = (np.arange(2 * D)[None, :] % D) // VW
    c["D_blocks"] = (rows == cols).astype(np.float32)
    c["group_mask"] = (np.arange(96)[:, None] % 32 // DH1 == np.arange(4)[None, :]).astype(np.float32)
    heads = KV1 * G1
    slope = 2.0 ** (-8.0 * np.arange(heads) / heads) * np.sqrt(float(DH1))
    pos = np.arange(P) - 64.0
    rows = []
    for row in (-slope[:, None] * pos, slope[:, None] + 0 * pos):
        row = row.reshape(-1).astype(np.float32)
        m, ex = np.frexp(row)
        high = np.ldexp(np.round(m * 2048) / 2048, ex).astype(np.float32)
        rows += [high, row - high]
    c["E_qrow"] = np.stack(rows)
    c["E_krow"] = np.stack([0 * pos + 1, 0 * pos + 1, pos, pos]).astype(np.float32)
    c["E_krow"] = np.concatenate([c["E_krow"]] * 2, 1)
    return c


def kernel(**inputs):
    import concourse.bacc as bacc
    from concourse.bass_utils import run_bass_kernel_spmd

    n = {k: np.asarray(v) for k, v in inputs.items()}

    def chunks(w):
        return w.reshape(-1, P, w.shape[1]).transpose(1, 0, 2)

    def T_layout(x):
        return chunks(x.reshape(T, D).T)

    def cols(b):
        return b.reshape(-1, P).T

    def spread(b):
        return np.broadcast_to(b, (P, b.shape[-1]))

    def in_turn(layer, w, at):
        head, (e, u), tail = w.shape[:at], w.shape[at:at + 2], w.shape[at + 2:]
        w = np.swapaxes(w.reshape(head + (e, u // RUN[layer], RUN[layer]) + tail), at, at + 1)
        return w.reshape(head + (e * u,) + tail)

    def blocks(layer, gu, down):
        nb = BLOCKS[layer]
        pad = nb * P - down.shape[0]
        gu = np.concatenate([gu, np.zeros((D, 2, pad), gu.dtype)], 2)
        down = np.concatenate([down, np.zeros((pad, D), down.dtype)])
        gu = gu.reshape(C, P, 2, nb, P).transpose(3, 1, 0, 2, 4).reshape(nb, P, C * 2 * P)
        return np.concatenate([gu, down.reshape(nb, P, D)], 2)

    d = constants()
    d["x_t"], d["ctx_t"] = T_layout(n["x"]), T_layout(n["ctx_2048"])
    d["x_rows"] = n["x"].transpose(1, 0, 2)
    w, b = n["L0_attn_W_in"].T, n["L0_attn_b_in"]
    d["A_wq"], d["A_wk"], d["A_wv"] = chunks(w[:, :D]), chunks(w[:, D:2 * D]), chunks(w[:, 2 * D:])
    d["A_bq"], d["A_bk"], d["A_bv"] = cols(b[:D]), cols(b[D:2 * D]), spread(b[2 * D:])
    d["A_wo"], d["A_bo"] = chunks(n["L0_attn_W_out"].T), spread(n["L0_attn_b_out"])
    p = "L0_xattn_"
    d["B_wfc"], d["B_bfc"] = chunks(n[p + "W_fc"].T), cols(n[p + "b_fc"])
    d["B_wq"], d["B_bq"] = chunks(n[p + "W_q"].T), cols(n[p + "b_q"])
    d["B_wk"], d["B_bk"] = chunks(n[p + "W_k"].T), cols(n[p + "b_k"])
    d["B_wv"] = chunks(n[p + "W_v"].reshape(D, D).T)
    d["B_bv"] = spread(n[p + "b_v"])
    d["B_wr"] = chunks(n["L0_ffn_gate_weight"].T)
    gu = n["L0_ffn_gate_up_weights"].reshape(E0, D, 2, I0).transpose(1, 2, 0, 3)
    d["C_w"] = blocks("C", in_turn("C", gu, 2), in_turn("C", n["L0_ffn_down_weights"], 0))
    p = "L1_attn_"
    d["D_wqk"] = chunks(np.concatenate([n[p + "Wq"].T, n[p + "Wk"].T], 1))
    d["D_bqk"] = spread(np.concatenate([n[p + "bq"], n[p + "bk"]]))
    d["D_wv"], d["D_bv"] = chunks(n[p + "Wv"].T), spread(n[p + "bv"])
    d["D_wg"], d["D_bg"] = chunks(n[p + "Wg"].T), spread(n[p + "bg"])
    d["D_wo"], d["D_bo"] = chunks(n[p + "Wo"].T), spread(n[p + "bo"])
    p = "L1_xattn_"
    d["E_wq"] = chunks(n[p + "Wq"].reshape(2 * D, KV1, G1, DH1).transpose(0, 2, 1, 3).reshape(2 * D, D))
    d["E_wk"], d["E_wsk"] = chunks(n[p + "Wk"]), chunks(n[p + "Wsk"])
    d["E_wv"], d["E_wsv"] = chunks(n[p + "Wv"]), chunks(n[p + "Wsv"])
    d["E_wo"] = chunks(n[p + "Wo"])
    p = "L1_ffn_"
    wr = np.zeros((D, 16), np.float32)
    wr[:, :E1], wr[:, 15] = n[p + "router_weight"].T, n[p + "shared_gate_w"][0]
    d["E_wr"] = chunks(wr)
    gu = in_turn("F", n[p + "gate_up_proj"].reshape(E1, 2, I1, D).transpose(3, 1, 0, 2), 2)
    sh = np.stack([n[p + "sh_gate_w"].T, n[p + "sh_up_w"].T], 1)
    down = [in_turn("F", n[p + "down_proj"].transpose(0, 2, 1), 0), n[p + "sh_down_w"].T]
    d["F_w"] = blocks("F", np.concatenate([gu, sh], 2), np.concatenate(down))

    nc = bacc.Bacc("TRN2", target_bir_lowering=False, num_devices=1)
    arrays, args = {}, {}
    for name, x in d.items():
        arrays[f"in_{name}"] = np.ascontiguousarray(x)
        args[name] = nc.dram_tensor(f"in_{name}", x.shape, mybir.dt.from_np(x.dtype), kind="ExternalInput").ap()
    out = nc.dram_tensor("out", (B, P, D), F32, kind="ExternalOutput").ap()
    build(nc, args, out)
    r = run_bass_kernel_spmd(nc, [arrays], core_ids=[0])
    return r.results[0]["out"]
```
